# Optimizing a Trainium2 kernel written in Bass

```python
import numpy as np
import jax
import jax.numpy as jnp

def _softmax(x, axis=-1):
    return jax.nn.softmax(x, axis=axis)

def _gelu(x):
    return jax.nn.gelu(x, approximate=True)

def _silu(x):
    return jax.nn.silu(x)

def _sigmoid(x):
    return jax.nn.sigmoid(x)

def _layernorm(x, axis=-1, eps=1e-05):
    m = jnp.mean(x, axis=axis, keepdims=True)
    v = jnp.var(x, axis=axis, keepdims=True)
    return (x - m) / jnp.sqrt(v + eps)

def _scatter_add(tgt, idx, src, axis=0):
    return tgt.at[idx].add(src)

def _segment_sum(src, seg, n):
    return jax.ops.segment_sum(src, seg, n)
kernel_name = 'mk_recurrent_d1_jaxref_r8_1110f9'

def setup_inputs(seed: int=0):
    np.random.seed(seed)
    _w = jnp.asarray

    def _L0_attn_setup():
        import jax, jax.numpy as jnp
        import numpy as np
        H = 16
        HKV = 4
        DK = 128
        DV = 128
        HID = 256
        KSZ = 4
        EPS = 1e-05
        NORMALIZER = 16.0

        def _causal_dwconv_silu(x, w):
            B, S, C = x.shape
            K = w.shape[1]
            xp = jnp.pad(x, ((0, 0), (K - 1, 0), (0, 0)))
            y = jnp.zeros_like(x)
            for i in range(K):
                y = y + w[:, i] * xp[:, i:i + S, :]
            return jax.nn.silu(y)

        def _l2norm(x, eps=1e-06):
            return x * jax.lax.rsqrt(jnp.sum(x * x, axis=-1, keepdims=True) + eps)
        key = jax.random.key(seed)
        ks = jax.random.split(key, 8)
        B, S = (2, 256)
        qkv_dim = H * DK + HKV * DK + HKV * DV
        s = lambda fan_in: 1.0 / np.sqrt(fan_in)
        return {'hidden_states': jax.random.normal(ks[0], (B, S, HID), jnp.float32), 'qkv_w': jax.random.uniform(ks[1], (qkv_dim, HID), jnp.float32, -s(HID), s(HID)), 'g_w': jax.random.uniform(ks[2], (H * DV, HID), jnp.float32, -s(HID), s(HID)), 'b_w': jax.random.uniform(ks[3], (H, HID), jnp.float32, -s(HID), s(HID)), 'gk_w': jax.random.uniform(ks[4], (H, HID), jnp.float32, -s(HID), s(HID)), 'conv_w': jax.random.uniform(ks[5], (qkv_dim, KSZ), jnp.float32, -s(KSZ), s(KSZ)), 'out_norm_w': jnp.ones((DV,), jnp.float32), 'o_w': jax.random.uniform(ks[6], (HID, H * DV), jnp.float32, -s(H * DV), s(H * DV))}
    _L0_attn_in = _L0_attn_setup()

    def _L0_ffn_setup():
        import jax, jax.numpy as jnp
        import numpy as np
        EPS = 1e-08

        def _quantize(w):
            gamma = jnp.mean(jnp.abs(w))
            return jnp.clip(jnp.round(w / (gamma + EPS)), -1.0, 1.0)

        def _bitlinear(x, w):
            return jnp.matmul(x, _quantize(w).T)
        key = jax.random.key(seed)
        k1, k2, k3, k4 = jax.random.split(key, 4)
        d, h = (256, 704)
        x = jax.random.normal(k1, (4, 256, d), dtype=jnp.float32)
        w1 = jax.random.normal(k2, (h, d), dtype=jnp.float32)
        w2 = jax.random.normal(k3, (h, d), dtype=jnp.float32)
        w3 = jax.random.normal(k4, (d, h), dtype=jnp.float32)
        return {'x': x, 'w1': w1, 'w2': w2, 'w3': w3}
    _L0_ffn_in = _L0_ffn_setup()
    _d = {'L0_attn_hidden_states': _L0_attn_in['hidden_states'], 'L0_attn_qkv_w': _L0_attn_in['qkv_w'], 'L0_attn_g_w': _L0_attn_in['g_w'], 'L0_attn_b_w': _L0_attn_in['b_w'], 'L0_attn_gk_w': _L0_attn_in['gk_w'], 'L0_attn_conv_w': _L0_attn_in['conv_w'], 'L0_attn_out_norm_w': _L0_attn_in['out_norm_w'], 'L0_attn_o_w': _L0_attn_in['o_w'], 'L0_ffn_w1': _L0_ffn_in['w1'], 'L0_ffn_w2': _L0_ffn_in['w2'], 'L0_ffn_w3': _L0_ffn_in['w3']}
    _x0 = _d['L0_attn_hidden_states']
    _d['L0_attn_hidden_states'] = jax.random.normal(jax.random.fold_in(jax.random.key(seed), 1), (4, 512, 256), dtype=_x0.dtype)
    del _x0
    return _d

def reference(L0_attn_hidden_states, L0_attn_qkv_w, L0_attn_g_w, L0_attn_b_w, L0_attn_gk_w, L0_attn_conv_w, L0_attn_out_norm_w, L0_attn_o_w, L0_ffn_w1, L0_ffn_w2, L0_ffn_w3):

    def _L0_attn_ref(hidden_states, qkv_w, g_w, b_w, gk_w, conv_w, out_norm_w, o_w):
        import jax, jax.numpy as jnp
        import numpy as np
        H = 16
        HKV = 4
        DK = 128
        DV = 128
        HID = 256
        KSZ = 4
        EPS = 1e-05
        NORMALIZER = 16.0

        def _causal_dwconv_silu(x, w):
            B, S, C = x.shape
            K = w.shape[1]
            xp = jnp.pad(x, ((0, 0), (K - 1, 0), (0, 0)))
            y = jnp.zeros_like(x)
            for i in range(K):
                y = y + w[:, i] * xp[:, i:i + S, :]
            return jax.nn.silu(y)

        def _l2norm(x, eps=1e-06):
            return x * jax.lax.rsqrt(jnp.sum(x * x, axis=-1, keepdims=True) + eps)
        x = hidden_states
        B, S, _ = x.shape
        grp = H // HKV
        qkv = x @ qkv_w.T
        qkv = _causal_dwconv_silu(qkv, conv_w)
        q, k, v = jnp.split(qkv, [H * DK, H * DK + HKV * DK], axis=-1)
        q = q.reshape(B, S, H, DK)
        k = k.reshape(B, S, HKV, DK)
        v = v.reshape(B, S, HKV, DV)
        k = jnp.repeat(k, grp, axis=2)
        v = jnp.repeat(v, grp, axis=2)
        q = _l2norm(q) * DK ** (-0.5)
        k = _l2norm(k)
        g_log = jax.nn.log_sigmoid(x @ gk_w.T) / NORMALIZER
        alpha = jnp.exp(g_log)
        beta = jax.nn.sigmoid(x @ b_w.T)

        def step(Sstate, inp):
            q_t, k_t, v_t, a_t, b_t = inp
            Sstate = Sstate * a_t[..., None, None]
            v_pred = jnp.einsum('bhk,bhkv->bhv', k_t, Sstate)
            delta = (v_t - v_pred) * b_t[..., None]
            Sstate = Sstate + jnp.einsum('bhk,bhv->bhkv', k_t, delta)
            o_t = jnp.einsum('bhk,bhkv->bhv', q_t, Sstate)
            return (Sstate, o_t)
        tfirst = lambda a: jnp.moveaxis(a, 1, 0)
        S0 = jnp.zeros((B, H, DK, DV), x.dtype)
        _, o = jax.lax.scan(step, S0, (tfirst(q), tfirst(k), tfirst(v), tfirst(alpha), tfirst(beta)))
        o = jnp.moveaxis(o, 0, 1)
        g = (x @ g_w.T).reshape(B, S, H, DV)
        o = o * jax.lax.rsqrt(jnp.mean(o * o, axis=-1, keepdims=True) + EPS) * out_norm_w
        o = o * jax.nn.silu(g)
        return o.reshape(B, S, H * DV) @ o_w.T

    def _L0_ffn_ref(x, w1, w2, w3):
        import jax, jax.numpy as jnp
        import numpy as np
        EPS = 1e-08

        def _quantize(w):
            gamma = jnp.mean(jnp.abs(w))
            return jnp.clip(jnp.round(w / (gamma + EPS)), -1.0, 1.0)

        def _bitlinear(x, w):
            return jnp.matmul(x, _quantize(w).T)
        x1 = _bitlinear(x, w1)
        x2 = _bitlinear(x, w2)
        hidden = jax.nn.sigmoid(x1) * x2
        return _bitlinear(hidden, w3)
    x = L0_attn_hidden_states
    xn = _layernorm(x, axis=-1)
    s = _L0_attn_ref(xn, L0_attn_qkv_w, L0_attn_g_w, L0_attn_b_w, L0_attn_gk_w, L0_attn_conv_w, L0_attn_out_norm_w, L0_attn_o_w)
    g = _silu(_L0_ffn_ref(xn, L0_ffn_w1, L0_ffn_w2, L0_ffn_w3))
    x = x + s * g
    return x

_drawn_inputs = setup_inputs


def setup_inputs(seed=0):
    import zlib

    import numpy as np

    out = dict(_drawn_inputs(seed))
    spreads = {'L0_attn_out_norm_w': (1.0, 0.2)}
    factors = {}
    for name, (base, spread) in spreads.items():
        noise = np.random.default_rng([zlib.crc32(name.encode()), seed]).standard_normal(out[name].shape)
        drawn = base * np.exp(spread * noise) if base else spread * noise
        out[name] = jnp.asarray(drawn.astype(out[name].dtype))
    for name, factor in factors.items():
        out[name] = (out[name] * factor).astype(out[name].dtype)
    return out
```

```python
from contextlib import ExitStack

import concourse.bass as bass
from concourse import mybir

F32 = mybir.dt.float32
BF16 = mybir.dt.bfloat16
I32 = mybir.dt.int32
ALU = mybir.AluOpType
ACT = mybir.ActivationFunctionType
AX = mybir.AxisListType

P = 128
NB = 4
HG = 4
NC = 4
SEQ = NC * P
NG = 4
NI = NB * NG
D = 256
KD = D // P
F = 704
FM = 6
FR = F - (FM - 1) * P
NT = 2 * HG + 2
RSQRT_SEED = float(0x5F3759DF)
NEWTON = 3

C_ID, C_TRI, C_STR, C_ONES, C_EYE, C_NEG, C_EVEN, C_ODD = 0, 128, 256, 384, 512, 768, 832, 833
C_ALL = 834
C_CAU, C_IND, C_THREE = 834, 962, 1474
C_END = C_THREE + P


class Count:

    def __init__(self, sem, per, step=1, start=0):
        self.sem, self.per, self.step, self.start = sem, per, step, start

    def after(self, n, k):
        return (n * self.per + k) * self.step + self.start


def wait(eng, count, n, k):
    v = count.after(n, k)
    if not isinstance(v, int) or v > count.start:
        eng.wait_ge(count.sem, v)


RING = [
    ("P0", "conv", 3, 0), ("P1", "conv", 6, 0), ("SK", "nk", 1, 0), ("GR", "gh", 1, 0), ("TV", "vn", 1, 0),
    ("TK", "kn", 1, 0), ("GT", "gr", 1, 0), ("E0", "e", 1, 0), ("E1", "e", 2, 0), ("E2", "e", 3, 0),
    ("E3", "e", 4, 0), ("P2", "conv", 9, 0), ("P3", "conv", 12, 0), ("OT0", "ot", 1, 1), ("P4", "conv", 15, 0),
    ("OUT0", "acc", 1, 1), ("P5", "conv", 18, 0), ("OT1", "ot", 2, 1), ("SQ0", "nq", 1, 0), ("OUT1", "acc", 2, 1),
    ("QK0", "pt", 1, 0), ("QK1", "pt", 2, 0), ("OT2", "ot", 3, 1), ("QK2", "pt", 3, 0), ("OUT2", "acc", 3, 1),
    ("QK3", "pt", 4, 0), ("OT3", "ot", 4, 1), ("QR1", "eq", 1, 0), ("QR2", "eq", 2, 0), ("OUT3", "acc", 4, 1),
    ("QR3", "eq", 3, 0), ("G0", "gate", 1, 0), ("G1", "gate", 2, 0), ("G2", "gate", 3, 0), ("G3", "gate", 4, 0),
    None,
]
RING_AT = {u[0]: j for j, u in enumerate(RING) if u}
BANKS = 3

CORE = "La . Ra . Lb . Lc . Rb . Ld . Le . Rc . Lf .".split()
FILL = [
    ["P0", "P1", "H0", "H1 SK", "GR", "TV", "TK GS", "GT E0", "E1"],
    ["FN E2", "E3", "P2", "P3 H2", "OT0 H3", "P4", "OUT0 H4", "P5", "OT1 H5"],
    ["SQ0 SQ1", "OUT1", "SQ2 SQ3", "QK0", "QK1", "OT2 IV", "QK2", "OUT2", "QK3"],
    ["OT3", "QR1 QR2", "OUT3", "QR3", "G0", "G1", "G2", "G3", ""],
]


def steps():
    for c in range(NC):
        gaps = iter(FILL[c])
        for s in CORE:
            if s[0] == "L":
                yield s, c, 0
            elif s[0] == "R":
                yield (s, c - 1, 0) if c else (s, NC - 1, -1)
            else:
                for f in next(gaps).split():
                    name = f.rstrip("0123456789")
                    yield name, int(f[len(name):] or 0), -1 if name in ("FN", "OT", "OUT") else 1


STEPS = list(steps())


def bodies(eng, stages):
    def body(k, parity):
        for name, j, shift in STEPS:
            n = k + shift
            if name in stages and not (isinstance(n, int) and not 0 <= n < NI):
                stages[name](n, (parity + shift) % 2, j)

    body(-1, 1)
    body(0, 0)
    with eng.Fori(0, (NI - 2) // 2) as i:
        body(2 * i + 1, 1)
        body(2 * i + 2, 0)
    body(NI - 1, 1)
    body(NI, 0)


RSQRT_STEPS = 3 + 3 * NEWTON


def rsqrt_steps(dve, sem, done, x, h, y, t):
    dve.wait_ge(sem, done)
    dve.tensor_scalar(h, x, -0.5, None, ALU.mult).then_inc(sem, 1)
    dve.tensor_scalar(y.bitcast(I32), x.bitcast(I32), 1, None, ALU.arith_shift_right).then_inc(sem, 1)
    dve.wait_ge(sem, done + 2)
    dve.tensor_scalar(y.bitcast(I32), y.bitcast(I32), -1.0, RSQRT_SEED, ALU.mult, ALU.add).then_inc(sem, 1)
    for i in range(NEWTON):
        dve.wait_ge(sem, done + 3 + 3 * i)
        dve.tensor_tensor(t, y, y, ALU.mult).then_inc(sem, 1)
        dve.wait_ge(sem, done + 4 + 3 * i)
        dve.tensor_tensor(t, t, h, ALU.mult).then_inc(sem, 1)
        dve.wait_ge(sem, done + 5 + 3 * i)
        dve.scalar_tensor_tensor(y, t, 1.5, y, ALU.add, ALU.mult).then_inc(sem, 1)


def attention_kernel(nc, x, wa, cw, bgk, wo, onw, w1t, w2t, w3t, cst, rows, diag, tri_d, out):
    ctx = ExitStack()
    with ctx:
        def sb(name, shape, dt=F32):
            return ctx.enter_context(nc.sbuf_tensor(name, shape, dt))

        def two(name, cols, dt=F32):
            return [sb(f"{name}{j}", [P, cols], dt) for j in range(2)]

        xnT = sb("xnT", [P, KD, NB * SEQ])
        acc = sb("acc", [P, NB * NC * D])
        cs = sb("cs", [P, C_ALL])
        cau = sb("cau", [P, HG * P], BF16)
        idb = sb("idb", [P, P], BF16)
        one3 = sb("one3", [P, P], BF16)
        HX = sb("HX", [P, NC, P], BF16)
        GX = sb("GX", [P, NC, HG * P], BF16)
        eG, eGC, wK = sb("eG", [P, NI * 16]), sb("eGC", [P, NI * 16]), sb("wK", [P, NI * 16])
        wv = sb("wv", [P, 1])
        KT, Kn, Vn = two("KT", SEQ), two("Kn", SEQ), two("Vn", SEQ)
        QT, SG, BP, PT = two("QT", 4 * SEQ), two("SG", 4 * SEQ), two("BP", 4 * SEQ), two("PT", 4 * SEQ)
        rk, cq, so = two("rk", NC), two("cq", 16), two("so", 16)
        wk, sR, dec = two("wk", 16), two("sR", 16), two("dec", 16)
        T16, U16, OB = sb("T16", [P, 4 * SEQ]), sb("U16", [P, 4 * SEQ]), sb("OB", [P, 4 * SEQ])
        wt = sb("wt", [P, NT, KD, P])
        wot = sb("wot", [P, HG, D])
        cwt = sb("cwt", [P, 6, 4])
        cacc, th = two("cacc", SEQ), two("th", SEQ)
        sqr = sb("sqr", [P, SEQ])
        VT = sb("VT", [P, SEQ])
        gr = sb("gr", [P, SEQ])
        gsb = VT
        Xf, X32, X64 = sb("Xf", [P, SEQ]), sb("X32", [P, SEQ]), sb("X64", [P, HG * 64])
        T32, U32 = sb("T32", [P, SEQ]), two("U32", SEQ)
        Rb, Yb, S, o2 = sb("Rb", [P, SEQ]), sb("Yb", [P, SEQ]), sb("S", [P, SEQ]), sb("o2", [P, SEQ])
        Kh, OT = two("Kh", SEQ), two("OT", SEQ)
        blkB, blkU, blkt = sb("blkB", [P, 16, 16]), sb("blkU", [P, 16, 16]), sb("blkt", [P, 64])
        blkO = sb("blkO", [P, 2, 16, 32])
        newton = [sb(f"newton{j}", [P, 16]) for j in range(4)]
        fo = sb("fo", [P, 16])

        banks = [ctx.enter_context(nc.psum_tensor(f"bank{j}", [P, 512], F32)) for j in range(8)]
        bX, bZ, bO, bY, bS = banks[3:8]

        def sem(name):
            return ctx.enter_context(nc.semaphore(name))

        def heads(t, c=None):
            a = t[:, :] if c is None else t[:, c * SEQ:(c + 1) * SEQ]
            return a.rearrange("p (h t) -> p h t", h=HG)

        def halves(t, c, odd, w):
            a = t[:, c * SEQ:(c + 1) * SEQ] if not isinstance(t, bass.AP) else t
            return a.rearrange("p (g a u) -> p g a u", a=2, u=w)[:, :, odd, :]

        def each(v, n=P):
            return v.unsqueeze(2).to_broadcast([P, v.shape[1], n])

        ident = cs[:, C_ID:C_ID + P]

        X = [QT[t // 8][:, (t % 8) * D:(t % 8 + 1) * D] for t in range(16)]
        bst, mv = SG[0][:, 0:96], SG[0][:, 128:160]
        zs, na, ez, spl = SG[0][:, 256:768], SG[0][:, 768:1280], SG[0][:, 1280:1792], SG[1][:, 0:512]
        gl, lb, Gs, Hs, Ws = (SG[1][:, 512 + 256 * j:768 + 256 * j] for j in range(5))
        rowf = BP[0][:, 0:512]
        rest = BP[0][:, 512:1024]
        rowp = BP[1][:, 0:768].bitcast(BF16).rearrange("p (q a t) -> p q a t", q=4, a=3)
        c0 = PT[0][:, 0:C_END - C_ALL]
        bgs = BP[1][:, 1024:1088].rearrange("p (k o) -> p k o", k=KD)
        with nc.Block() as block:
            s_x, s_c, s_bg, s_rows = sem("x_loaded"), sem("constants_loaded"), sem("bgk_loaded"), sem("rows_stored")
            s_init, s_ln, s_xt, s_xte = sem("constants_cast"), sem("layernorm_steps"), sem("x_transposed"), sem("xT_copied")
            s_z, s_zc, s_abs, s_exp, s_log = sem("z_ready"), sem("z_steps"), sem("abs_ready"), sem("exp_ready"), sem("log_ready")
            s_cum, s_g, s_w, s_rt, s_split = sem("cumsum_ready"), sem("G_steps"), sem("weights_ready"), sem("rows_transposed"), sem("split_steps")
            s_eg = sem("decays_ready")

            @block.sync
            def _(sp):
                xv = x.rearrange("(n t p) d -> n p t d", p=P, n=2)
                for j in range(2):
                    sp.dma_start(QT[j][:, :].rearrange("p (t d) -> p t d", d=D), xv[j]).then_inc(s_x, 16)
                sp.dma_start(cs[:, :], cst[:, 0:C_ALL]).then_inc(s_c, 16)
                sp.dma_start(c0, cst[:, C_ALL:C_END]).then_inc(s_c, 16)
                sp.dma_start(bgs, bgk).then_inc(s_bg, 16)
                sp.dma_start(wv[:, :], onw).then_inc(s_bg, 16)
                for q in range(4):
                    sp.wait_ge(s_split, 5)
                    sp.dma_start(rows[q * P:(q + 1) * P], rowp[:, q]).then_inc(s_rows, 16)
                sp.wait_ge(s_rows, 64)

            @block.gpsimd
            def _(pool):
                for t in (Xf, X32, X64, HX, GX):
                    pool.memset(t[:], 0.0).then_inc(s_init, 1)
                pool.memset(acc[:, :], 0.0).then_inc(s_init, 1)
                for t in (T16, U16):
                    pool.memset(t[:, :], 0.0).then_inc(s_init, 1)
                pool.wait_ge(s_c, 32)
                pool.wait_ge(s_init, 8)
                for c in range(NC):
                    pool.tensor_copy(GX[:, c, :], c0[:, C_IND - C_ALL:C_IND - C_ALL + 512]).then_inc(s_init, 1)
                    pool.tensor_copy(HX[:, c, :], c0[:, C_THREE - C_ALL:C_THREE - C_ALL + P]).then_inc(s_init, 1)
                    pool.tensor_copy(cau[:, c * P:(c + 1) * P], c0[:, C_CAU - C_ALL:C_CAU - C_ALL + P]).then_inc(s_init, 1)
                pool.tensor_copy(one3[:, :], c0[:, C_THREE - C_ALL:C_THREE - C_ALL + P]).then_inc(s_init, 1)
                pool.tensor_copy(idb[:, :], ident).then_inc(s_init, 1)

            @block.vector
            def _(dve):
                dve.wait_ge(s_x, 32)
                for t in range(16):
                    dve.bn_stats(bst[:, 6 * t:6 * t + 6], X[t]).then_inc(s_ln, 1)
                for t in range(16):
                    dve.wait_ge(s_ln, t + 1)
                    dve.bn_aggr(mv[:, 2 * t:2 * t + 2], bst[:, 6 * t:6 * t + 6]).then_inc(s_ln, 1)
                dve.wait_ge(s_ln, 32)
                var = mv.rearrange("p (t a) -> p t a", a=2)[:, :, 1]
                tx, th_, ty, tt = (t[:, :] for t in newton)
                dve.tensor_scalar(tx, var, 1e-5, None, ALU.add).then_inc(s_ln, 1)
                rsqrt_steps(dve, s_ln, 33, tx, th_, ty, tt)
                for t in range(16):
                    if t == 0:
                        dve.wait_ge(s_ln, 33 + RSQRT_STEPS)
                    dve.tensor_scalar(X[t], X[t], mv[:, 2 * t:2 * t + 1], ty[:, t:t + 1],
                                      ALU.subtract, ALU.mult).then_inc(s_ln, 1)
                for q in range(8):
                    if q % 2:
                        dve.wait_ge(s_xt, q + 1)
                        dve.tensor_copy(xnT[:, q // 4, (q % 4) * 512:(q % 4 + 1) * 512], banks[q][:, :]).then_inc(s_xte, 1)
                dve.wait_ge(s_z, 1)
                dve.tensor_copy(zs, banks[0][:, :]).then_inc(s_zc, 1)
                dve.wait_ge(s_zc, 1)
                dve.tensor_scalar(na, zs, -1.0, None, ALU.mult).then_inc(s_zc, 1)
                dve.wait_ge(s_zc, 2)
                dve.tensor_tensor(na, na, zs, ALU.min).then_inc(s_abs, 1)
                dve.wait_ge(s_log, 1)
                dve.scalar_tensor_tensor(spl, zs, 0.0, ez, ALU.min, ALU.subtract).then_inc(s_zc, 1)
                dve.wait_ge(s_zc, 3)
                sv = spl.rearrange("p (b c o) -> p b c o", b=NB, c=NC)
                for b in range(NB):
                    for dst, o, f in ((gl, 0, 1.0 / 16.0), (lb, 16, 1.0)):
                        dve.tensor_scalar(dst[:, b * 64:(b + 1) * 64].rearrange("p (g c h) -> p g c h", g=NG, c=NC),
                                          sv[:, b, :, o:o + 16].rearrange("p c (g h) -> p g c h", g=NG),
                                          f, None, ALU.mult).then_inc(s_g, 1)
                dve.wait_ge(s_eg, 2)
                dve.wait_ge(s_g, 8)
                dve.tensor_copy(Gs, banks[1][:, 0:256]).then_inc(s_g, 1)
                dve.tensor_tensor(Hs, lb, banks[1][:, 0:256], ALU.subtract).then_inc(s_g, 1)
                dve.wait_ge(s_g, 10)
                dve.tensor_tensor(Ws, Hs, banks[1][:, 256:512], ALU.add).then_inc(s_w, 1)
                dve.wait_ge(s_bg, 32)
                dve.tensor_scalar(wv[:, :], wv[:, :], 0.5, None, ALU.mult).then_inc(s_w, 1)
                dve.wait_ge(s_rt, 1)
                rp = [rowp[:, :, a, :] for a in range(3)]
                rf = rowf.rearrange("p (q t) -> p q t", q=4)
                rr = rest.rearrange("p (q t) -> p q t", q=4)
                dve.tensor_copy(rp[0], banks[2][:, :].rearrange("p (q t) -> p q t", q=4)).then_inc(s_split, 1)
                dve.wait_ge(s_split, 1)
                dve.tensor_tensor(rf, banks[2][:, :].rearrange("p (q t) -> p q t", q=4), rp[0], ALU.subtract).then_inc(s_split, 1)
                dve.wait_ge(s_split, 2)
                dve.tensor_copy(rp[1], rf).then_inc(s_split, 1)
                dve.wait_ge(s_split, 3)
                dve.tensor_tensor(rr, rf, rp[1], ALU.subtract).then_inc(s_split, 1)
                dve.wait_ge(s_split, 4)
                dve.tensor_copy(rp[2], rr).then_inc(s_split, 1)

            @block.scalar
            def _(act):
                for q in range(0, 8, 2):
                    act.wait_ge(s_xt, q + 1)
                    act.copy(xnT[:, q // 4, (q % 4) * 512:(q % 4 + 1) * 512], banks[q][:, :]).then_inc(s_xte, 1)
                act.wait_ge(s_abs, 1)
                act.activation(ez, na, ACT.Exp).then_inc(s_exp, 1)
                act.wait_ge(s_exp, 1)
                act.activation(ez, ez, ACT.Ln, bias=1.0).then_inc(s_log, 1)
                act.wait_ge(s_cum, 1)
                act.activation(eG[:, :], banks[1][:, 0:256], ACT.Exp).then_inc(s_eg, 1)
                act.activation(eGC[:, :], banks[1][:, 256:512], ACT.Exp).then_inc(s_eg, 1)
                act.wait_ge(s_w, 1)
                act.activation(wK[:, :], Ws, ACT.Exp).then_inc(s_eg, 1)

            @block.tensor
            def _(pe):
                pe.wait_ge(s_c, 32)
                for q in range(8):
                    kk, tq = q // 4, q % 4
                    pe.wait_ge(s_ln, 33 + RSQRT_STEPS + 4 * tq + 4)
                    for j in range(4):
                        mm = pe.transpose(banks[q][:, j * P:(j + 1) * P], X[4 * tq + j][:, kk * P:(kk + 1) * P], ident)
                    mm.then_inc(s_xt, 1)
                pe.wait_ge(s_bg, 32)
                pe.wait_ge(s_xte, 8)
                for t in range(16):
                    for kk in range(KD):
                        mm = pe.matmul(banks[0][:, 32 * t:32 * t + 32], xnT[:, kk, t * P:(t + 1) * P], bgs[:, kk, :],
                                       start=(kk == 0), stop=(kk == KD - 1))
                mm.then_inc(s_z, 1)
                pe.wait_ge(s_g, 8)
                pe.matmul(banks[1][:, 0:256], cs[:, C_TRI:C_TRI + P], gl, start=True, stop=True)
                pe.matmul(banks[1][:, 256:512], cs[:, C_ONES:C_ONES + P], gl, start=True, stop=True).then_inc(s_cum, 1)
                pe.wait_ge(s_g, 10)
                for q, src in enumerate((Gs, Gs, Hs, Hs)):
                    mm = pe.transpose(banks[2][:, q * P:(q + 1) * P], src[:, (q % 2) * P:(q % 2 + 1) * P], ident)
                mm.then_inc(s_rt, 1)

        C = {name: Count(sem(name), per) for name, per in dict(
            proj=NT, acc_=6, conv=18, th=6 + HG, silu=6, sq=5, stat=1, sqp=4, nk=RSQRT_STEPS + 4, nq=RSQRT_STEPS + 2,
            tkp=1, kn=1, tvp=1, vn=1, grp=1, gh=1, gtp=1, gr=1, ep=4, e=4, bp=4, qkp=4, pt=4, qrp=3, eq=3, qt=3,
            gate=4, sub=33, x16=4, xm=4, z16=4, u32=4, cp=4, x32=4, xe32=4, z32=4, u64=4, x64=4, xe64=4, z64=4, uf=4,
            ks=3, rr=3, y=4, ye=4, o=4, oe=4, su=3, s=3, kh=3, o2=4, sr=4, nf=RSQRT_STEPS + 4, fs=4, otp=4, ot=4,
            outp=4, acc=4).items()}
        C["outp"].start = 1
        for name, per in dict(wkv=1, wq=1, wg=1, cl=1, wol=1, rowl=6, dgw=8, dgr=1, tuw=2, tur=16).items():
            C[name] = Count(sem(name + "_dma"), per, 16)

        def bank(name):
            return banks[RING_AT[name] % BANKS]

        def wait_bank(pe, name, n):
            j, m = RING_AT[name] - BANKS, n
            while True:
                if j < 0:
                    j, m = j + len(RING), m - 1
                    if isinstance(m, int) and m < 0:
                        return
                use = RING[j]
                here = use is not None
                if here and isinstance(m, int):
                    here = 2 <= m < NI + 2 if use[3] else m < NI
                if here:
                    wait(pe, C[use[1]], m - 2 * use[3], use[2])
                    return
                j -= BANKS

        with nc.Block() as block:
            @block.tensor
            def _(pe):
                def project(n, p, t):
                    name = f"P{t}" if t < 6 else f"G{t - 6}"
                    if t in (0, 2, 6):
                        wait(pe, C[{0: "wkv", 2: "wq", 6: "wg"}[t]], n, 1)
                    wait_bank(pe, name, n)
                    for kk in range(KD):
                        mm = pe.matmul(bank(name)[:, :], wt[:, t, kk, :], xnT[:, kk, bass.ds((n // NG) * SEQ, SEQ)],
                                       start=(kk == 0), stop=(kk == KD - 1))
                    mm.then_inc(C["proj"].sem, 1)

                def gram(n, p, _):
                    wait(pe, C["silu"], n, 1)
                    wait_bank(pe, "GR", n)
                    for c in range(NC):
                        kc = KT[p][:, c * P:(c + 1) * P]
                        mm = pe.matmul(bank("GR")[:, c * P:(c + 1) * P], kc, kc, start=True, stop=True)
                    mm.then_inc(C["grp"].sem, 1)

                def gram_t(n, p, _):
                    wait(pe, C["gh"], n, 1)
                    wait_bank(pe, "GT", n)
                    for c in range(NC):
                        mm = pe.transpose(bank("GT")[:, c * P:(c + 1) * P], gsb[:, c * P:(c + 1) * P], ident)
                    mm.then_inc(C["gtp"].sem, 1)

                def rows_of(src, ready, k, name, done):
                    def go(n, p, _):
                        wait(pe, C[ready], n, k)
                        wait_bank(pe, name, n)
                        t = src[p] if isinstance(src, list) else src
                        for c in range(NC):
                            mm = pe.transpose(bank(name)[:, c * P:(c + 1) * P], t[:, c * P:(c + 1) * P], ident)
                        mm.then_inc(C[done].sem, 1)
                    return go

                def stats_k(n, p, _):
                    wait(pe, C["sq"], n, 1)
                    wait_bank(pe, "SK", n)
                    for c in range(NC):
                        mm = pe.matmul(bank("SK")[:, c:c + 1], sqr[:, c * P:(c + 1) * P], cs[:, C_ONES:C_ONES + 1],
                                       start=True, stop=True)
                    mm.then_inc(C["stat"].sem, 1)

                def stats_q(n, p, c):
                    wait(pe, C["sq"], n, 2 + c)
                    if c == 0:
                        wait_bank(pe, "SQ0", n)
                    for h in range(HG):
                        mm = pe.matmul(bank("SQ0")[:, 4 * c + h:4 * c + h + 1], sqr[:, h * P:(h + 1) * P],
                                       cs[:, C_ONES:C_ONES + 1], start=True, stop=True)
                    mm.then_inc(C["sqp"].sem, 1)

                def exponent(n, p, c):
                    wait(pe, C["rowl"], n, 6)
                    wait_bank(pe, f"E{c}", n)
                    b = bank(f"E{c}")
                    pe.matmul(b[:, :], idb[:, :], cau[:, :], start=True, stop=False)
                    pe.matmul(b[:, :], HX[:, c, :], GX[:, c, :], start=False, stop=True).then_inc(C["ep"].sem, 1)

                def row_g(n, p, c):
                    wait_bank(pe, f"QR{c}", n)
                    pe.matmul(bank(f"QR{c}")[:, :], one3[:, :], GX[:, c, :], start=True, stop=True).then_inc(C["qrp"].sem, 1)

                def qk(n, p, c):
                    wait(pe, C["silu"], n, 6)
                    wait_bank(pe, f"QK{c}", n)
                    pe.matmul(bank(f"QK{c}")[:, :], KT[p][:, c * P:(c + 1) * P], QT[p][:, c * SEQ:(c + 1) * SEQ],
                              start=True, stop=True).then_inc(C["qkp"].sem, 1)

                def out_t(n, p, c):
                    wait(pe, C["fs"], n, c + 1)
                    wait_bank(pe, f"OT{c}", n + 2)
                    for h in range(HG):
                        o = c * SEQ + h * P
                        mm = pe.transpose(bank(f"OT{c}")[:, h * P:(h + 1) * P], OB[:, o:o + P], ident)
                    mm.then_inc(C["otp"].sem, 1)

                def out_proj(n, p, c):
                    wait(pe, C["ot"], n, c + 1)
                    wait(pe, C["wol"], n, 1)
                    wait_bank(pe, f"OUT{c}", n + 2)
                    for h in range(HG):
                        mm = pe.matmul(bank(f"OUT{c}")[:, 0:D], OT[c % 2][:, h * P:(h + 1) * P], wot[:, h, :],
                                       start=(h == 0), stop=(h == HG - 1))
                    mm.then_inc(C["outp"].sem, 1)

                def half(t, c, odd, w):
                    a = halves(t, c or 0, odd, w)
                    n = a.shape[1] // HG
                    return [a[:, h * n:(h + 1) * n, :] for h in range(HG)]

                def pair(b, h, o):
                    return b[:, o + 64 * h:o + 64 * h + 64]

                def la(n, p, c):
                    if c == 0:
                        wait(pe, C["tur"], n, 16)
                    wait(pe, C["xe64"], n, c)
                    for h in range(HG):
                        mm = pe.matmul(pair(bX, h, 0), heads(BP[p], c)[:, h, :], half(T16, c, 0, 16)[h], start=True, stop=True)
                    mm.then_inc(C["x16"].sem, 1)

                def lb_(n, p, c):
                    wait(pe, C["xm"], n, c + 1)
                    wait(pe, C["uf"], n, c)
                    for h in range(HG):
                        pe.matmul(pair(bZ, h, 0), heads(U16, c)[:, h, :], half(Xf, None, 0, 16)[h], start=True, stop=True)
                        mm = pe.matmul(pair(bZ, h, 256), heads(Xf)[:, h, :], half(U16, c, 1, 16)[h], start=True, stop=True)
                    mm.then_inc(C["z16"].sem, 1)

                def lc(n, p, c):
                    wait(pe, C["u32"], n, c + 1)
                    wait(pe, C["cp"], n, c + 1)
                    for h in range(HG):
                        mm = pe.matmul(pair(bX, h, 0), heads(BP[p], c)[:, h, :], half(T32, None, 0, 32)[h], start=True, stop=True)
                    mm.then_inc(C["x32"].sem, 1)

                def ld(n, p, c):
                    wait(pe, C["xe32"], n, c + 1)
                    u = U32[c % 2]
                    for h in range(HG):
                        pe.matmul(bZ[0:64, 32 * h:32 * h + 32], heads(u)[:, h, 0:64], heads(X32)[:, h, 0:32], start=True, stop=True)
                    for h in range(HG):
                        mm = pe.matmul(pair(bZ, h, 256), heads(X32)[:, h, :], half(u, None, 1, 32)[h], start=True, stop=True)
                    mm.then_inc(C["z32"].sem, 1)

                def le(n, p, c):
                    wait(pe, C["u64"], n, c + 1)
                    for h in range(HG):
                        mm = pe.matmul(bX[64:128, 64 * h:64 * h + 64], heads(BP[p], c)[:, h, 64:128], heads(T32)[:, h, 0:64],
                                       start=True, stop=True)
                    mm.then_inc(C["x64"].sem, 1)

                def lf(n, p, c):
                    wait(pe, C["xe64"], n, c + 1)
                    for h in range(HG):
                        mm = pe.matmul(bZ[0:64, 64 * h:64 * h + 64], X64[:, 64 * h:64 * h + 64], heads(U32[c % 2])[:, h, 64:128],
                                       start=True, stop=True)
                    mm.then_inc(C["z64"].sem, 1)

                def ra(n, p, c):
                    if c == 0:
                        return
                    wait(pe, C["s"], n, c)
                    wait(pe, C["oe"], n, c)
                    pe.matmul(bO[:, :], KT[p][:, c * P:(c + 1) * P], S[:, :], start=True, stop=True).then_inc(C["ks"].sem, 1)

                def rb(n, p, c):
                    if c:
                        wait(pe, C["rr"], n, c)
                    else:
                        wait(pe, C["vn"], n, 1)
                    wait(pe, C["uf"], n, c + 1)
                    wait(pe, C["ye"], n, c)
                    for h in range(HG):
                        rhs = Rb[:, h * P:(h + 1) * P] if c else Vn[p][:, 0:P]
                        mm = pe.matmul(bY[:, h * P:(h + 1) * P], heads(U32[c % 2])[:, h, :], rhs, start=True, stop=True)
                    mm.then_inc(C["y"].sem, 1)

                def rc(n, p, c):
                    wait(pe, C["ye"], n, c + 1)
                    wait(pe, C["pt"], n, c + 1)
                    if c:
                        wait(pe, C["qt"], n, c)
                    else:
                        wait(pe, C["oe"], n, 0)
                    for h in range(HG):
                        if c:
                            pe.matmul(bO[:, h * P:(h + 1) * P], heads(QT[p], c)[:, h, :], S[:, h * P:(h + 1) * P],
                                      start=True, stop=False)
                        mm = pe.matmul(bO[:, h * P:(h + 1) * P], heads(PT[p], c)[:, h, :], Yb[:, h * P:(h + 1) * P],
                                       start=(c == 0), stop=True)
                    mm.then_inc(C["o"].sem, 1)
                    if c == NC - 1:
                        return
                    wait(pe, C["kh"], n, c + 1)
                    if c == 0:
                        wait(pe, C["s"], n, 0)
                    for h in range(HG):
                        mm = pe.matmul(bS[:, h * P:(h + 1) * P], Kh[c % 2][:, h * P:(h + 1) * P], Yb[:, h * P:(h + 1) * P],
                                       start=True, stop=True)
                    mm.then_inc(C["su"].sem, 1)

                pe.sem_inc(C["outp"].sem, 1)
                bodies(pe, dict(
                    P=project, G=lambda n, p, t: project(n, p, t + 6), GR=gram, GT=gram_t,
                    TK=rows_of(KT, "silu", 1, "TK", "tkp"), TV=rows_of(VT, "silu", 2, "TV", "tvp"),
                    SK=stats_k, SQ=stats_q, E=exponent, QR=row_g, QK=qk, OT=out_t, OUT=out_proj,
                    La=la, Lb=lb_, Lc=lc, Ld=ld, Le=le, Lf=lf, Ra=ra, Rb=rb, Rc=rc))

            @block.scalar
            def _(act):
                def conv_start(n, p, t):
                    if t == 0:
                        wait(act, C["cl"], n, 1)
                    wait(act, C["proj"], n, t + 1)
                    wait(act, C["silu"], n, t - 1)
                    act.activation(cacc[t % 2][:, :], bank(f"P{t}")[:, :], ACT.Identity,
                                   scale=cwt[:, t, 3:4]).then_inc(C["acc_"].sem, 1)

                def silu_tanh(n, p, t):
                    wait(act, C["conv"], n, 3 * t + 3)
                    wait(act, C["silu"], n, t - 1)
                    if t < 2:
                        wait(act, C["gate"], n - 1, HG)
                    act.activation(th[t % 2][:, :], cacc[t % 2][:, :], ACT.Tanh, scale=0.5).then_inc(C["th"].sem, 1)

                def gate_tanh(n, p, h):
                    wait(act, C["proj"], n, 7 + h)
                    if h < 2:
                        wait(act, C["silu"], n, 6)
                    else:
                        wait(act, C["gate"], n, h - 1)
                    act.activation(th[h % 2][:, :], bank(f"G{h}")[:, :], ACT.Tanh, scale=0.5).then_inc(C["th"].sem, 1)

                def gram_scaled(n, p, _):
                    wait(act, C["nk"], n, RSQRT_STEPS + 1)
                    wait(act, C["grp"], n, 1)
                    for c in range(NC):
                        last = act.activation(gsb[:, c * P:(c + 1) * P], bank("GR")[:, c * P:(c + 1) * P], ACT.Identity,
                                              scale=rk[p][:, c:c + 1])
                    last.then_inc(C["gh"].sem, 1)

                def k_rows(n, p, _):
                    wait(act, C["tkp"], n, 1)
                    wait(act, C["kh"], n - 2, 3)
                    act.copy(Kn[p][:, :], bank("TK")[:, :]).then_inc(C["kn"].sem, 1)

                def v_rows(n, p, _):
                    wait(act, C["tvp"], n, 1)
                    wait(act, C["rr"], n - 2, 3)
                    act.mul(Vn[p][:, :], bank("TV")[:, :], 0.5).then_inc(C["vn"].sem, 1)

                def decay(n, p, c):
                    wait(act, C["ep"], n, c + 1)
                    wait(act, C["o"], n - 2, c + 1)
                    act.activation(PT[p][:, c * SEQ:(c + 1) * SEQ], bank(f"E{c}")[:, :], ACT.Exp).then_inc(C["e"].sem, 1)

                def row_decay(n, p, c):
                    wait(act, C["qrp"], n, c)
                    wait(act, C["bp"], n, 4)
                    wait(act, C["qt"], n, c - 1)
                    act.activation(gr[:, :], bank(f"QR{c}")[:, :], ACT.Exp).then_inc(C["eq"].sem, 1)

                def lc(n, p, c):
                    wait(act, C["x32"], n, c + 1)
                    act.mul(halves(X32, 0, 0, 32), bX[:, 0:256].rearrange("p (g u) -> p g u", u=32), -1.0).then_inc(C["xe32"].sem, 1)

                def le(n, p, c):
                    wait(act, C["x64"], n, c + 1)
                    act.mul(X64[64:128, :], bX[64:128, 0:256], -1.0).then_inc(C["xe64"].sem, 1)

                def lf(n, p, c):
                    wait(act, C["z64"], n, c + 1)
                    act.copy(heads(U32[c % 2])[0:64, :, 64:128],
                             bZ[0:64, 0:256].rearrange("p (h u) -> p h u", h=HG)).then_inc(C["uf"].sem, 1)

                def rb(n, p, c):
                    wait(act, C["y"], n, c + 1)
                    act.copy(Yb[:, :], bY[:, :]).then_inc(C["ye"].sem, 1)

                def rc(n, p, c):
                    wait(act, C["o"], n, c + 1)
                    wait(act, C["otp"], n - 1, c + 1)
                    act.copy(OB[:, c * SEQ:(c + 1) * SEQ], bO[:, :]).then_inc(C["oe"].sem, 1)

                def scale_out(n, p, c):
                    wait(act, C["nf"], n, RSQRT_STEPS + 4)
                    for h in range(HG):
                        o = OB[:, c * SEQ + h * P:c * SEQ + (h + 1) * P]
                        last = act.activation(o, o, ACT.Identity, scale=fo[:, 4 * c + h:4 * c + h + 1])
                    last.then_inc(C["fs"].sem, 1)

                bodies(act, dict(P=conv_start, H=silu_tanh, G=gate_tanh, GS=gram_scaled, TK=k_rows, TV=v_rows, E=decay,
                                  QR=row_decay, OT=scale_out, Lc=lc, Le=le, Lf=lf, Rb=rb, Rc=rc))

            @block.vector
            def _(dve):
                def conv(n, p, t):
                    wait(dve, C["acc_"], n, t + 1)
                    a, b = cacc[t % 2], bank(f"P{t}")
                    for d in range(1, 4):
                        if d > 1:
                            wait(dve, C["conv"], n, 3 * t + d - 1)
                        dve.scalar_tensor_tensor(a[:, d:SEQ], b[:, 0:SEQ - d], cwt[:, t, 3 - d:4 - d], a[:, d:SEQ],
                                                 ALU.mult, ALU.add).then_inc(C["conv"].sem, 1)

                def silu(n, p, t):
                    wait(dve, C["th"], n, t + 1)
                    if t == 0:
                        wait(dve, C["ks"], n - 2, 3)
                        dst = KT[p][:, :]
                    elif t == 1:
                        wait(dve, C["gtp"], n - 1, 1)
                        dst = VT[:, :]
                    else:
                        wait(dve, C["o"], n - 2, 4)
                        dst = QT[p][:, :].rearrange("p (c h t) -> p c h t", c=NC, h=HG)[:, :, t - 2, :]
                    a, b = th[t % 2][:, :], cacc[t % 2][:, :]
                    if t >= 2:
                        a, b = (v.rearrange("p (c t) -> p c t", c=NC) for v in (a, b))
                    dve.scalar_tensor_tensor(dst, a, 1.0, b, ALU.add, ALU.mult).then_inc(C["silu"].sem, 1)

                def gate(n, p, h):
                    wait(dve, C["th"], n, 7 + h)
                    wait(dve, C["ot"], n - 2, 4)
                    dve.scalar_tensor_tensor(SG[p][:, h * SEQ:(h + 1) * SEQ], th[h % 2][:, :], 1.0, bank(f"G{h}")[:, :],
                                             ALU.add, ALU.mult).then_inc(C["gate"].sem, 1)

                def stats_k(n, p, _):
                    tx, hx, ty, tt = (t[:, 0:NC] for t in newton)
                    wait(dve, C["stat"], n, 1)
                    dve.tensor_scalar(tx, bank("SK")[:, 0:NC], 4e-6, None, ALU.add).then_inc(C["nk"].sem, 1)
                    rsqrt_steps(dve, C["nk"].sem, C["nk"].after(n, 1), tx, hx, rk[p][:, :], tt)
                    wait(dve, C["nk"], n, RSQRT_STEPS + 1)
                    wait(dve, C["kh"], n - 2, 3)
                    r = each(rk[p][:, :], HG)
                    g = bass.ds(n * 16, 16)

                    def by(t):
                        return t.rearrange("p (c h) -> p c h", c=NC)
                    dve.tensor_tensor(by(wk[p][:, :]), by(wK[:, g]), r, ALU.mult).then_inc(C["nk"].sem, 1)
                    dve.scalar_tensor_tensor(by(sR[p][:, :]), by(eG[:, g]), -1.0, r, ALU.mult, ALU.mult).then_inc(C["nk"].sem, 1)
                    dve.tensor_copy(dec[p][:, :], eGC[:, g]).then_inc(C["nk"].sem, 1)

                def gram_cols(n, p, _):
                    wait(dve, C["gtp"], n, 1)
                    wait(dve, C["qt"], n - 1, 3)
                    for c in range(NC):
                        last = dve.scalar_tensor_tensor(gr[:, c * P:(c + 1) * P], bank("GT")[:, c * P:(c + 1) * P],
                                                        rk[p][:, c:c + 1], cs[:, C_STR:C_STR + P], ALU.mult, ALU.mult)
                    last.then_inc(C["gr"].sem, 1)

                def stats_q(n, p, c):
                    if c < NC - 1:
                        return
                    tx, hx, ty, tt = (t[:, :] for t in newton)
                    wait(dve, C["sqp"], n, 4)
                    dve.tensor_scalar(tx, bank("SQ0")[:, 0:16], 4e-6, None, ALU.add).then_inc(C["nq"].sem, 1)
                    rsqrt_steps(dve, C["nq"].sem, C["nq"].after(n, 1), tx, hx, ty, tt)
                    wait(dve, C["nq"], n, RSQRT_STEPS + 1)
                    dve.tensor_scalar(cq[p][:, :], ty, float(P) ** -0.5, None, ALU.mult).then_inc(C["nq"].sem, 1)

                def weigh(n, p, c):
                    wait(dve, C["qkp"], n, c + 1)
                    wait(dve, C["bp"], n, c + 1)
                    t = PT[p][:, c * SEQ:(c + 1) * SEQ]
                    dve.scalar_tensor_tensor(t, bank(f"QK{c}")[:, :], rk[p][:, c:c + 1], t,
                                             ALU.mult, ALU.mult).then_inc(C["pt"].sem, 1)

                def la(n, p, c):
                    wait(dve, C["x16"], n, c + 1)
                    neg = cs[:, C_NEG:C_NEG + 64].unsqueeze(1).to_broadcast([P, HG, 64])
                    dve.tensor_tensor(halves(Xf, 0, 0, 16).rearrange("p (h m) u -> p h m u", h=HG),
                                      bX[:, 0:256].rearrange("p (h m u) -> p h m u", h=HG, m=4),
                                      neg.rearrange("p h (m u) -> p h m u", m=4), ALU.mult).then_inc(C["xm"].sem, 1)

                def lb_(n, p, c):
                    wait(dve, C["z16"], n, c + 1)
                    dve.tensor_tensor(halves(T32, 0, 0, 16), bZ[:, 0:256].rearrange("p (g u) -> p g u", u=16),
                                      halves(T16, c, 0, 16), ALU.add)
                    dve.tensor_tensor(halves(U32[c % 2], 0, 1, 16), bZ[:, 256:512].rearrange("p (g u) -> p g u", u=16),
                                      halves(U16, c, 1, 16), ALU.add).then_inc(C["u32"].sem, 1)

                def ld(n, p, c):
                    wait(dve, C["z32"], n, c + 1)
                    u = heads(U32[c % 2])
                    z = bZ[:, 256:512].rearrange("p (h m u) -> p h m u", h=HG, m=2)
                    dve.tensor_copy(u[0:32, :, 32:64], z[0:32, :, 0, :])
                    dve.tensor_copy(heads(T32)[32:64, :, 0:32], bZ[32:64, 0:128].rearrange("p (h u) -> p h u", h=HG))
                    dve.tensor_copy(u[64:96, :, 96:128], z[64:96, :, 1, :]).then_inc(C["u64"].sem, 1)

                def ra(n, p, c):
                    if c == 0:
                        return
                    wait(dve, C["ks"], n, c)
                    wait(dve, C["vn"], n, 1)
                    for h in range(HG):
                        j = 4 * c + h
                        last = dve.scalar_tensor_tensor(Rb[:, h * P:(h + 1) * P], bO[:, h * P:(h + 1) * P], sR[p][:, j:j + 1],
                                                        Vn[p][:, c * P:(c + 1) * P], ALU.mult, ALU.add)
                    last.then_inc(C["rr"].sem, 1)

                def rc(n, p, c):
                    if c < NC - 1:
                        wait(dve, C["su"], n, c + 1)
                        if c == 0:
                            dve.tensor_copy(S[:, :], bS[:, :]).then_inc(C["s"].sem, 1)
                        else:
                            wait(dve, C["s"], n, c)
                            for h in range(HG):
                                j = 4 * c + h
                                s = S[:, h * P:(h + 1) * P]
                                last = dve.scalar_tensor_tensor(s, s, dec[p][:, j:j + 1], bS[:, h * P:(h + 1) * P],
                                                                ALU.mult, ALU.add)
                            last.then_inc(C["s"].sem, 1)
                    wait(dve, C["o2"], n, c + 1)
                    dve.tensor_reduce(so[p][:, 4 * c:4 * c + 4], heads(o2), AX.X, ALU.add).then_inc(C["sr"].sem, 1)

                def out_factor(n, p, _):
                    tx, hx, ty, tt = (t[:, :] for t in newton)
                    wait(dve, C["sr"], n, 4)
                    wait(dve, C["nq"], n, RSQRT_STEPS + 2)
                    dve.tensor_tensor(tx, so[p][:, :], cq[p][:, :], ALU.mult).then_inc(C["nf"].sem, 1)
                    wait(dve, C["nf"], n, 1)
                    dve.scalar_tensor_tensor(tx, tx, 1.0 / P, cq[p][:, :], ALU.mult, ALU.mult).then_inc(C["nf"].sem, 1)
                    wait(dve, C["nf"], n, 2)
                    dve.tensor_scalar(tx, tx, 1e-5, None, ALU.add).then_inc(C["nf"].sem, 1)
                    rsqrt_steps(dve, C["nf"].sem, C["nf"].after(n, 3), tx, hx, ty, tt)
                    wait(dve, C["nf"], n, RSQRT_STEPS + 3)
                    dve.tensor_tensor(fo[:, :], ty, cq[p][:, :], ALU.mult).then_inc(C["nf"].sem, 1)

                def gated(n, p, c):
                    wait(dve, C["otp"], n, c + 1)
                    wait(dve, C["outp"], n, max(c - 1, 0))
                    sg = SG[p][:, :].rearrange("p (h t) -> p h t", h=HG)[:, :, c * P:(c + 1) * P]
                    dve.scalar_tensor_tensor(heads(OT[c % 2]), bank(f"OT{c}")[:, :].rearrange("p (h t) -> p h t", h=HG),
                                             wv[:, 0:1], sg, ALU.mult, ALU.mult).then_inc(C["ot"].sem, 1)

                def add_out(n, p, c):
                    wait(dve, C["outp"], n, c + 1)
                    a = acc[:, bass.ds((n // NG) * (NC * D) + c * D, D)]
                    dve.tensor_tensor(a, bank(f"OUT{c}")[:, 0:D], a, ALU.add).then_inc(C["acc"].sem, 1)

                bodies(dve, dict(P=conv, H=silu, G=gate, SK=stats_k, GT=gram_cols, SQ=stats_q, QK=weigh,
                                  La=la, Lb=lb_, Ld=ld, Ra=ra, Rc=rc, FN=out_factor, OT=gated, OUT=add_out))

            @block.gpsimd
            def _(pool):
                def square_k(n, p, t):
                    if t:
                        return
                    wait(pool, C["silu"], n, 1)
                    wait(pool, C["sqp"], n - 1, 4)
                    pool.tensor_tensor(sqr[:, :], KT[p][:, :], KT[p][:, :], ALU.mult).then_inc(C["sq"].sem, 1)

                def square_q(n, p, c):
                    wait(pool, C["silu"], n, 6)
                    wait(pool, C["sqp"], n, c)
                    wait(pool, C["stat"], n, 1)
                    q = QT[p][:, c * SEQ:(c + 1) * SEQ]
                    pool.tensor_tensor(sqr[:, :], q, q, ALU.mult).then_inc(C["sq"].sem, 1)

                def build_b(n, p, c):
                    wait(pool, C["e"], n, c + 1)
                    if c == 0:
                        wait(pool, C["gr"], n, 1)
                    g = gr[:, c * P:(c + 1) * P].unsqueeze(1).to_broadcast([P, HG, P])
                    pool.tensor_tensor(heads(BP[p], c), heads(PT[p], c), g, ALU.mult).then_inc(C["bp"].sem, 1)

                def q_decay(n, p, c):
                    wait(pool, C["eq"], n, c)
                    wait(pool, C["qkp"], n, c + 1)
                    q = QT[p][:, c * SEQ:(c + 1) * SEQ]
                    pool.tensor_tensor(q, q, gr[:, :], ALU.mult).then_inc(C["qt"].sem, 1)

                def invert_blocks(n, p, _):
                    sub = C["sub"]
                    eye = cs[:, C_EYE:C_EYE + 256].rearrange("p (r t) -> p r t", r=16)
                    pool.tensor_copy(blkU[:, :, :], eye).then_inc(sub.sem, 1)
                    wait(pool, C["dgr"], n, 1)
                    wait(pool, C["tuw"], n - 1, 2)
                    k = 1
                    for s in range(15, 0, -1):
                        w = 16 - s
                        t = blkt[:, 0:s * w].rearrange("p (r t) -> p r t", r=s)
                        col = blkB[:, 0:s, s:s + 1].to_broadcast([P, s, w])
                        row = blkU[:, s:s + 1, s:16].to_broadcast([P, s, w])
                        wait(pool, sub, n, k)
                        pool.tensor_tensor(t, col, row, ALU.mult).then_inc(sub.sem, 1)
                        k += 1
                        wait(pool, sub, n, k)
                        u = blkU[:, 0:s, s:16]
                        pool.tensor_tensor(u, u, t, ALU.subtract).then_inc(sub.sem, 1)
                        k += 1
                    wait(pool, sub, n, k)
                    for a, src in ((0, blkU[:, :, :].rearrange("p r t -> p t r")), (1, blkU[:, :, :])):
                        for half, mcol in ((0, C_EVEN), (1, C_ODD)):
                            last = pool.tensor_tensor(blkO[:, a, :, 16 * half:16 * half + 16], src,
                                                      cs[:, mcol:mcol + 1].unsqueeze(2).to_broadcast([P, 16, 16]), ALU.mult)
                            if half:
                                last.then_inc(sub.sem, 1)

                def lb_(n, p, c):
                    wait(pool, C["x16"], n, c + 1)
                    if c == 0:
                        wait(pool, C["tur"], n, 16)

                    one = cs[:, C_ONES:C_ONES + 1].unsqueeze(2).to_broadcast([P, 16, 16])
                    pool.tensor_tensor(halves(T32, 0, 1, 16), halves(T16, c, 1, 16), one, ALU.mult)
                    pool.tensor_copy(halves(U32[c % 2], 0, 0, 16), halves(U16, c, 0, 16)).then_inc(C["cp"].sem, 1)

                def k_scaled(n, p, c):
                    if c == NC - 1:
                        return
                    wait(pool, C["nk"], n, RSQRT_STEPS + 4)
                    wait(pool, C["kn"], n, 1)
                    wait(pool, C["su"], n, c - 1 if c else 0)
                    k = Kn[p][:, c * P:(c + 1) * P].unsqueeze(1).to_broadcast([P, HG, P])
                    pool.tensor_tensor(heads(Kh[c % 2]), k, each(wk[p][:, 4 * c:4 * c + 4]), ALU.mult).then_inc(C["kh"].sem, 1)

                def square_o(n, p, c):
                    wait(pool, C["oe"], n, c + 1)
                    wait(pool, C["sr"], n, c)
                    o = OB[:, c * SEQ:(c + 1) * SEQ]
                    pool.tensor_tensor(o2[:, :], o, o, ALU.mult).then_inc(C["o2"].sem, 1)

                bodies(pool, dict(H=square_k, SQ=square_q, E=build_b, QR=q_decay, IV=invert_blocks, Lb=lb_, Ra=k_scaled, Rc=square_o))

            @block.sync
            def _(sp):
                def weights(n, name, lo, hi):
                    wait(sp, C["proj"], n - 1, hi)
                    sp.dma_start(wt[:, lo:hi], wa[bass.ds(n % NG, 1), :, lo:hi].rearrange("a p t k o -> (a p) t k o")
                                 ).then_inc(C[name].sem, 16)

                def taps(n):
                    wait(sp, C["conv"], n - 1, 18)
                    sp.dma_start(cwt[:], cw[bass.ds(n % NG, 1)].rearrange("a p t i -> (a p) t i")).then_inc(C["cl"].sem, 16)

                def row_parts(n):
                    wait(sp, C["ep"], n - 1, 4)
                    wait(sp, C["qrp"], n - 1, 3)
                    i = n % NI
                    for a in range(3):
                        g = rows[bass.ds(i * 16, 16), a, :].rearrange("(o r) t -> o r t", o=1)
                        sp.dma_start(GX[a:a + 1].rearrange("p c (h t) -> p (c h) t", h=HG), g).then_inc(C["rowl"].sem, 16)
                        h = rows[bass.ds(256 + i * 16, 16), a, :].rearrange("(c h) t -> h c t", h=HG)
                        sp.dma_start(HX[3 + 4 * a:7 + 4 * a], h).then_inc(C["rowl"].sem, 16)

                def out_weights(n):
                    wait(sp, C["outp"], n - 1, 4)
                    sp.dma_start(wot[:], wo[bass.ds(n % NG, 1)].rearrange("a p h d -> (a p) h d")).then_inc(C["wol"].sem, 16)

                def blocks_out(n, p):
                    wait(sp, C["bp"], n, 4)
                    for b in range(8):
                        src = BP[p][16 * b:16 * b + 16, :].rearrange("p (u t) -> p u t", t=P)[:, :, 16 * b:16 * b + 16]
                        dst = diag.rearrange("(u b) r t -> b r u t", b=8)[b]
                        sp.dma_start(dst, src).then_inc(C["dgw"].sem, 16)
                    wait(sp, C["dgw"], n, 8)
                    wait(sp, C["sub"], n - 1, 34 - 1)
                    sp.dma_start(blkB[:], diag).then_inc(C["dgr"].sem, 16)

                def inverses(n):
                    wait(sp, C["sub"], n, 33)
                    if not (isinstance(n, int) and n == 0):
                        wait(sp, C["tur"], n - 1, 16)
                    for a in range(2):
                        sp.dma_start(tri_d[:, a], blkO[:, a]).then_inc(C["tuw"].sem, 16)
                    wait(sp, C["tuw"], n, 2)
                    wait(sp, C["z16"], n - 1, 4)
                    wait(sp, C["u32"], n - 1, 4)
                    wait(sp, C["cp"], n - 1, 4)
                    for a, t in enumerate((T16, U16)):
                        for b in range(8):
                            lo = 32 * (b // 2)
                            dst = t[16 * b:16 * b + 16, :].rearrange("p (u t) -> p u t", t=P)[:, :, lo:lo + 32]
                            src = tri_d[:, a].rearrange("(u b) r t -> b r u t", b=8)[b]
                            sp.dma_start(dst, src).then_inc(C["tur"].sem, 16)

                def body(k, p):
                    n = k + 1
                    blocks_out(n, (p + 1) % 2)
                    weights(n + 1, "wkv", 0, 2)
                    weights(n + 1, "wq", 2, 6)
                    taps(n + 1)
                    inverses(n)
                    row_parts(n + 1)
                    weights(n + 1, "wg", 6, NT)

                weights(0, "wkv", 0, 2)
                taps(0)
                row_parts(0)
                weights(0, "wq", 2, 6)
                weights(0, "wg", 6, NT)
                out_weights(0)
                body(-1, 1)
                body(0, 0)
                with sp.Fori(0, (NI - 2) // 2) as i:
                    body(2 * i + 1, 1)
                    out_weights(2 * i + 1)
                    body(2 * i + 2, 0)
                    out_weights(2 * i + 2)
                out_weights(NI - 1)
                for name, m in (("wkv", 1), ("wq", 1), ("wg", 1), ("cl", 1), ("rowl", 6)):
                    wait(sp, C[name], NI, m)

        FP = FM * P
        raw = [QT[0][:, 0:KD * F], QT[1][:, 0:KD * F], PT[0][:, 0:5 * D], PT[0][0:FR, 5 * D:6 * D]]
        w12 = [t[:, 0:KD * FP // 2].bitcast(BF16).rearrange("p (k f) -> p k f", k=KD) for t in (PT[1], SG[0])]
        lowt = BP[0][:, 0:KD * F]
        q3 = BP[1][:, 0:6 * D].rearrange("p (m d) -> p m d", m=6)
        parts = [t[:, :].bitcast(BF16).rearrange("p (k t) -> p k t", k=KD) for t in (T16, U16, OB)]
        hid = [QT[m // 3][:, (m % 3) * SEQ:(m % 3 + 1) * SEQ] for m in range(6)]
        xin = [Kn[j][:, 0:D] for j in range(2)]
        fin = [Vn[j][:, 0:D] for j in range(2)]
        tg = [Kh[j][:, 0:D] for j in range(2)]
        ug = [OT[j][:, 0:D] for j in range(2)]
        sums, thr, nthr = newton[0][:, 0:4], newton[1][:, 0:4], newton[2][:, 0:4]
        with nc.Block() as block:
            f_w, f_sum, f_tot, f_q, f_lo = (sem(x) for x in ("ffn_w_loaded", "abs_sums", "abs_totals", "ternary_steps", "split_low"))
            f_up, f_th, f_hid, f_dn, f_tg = (sem(x) for x in ("up_ready", "up_tanh", "hidden_ready", "down_ready", "down_tanh"))
            f_ug, f_xin, f_fin, f_st = (sem(x) for x in ("gated_steps", "x_reloaded", "final_ready", "stored"))

            @block.sync
            def _(sp):
                sp.sem_inc(f_st, 16)
                sp.dma_start(raw[0].rearrange("p (k f) -> p k f", k=KD), w1t.rearrange("(k p) f -> p k f", k=KD)).then_inc(f_w, 16)
                sp.dma_start(raw[1].rearrange("p (k f) -> p k f", k=KD), w2t.rearrange("(k p) f -> p k f", k=KD)).then_inc(f_w, 16)
                sp.dma_start(raw[2].rearrange("p (m d) -> p m d", m=5), w3t[0:5 * P].rearrange("(m p) d -> p m d", m=5)).then_inc(f_w, 16)
                sp.dma_start(raw[3], w3t[5 * P:F]).then_inc(f_w, 16)
                with sp.Fori(0, NB) as b:
                    for c in range(NC):
                        t = b * NC + c
                        sp.wait_ge(f_fin, t + 1 if c == 0 else t)
                        sp.dma_start(xin[c % 2], x[bass.ds(t * P, P), :]).then_inc(f_xin, 16)
                        sp.wait_ge(f_fin, t + 2)
                        sp.dma_start(out[bass.ds(t * P, P), :], fin[c % 2]).then_inc(f_st, 16)
                sp.wait_ge(f_st, 16 * NB * NC + 16)

            @block.vector
            def _(dve):
                for x1 in (f_hid, f_ug, f_fin):
                    dve.sem_inc(x1, 1)
                dve.wait_ge(f_w, 64)
                dve.memset(sums, 0.0).then_inc(f_sum, 1)
                dve.wait_ge(f_sum, 1)
                for j in range(4):
                    r = FR if j == 3 else P
                    dve.tensor_reduce(sums[0:r, j:j + 1], raw[j], AX.X, ALU.add, apply_absolute_value=True).then_inc(f_sum, 1)
                dve.wait_ge(f_tot, 1)
                half_mean = 0.5 / (F * D)
                dve.tensor_scalar(thr[:, 0:3], banks[0][:, 0:3], half_mean, 0.5e-8, ALU.mult, ALU.add).then_inc(f_q, 1)
                dve.tensor_scalar(nthr[:, 0:3], banks[0][:, 0:3], -half_mean, -0.5e-8, ALU.mult, ALU.add).then_inc(f_q, 1)
                dve.wait_ge(f_q, 2)
                for j, (dst, rows_, src) in enumerate((
                        (w12[0][:, :, 0:F], P, raw[0]), (w12[1][:, :, 0:F], P, raw[1]), (q3[:, 0:5], P, raw[2]), (q3[0:FR, 5], FR, raw[3]))):
                    col = min(j, 2)
                    low = lowt[0:rows_, 0:src.shape[1]]
                    if j:
                        dve.wait_ge(f_q, 2 + 2 * j)
                    dve.tensor_scalar(low, src, nthr[0:rows_, col:col + 1], None, ALU.is_lt).then_inc(f_q, 1)
                    dve.wait_ge(f_q, 3 + 2 * j)
                    if j < 2:
                        dst, src, low = (dst, *(v.rearrange("p (k f) -> p k f", k=KD) for v in (src, low)))
                    elif j == 2:
                        src, low = (v.rearrange("p (m d) -> p m d", m=5) for v in (src, low))
                    dve.scalar_tensor_tensor(dst, src, thr[0:rows_, col:col + 1], low, ALU.is_gt, ALU.subtract).then_inc(f_q, 1)

                for z in (w12[0][:, :, F:FP], w12[1][:, :, F:FP], q3[FR:P, 5]):
                    dve.memset(z, 0.0).then_inc(f_q, 1)

                def split(b):
                    at = bass.ds(b * SEQ, SEQ)
                    r = xnT[:, :, at]
                    for j in range(3):
                        if j:
                            dve.wait_ge(f_lo, b * 5 + 2 * j)
                        dve.tensor_copy(parts[j][:, :, at], r).then_inc(f_lo, 1)
                        if j < 2:
                            dve.wait_ge(f_lo, b * 5 + 2 * j + 1)
                            dve.tensor_tensor(r, r, parts[j][:, :, at], ALU.subtract).then_inc(f_lo, 1)

                for b in range(NB):
                    split(b)
                with dve.Fori(0, NB) as b:
                    for m in range(FM):
                        dve.wait_ge(f_th, b * FM + m + 1)
                        dve.wait_ge(f_dn, b * NC + 1)
                        dve.scalar_tensor_tensor(hid[m], th[m % 2][:, :], 1.0, banks[2 + m % 2][:, :],
                                                 ALU.add, ALU.mult).then_inc(f_hid, 1)
                    for c in range(NC):
                        t = b * NC + c
                        dve.wait_ge(f_tg, t + 1)
                        dve.scalar_tensor_tensor(ug[c % 2], tg[c % 2], 1.0, banks[4 + c % 2][:, 0:D], ALU.add, ALU.mult).then_inc(f_ug, 1)
                        dve.wait_ge(f_ug, 2 * t + 2)
                        dve.scalar_tensor_tensor(ug[c % 2], ug[c % 2], 0.25, acc[:, bass.ds(t * D, D)], ALU.mult, ALU.mult).then_inc(f_ug, 1)
                        dve.wait_ge(f_ug, 2 * t + 3)
                        dve.wait_ge(f_xin, 16 * t + 16)
                        dve.wait_ge(f_st, 16 * t + 16 if c == 0 else 16 * t)
                        dve.tensor_tensor(fin[c % 2], ug[c % 2], xin[c % 2], ALU.add).then_inc(f_fin, 1)

            @block.scalar
            def _(act):
                with act.Fori(0, NB) as b:
                    for m in range(FM):
                        act.wait_ge(f_up, b * FM + m + 1)
                        act.wait_ge(f_hid, b * FM + (m or 1))
                        act.activation(th[m % 2][:, :], banks[m % 2][:, :], ACT.Tanh, scale=0.5).then_inc(f_th, 1)
                    for c in range(NC):
                        t = b * NC + c
                        act.wait_ge(f_dn, t + 2)
                        act.wait_ge(f_ug, 2 * t - 1 if c > 0 else 2 * t + 1)
                        act.activation(tg[c % 2], banks[4 + c % 2][:, 0:D], ACT.Tanh, scale=0.25).then_inc(f_tg, 1)

            @block.tensor
            def _(pe):
                pe.sem_inc(f_dn, 1)
                pe.wait_ge(f_sum, 5)
                pe.matmul(banks[0][:, 0:2], cs[:, C_ONES:C_ONES + P], sums[:, 0:2], start=True, stop=True)
                pe.matmul(banks[0][:, 2:3], cs[:, C_ONES:C_ONES + P], sums[:, 2:3], start=True, stop=False)
                pe.matmul(banks[0][:, 2:3], cs[:, C_ONES:C_ONES + P], sums[:, 3:4], start=False, stop=True).then_inc(f_tot, 1)
                pe.wait_ge(f_q, 13)
                pe.wait_ge(f_lo, 5 * NB)
                with pe.Fori(0, NB) as b:
                    at = bass.ds(b * SEQ, SEQ)
                    for m in range(FM):
                        pe.wait_ge(f_hid, b * FM + (m or 1))
                        for w in range(2):
                            o = banks[2 * w + m % 2][:, :]
                            for kk in range(KD):
                                for a in range(3):
                                    mm = pe.matmul(o, w12[w][:, kk, m * P:(m + 1) * P], parts[a][:, kk, at],
                                                   start=(kk == 0 and a == 0), stop=(kk == KD - 1 and a == 2))
                        mm.then_inc(f_up, 1)
                    for c in range(NC):
                        t = b * NC + c
                        if c == 0:
                            pe.wait_ge(f_hid, b * FM + FM + 1)
                            pe.wait_ge(f_ug, 2 * t + 1)
                        else:
                            pe.wait_ge(f_ug, 2 * t - 1)
                        for m in range(FM):
                            mm = pe.matmul(banks[4 + c % 2][:, 0:D], hid[m][:, c * P:(c + 1) * P], q3[:, m, :],
                                           start=(m == 0), stop=(m == FM - 1))
                        mm.then_inc(f_dn, 1)


def constants():
    import numpy as np
    p, t = np.arange(P)[:, None], np.arange(P)[None, :]
    c = np.zeros((P, C_END), np.float32)
    c[:, C_ID:C_ID + P] = p == t
    c[:, C_TRI:C_TRI + P] = p <= t
    c[:, C_STR:C_STR + P] = p < t
    c[:, C_CAU:C_CAU + P] = np.where(p <= t, 0.0, -1e30)
    head = np.arange(HG * P)[None, :] // P
    c[:, C_IND:C_IND + HG * P] = (p >= 3) & (p < 15) & ((p - 3) % HG == head)
    c[:, C_THREE:C_THREE + P] = p < 3
    j = np.arange(64)[None, :]
    c[:, C_NEG:C_NEG + 64] = np.where((p // 32 == j // 16) & (p % 32 >= 16), -1.0, 0.0)
    c[:, C_EVEN] = np.arange(P) % 2 == 0
    c[:, C_ODD] = np.arange(P) % 2 == 1
    c[:, C_ONES:C_ONES + P] = 1.0
    c[:, C_EYE:C_EYE + 256] = np.eye(16, dtype=np.float32).reshape(1, 256)
    return c


def kernel(**inputs):
    import numpy as np
    import concourse.bacc as bacc
    from concourse import mybir as mb
    from concourse.bass_utils import run_bass_kernel_spmd

    a = {k.replace("L0_", ""): np.ascontiguousarray(v) for k, v in inputs.items()}
    qkv = a["attn_qkv_w"].reshape(6 * HG, P, D)
    tap = a["attn_conv_w"].reshape(6 * HG, P, 4)
    gw = a["attn_g_w"].reshape(4 * HG, P, D)
    order = [[16 + g, 20 + g] + [4 * g + h for h in range(HG)] for g in range(NG)]
    tiles = np.stack([np.concatenate([qkv[order[g]], gw[4 * g:4 * g + 4]]) for g in range(NG)])
    arrays = {
        "x": a["attn_hidden_states"].reshape(NI * P, D),
        "wa": tiles.reshape(NG, NT, P, KD, P).transpose(0, 4, 1, 3, 2),
        "cw": np.stack([tap[order[g]] for g in range(NG)]).transpose(0, 2, 1, 3),
        "bgk": np.concatenate([a["attn_gk_w"], a["attn_b_w"]]).reshape(32, KD, P).transpose(2, 1, 0),
        "wo": a["attn_o_w"].reshape(D, NG, HG, P).transpose(1, 3, 2, 0),
        "onw": a["attn_out_norm_w"].reshape(P, 1),
        "w1t": a["ffn_w1"].T, "w2t": a["ffn_w2"].T, "w3t": a["ffn_w3"].T,
        "cst": constants(),
    }
    arrays = {f"in_{k}": np.ascontiguousarray(v) for k, v in arrays.items()}
    nc = bacc.Bacc("TRN2", target_bir_lowering=False, num_devices=1)
    args = {k[3:]: nc.dram_tensor(k, v.shape, mb.dt.from_np(v.dtype), kind="ExternalInput").ap() for k, v in arrays.items()}
    args["rows"] = nc.dram_tensor("rows", (4 * P, 3, P), BF16, kind="Internal").ap()
    args["diag"] = nc.dram_tensor("diag", (P, 16, 16), F32, kind="Internal").ap()
    args["tri_d"] = nc.dram_tensor("tri_d", (P, 2, 16, 32), F32, kind="Internal").ap()
    out = nc.dram_tensor("out", (NI * P, D), F32, kind="ExternalOutput").ap()
    attention_kernel(nc, out=out, **args)
    r = run_bass_kernel_spmd(nc, [arrays], core_ids=[0])
    return r.results[0]["out"].reshape(NB, SEQ, D)
```

```python
from contextlib import ExitStack

import concourse.bass as bass
from concourse import mybir

F32 = mybir.dt.float32
BF16 = mybir.dt.bfloat16
I32 = mybir.dt.int32
ALU = mybir.AluOpType
ACT = mybir.ActivationFunctionType
AX = mybir.AxisListType

P = 128
NB = 4
HG = 4
NC = 4
SEQ = NC * P
NG = 4
NI = NB * NG
D = 256
KD = D // P
F = 704
FM = 6
FR = F - (FM - 1) * P
NT = 2 * HG + 2
RSQRT_SEED = float(0x5F3759DF)
OUT_EPS = 1e-5
NEWTON = 3

C_ID, C_STR, C_ONES, C_EYE, C_NEG, C_EVEN, C_ODD = 0, 128, 256, 384, 640, 704, 705
C_ALL = 706
C_CAU, C_IND, C_THREE, C_TRI = C_ALL, C_ALL + P, C_ALL + P + HG * P, C_ALL + (2 + HG) * P
C_END = C_TRI + P


class Count:

    def __init__(self, sem, per, step=1, start=0):
        self.sem, self.per, self.step, self.start = sem, per, step, start

    def after(self, n, k):
        return (n * self.per + k) * self.step + self.start


def wait(eng, count, n, k):
    v = count.after(n, k)
    if not isinstance(v, int) or v > count.start:
        eng.wait_ge(count.sem, v)


ORDER = dict(
    pe="""
        P0 Ra3 La0 P1 Lb0 Rb3 P2 Lc0 Rc3 Ld0 SK Le0 TV GR Lf0 E0 La1 Rb0 TK Lb1 E1 E2 Rc0 P3 Lc1 GT E3 Rd0
        Ld1 P4 OT0 Le1 P5 La2 Lf1 Ra1 OT1 Lb2 OUT0 OUT1 Rb1 Lc2 OT2 OT3 Rc1 Ld2 Rd1 OUT2 OUT3 G0 Le2 G1 La3
        Lf2 Ra2 SQ0 SQ1 Lb3 Rb2 SQ2 SQ3 QR1 Lc3 QK0 QK1 Ld3 QK2 Rc2 QK3 QR2 G2 Le3 QR3 Rd2 G3 Lf3""".split(),
    act="""
        P0 P1 Rb3 H0 Lc0 H1 SK Rc3 P2 Ro3 Le0 TV Lf0 E0 GS Rb0 TK E1 E2 H2 P3 Lc1 FS0 FS1 E3 P4 Le1 Rc0 H3
        Ro0 Lf1 FS2 P5 FS3 Rb1 Lc2 H4 H5 Rc1 Le2 Ro1 SQ0 SQ1 G0 G1 Lf2 SQ2 SQ3 Lc3 Rb2 QR1 Rc2 Ro2 QR2 QR3
        Le3 G2 G3 Lf3""".split(),
    dve="""
        Lt0 Lt1 Ra3 La0 Ca0 Cb0 Cc0 Lb0 Ca1 Cb1 Cc1 H0 H1 Ld0 Lt2 Lt3 SK Ca2 Cb2 Cc2 La1 Rs3 FN Lb1 GT Rd0
        Ld1 H2 Ca3 Cb3 Cc3 OT0 La2 H3 OT1 Ra1 Rs0 Lb2 OUT0 OUT1 Ca4 OT2 Cb4 Cc4 OT3 Ca5 Cb5 Cc5 Ld2 H4 OUT2
        Rd1 H5 Rs1 OUT3 La3 G0 Ra2 Lb3 G1 SQ3 CL QK0 QK1 Ld3 QK2 QK3 Rd2 Rs2 G2 G3""".split(),
    pool="""
        SK Rk0 Rk1 FN E0 E1 E2 E3 Rk2 IV0 IV1 IV2 QR1 QR2 QR3""".split())
BACK = ("FN", "CL", "FS", "OT", "OUT")

FREED = {"P": ("raw", 6), "SK0": ("nk", 1), "GR0": ("gh", 1), "TV0": ("vn", 1), "TK0": ("kn", 1), "GT0": ("gr", 1),
         "E": ("e", 4), "OT": ("ot", 4), "OUT": ("acc", 4), "SQ0": ("nq", 1), "QK": ("pt", 4), "QR": ("eq", 3),
         "G": ("gate", 4)}
BANKS = 3


def parts_of(stage):
    name = stage.rstrip("0123456789")
    j = int(stage[len(name):] or 0)
    if name[0] in "LR":
        return name, j, -1 if name[0] == "R" and j == NC - 1 else 0
    return name, j, -1 if name in BACK else 1


def ring():
    uses = []
    for stage in ORDER["pe"]:
        name, j, shift = parts_of(stage)
        if name in FREED:
            uses.append((stage, FREED[name][0], j if name == "QR" else j + 1, shift < 0))
        elif f"{name}{j}" in FREED:
            uses.append((f"{name}{j}", FREED[f"{name}{j}"][0], 1, False))
    return uses + [None] * (-len(uses) % BANKS)


RING = ring()
RING_AT = {u[0]: j for j, u in enumerate(RING) if u}
assert not any(u[3] for u in RING[-BANKS:] if u)


def bodies(eng, name_, stages):
    def body(k, parity):
        for stage in ORDER[name_]:
            name, j, shift = parts_of(stage)
            n = k + shift
            if not (isinstance(n, int) and not 0 <= n < NI):
                stages[name](n, (parity + shift) % 2, j)

    body(-1, 1)
    body(0, 0)
    with eng.Fori(0, (NI - 2) // 2) as i:
        body(2 * i + 1, 1)
        body(2 * i + 2, 0)
    body(NI - 1, 1)
    body(NI, 0)


RSQRT_STEPS = 3 + 3 * NEWTON


def rsqrt_steps(dve, sem, done, x, h, y, t):
    dve.wait_ge(sem, done)
    dve.tensor_scalar(h, x, -0.5, None, ALU.mult).then_inc(sem, 1)
    dve.tensor_scalar(y.bitcast(I32), x.bitcast(I32), 1, None, ALU.arith_shift_right).then_inc(sem, 1)
    dve.wait_ge(sem, done + 2)
    dve.tensor_scalar(y.bitcast(I32), y.bitcast(I32), -1.0, RSQRT_SEED, ALU.mult, ALU.add).then_inc(sem, 1)
    for i in range(NEWTON):
        dve.wait_ge(sem, done + 3 + 3 * i)
        dve.tensor_tensor(t, y, y, ALU.mult).then_inc(sem, 1)
        dve.wait_ge(sem, done + 4 + 3 * i)
        dve.tensor_tensor(t, t, h, ALU.mult).then_inc(sem, 1)
        dve.wait_ge(sem, done + 5 + 3 * i)
        dve.scalar_tensor_tensor(y, t, 1.5, y, ALU.add, ALU.mult).then_inc(sem, 1)


def attention_kernel(nc, x, wa, cw, bgk, wo, onw, w1t, w2t, w3t, cst, rows, diag, tri_d, out):
    ctx = ExitStack()
    with ctx:
        def sb(name, shape, dt=F32):
            return ctx.enter_context(nc.sbuf_tensor(name, shape, dt))

        def two(name, cols, dt=F32):
            return [sb(f"{name}{j}", [P, cols], dt) for j in range(2)]

        xnT = sb("xnT", [P, KD, NB * SEQ])
        acc = sb("acc", [P, NB * NC * D])
        cs = sb("cs", [P, C_ALL])
        cau = sb("cau", [P, P], BF16)
        idb = sb("idb", [P, P], BF16)
        one3 = sb("one3", [P, P], BF16)
        HX = sb("HX", [P, NC, P], BF16)
        GX = sb("GX", [P, NC, HG * P], BF16)
        eG, eGC, wK = sb("eG", [P, NI * 16]), sb("eGC", [P, NI * 16]), sb("wK", [P, NI * 16])
        wv = sb("wv", [P, 1])
        KT, Kn, Vn = two("KT", SEQ), two("Kn", SEQ), two("Vn", SEQ)
        QT, SG, BP, PT = two("QT", 4 * SEQ), two("SG", 4 * SEQ), two("BP", 4 * SEQ), two("PT", 4 * SEQ)
        rk, eq2, so = two("rk", NC), two("eq2", 16), two("so", 16)
        wk, sR, dec = two("wk", 16), two("sR", 16), two("dec", 16)
        T, U = sb("T", [P, 4 * SEQ]), two("U", 4 * SEQ)
        OB = sb("OB", [P, 4 * SEQ])
        wt = sb("wt", [P, 6, KD, P])
        wot = sb("wot", [P, HG, D])
        cwt = sb("cwt", [P, 6, 4])
        xr, cacc, th = two("xr", SEQ), two("cacc", SEQ), two("th", SEQ)
        sqr = two("sqr", SEQ)
        VT = sb("VT", [P, SEQ])
        gr = sb("gr", [P, SEQ])
        gsb = VT
        Xf, X32, X64 = sb("Xf", [P, SEQ]), sb("X32", [P, SEQ]), sb("X64", [P, HG * 64])
        RY = sb("RY", [P, SEQ])
        S, o2 = sb("S", [P, SEQ]), sb("o2", [P, SEQ])
        Kh, OT = two("Kh", SEQ), two("OT", SEQ)
        blkB, blkU, blkt = sb("blkB", [P, 16, 16]), sb("blkU", [P, 16, 16]), sb("blkt", [P, 64])
        blkO = sb("blkO", [P, 16, 32])
        newton = [sqr[0][:, 16 * j:16 * j + 16] for j in range(4)]
        kx, fx, fo = sb("kx", [P, NC]), sb("fx", [P, 16]), sb("fo", [P, 16])
        nhalf = sb("nhalf", [P, 16])

        banks = [ctx.enter_context(nc.psum_tensor(f"bank{j}", [P, 512], F32)) for j in range(8)]
        bX, bZ, bO, bY, bS = banks[3:8]

        def sem(name):
            return ctx.enter_context(nc.semaphore(name))

        def heads(t, c=None):
            a = t[:, :] if c is None else t[:, c * SEQ:(c + 1) * SEQ]
            return a.rearrange("p (h t) -> p h t", h=HG)

        def halves(t, c, odd, w):
            a = t[:, c * SEQ:(c + 1) * SEQ] if not isinstance(t, bass.AP) else t
            return a.rearrange("p (g a u) -> p g a u", a=2, u=w)[:, :, odd, :]

        def each(v, n=P):
            return v.unsqueeze(2).to_broadcast([P, v.shape[1], n])

        ident = cs[:, C_ID:C_ID + P]

        X = [QT[t // 8][:, (t % 8) * D:(t % 8 + 1) * D] for t in range(16)]
        bst, mv = SG[0][:, 0:96], SG[0][:, 128:160]
        zs, na, ez, spl = SG[0][:, 256:768], SG[0][:, 768:1280], SG[0][:, 1280:1792], SG[1][:, 0:512]
        gl, lb, Gs, Hs, Ws = (SG[1][:, 512 + 256 * j:768 + 256 * j] for j in range(5))
        rowf = BP[0][:, 0:512]
        rest = BP[0][:, 512:1024]
        rowp = BP[1][:, 0:768].bitcast(BF16).rearrange("p (q a t) -> p q a t", q=4, a=3)
        c0 = PT[0][:, 0:C_END - C_ALL]
        bgs = BP[1][:, 1024:1088].rearrange("p (k o) -> p k o", k=KD)
        with nc.Block() as block:
            s_x, s_c, s_bg, s_rows = sem("x_loaded"), sem("constants_loaded"), sem("bgk_loaded"), sem("rows_stored")
            s_init, s_ln, s_xt, s_xte = sem("constants_cast"), sem("layernorm_steps"), sem("x_transposed"), sem("xT_copied")
            s_z, s_zc, s_abs, s_exp, s_log = sem("z_ready"), sem("z_steps"), sem("abs_ready"), sem("exp_ready"), sem("log_ready")
            s_cum, s_g, s_w, s_rt, s_split = sem("cumsum_ready"), sem("G_steps"), sem("weights_ready"), sem("rows_transposed"), sem("split_steps")
            s_eg = sem("decays_ready")

            @block.sync
            def _(sp):
                xv = x.rearrange("(n t p) d -> n p t d", p=P, n=2)
                for j in range(2):
                    sp.dma_start(QT[j][:, :].rearrange("p (t d) -> p t d", d=D), xv[j]).then_inc(s_x, 16)
                sp.dma_start(cs[:, :], cst[:, 0:C_ALL]).then_inc(s_c, 16)
                sp.dma_start(c0, cst[:, C_ALL:C_END]).then_inc(s_c, 16)
                sp.dma_start(bgs, bgk).then_inc(s_bg, 16)
                sp.dma_start(wv[:, :], onw).then_inc(s_bg, 16)
                for q in range(4):
                    sp.wait_ge(s_split, 5)
                    sp.dma_start(rows[q * P:(q + 1) * P], rowp[:, q]).then_inc(s_rows, 16)
                sp.wait_ge(s_rows, 64)

            @block.gpsimd
            def _(pool):
                for t in (Xf, X32, X64, HX, GX):
                    pool.memset(t[:], 0.0).then_inc(s_init, 1)
                pool.memset(acc[:, :], 0.0).then_inc(s_init, 1)
                for t in U:
                    pool.memset(t[:, :], 0.0).then_inc(s_init, 1)
                pool.memset(nhalf[:, :], -0.5).then_inc(s_init, 1)
                pool.wait_ge(s_c, 32)
                pool.wait_ge(s_init, 9)
                for c in range(NC):
                    pool.tensor_copy(GX[:, c, :], c0[:, C_IND - C_ALL:C_IND - C_ALL + 512]).then_inc(s_init, 1)
                    pool.tensor_copy(HX[:, c, :], c0[:, C_THREE - C_ALL:C_THREE - C_ALL + P]).then_inc(s_init, 1)
                pool.tensor_copy(cau[:, :], c0[:, C_CAU - C_ALL:C_CAU - C_ALL + P]).then_inc(s_init, 1)
                pool.tensor_copy(one3[:, :], c0[:, C_THREE - C_ALL:C_THREE - C_ALL + P]).then_inc(s_init, 1)
                pool.tensor_copy(idb[:, :], ident).then_inc(s_init, 1)

            @block.vector
            def _(dve):
                dve.wait_ge(s_x, 32)
                for t in range(16):
                    dve.bn_stats(bst[:, 6 * t:6 * t + 6], X[t]).then_inc(s_ln, 1)
                for t in range(16):
                    dve.wait_ge(s_ln, t + 1)
                    dve.bn_aggr(mv[:, 2 * t:2 * t + 2], bst[:, 6 * t:6 * t + 6]).then_inc(s_ln, 1)
                dve.wait_ge(s_ln, 32)
                var = mv.rearrange("p (t a) -> p t a", a=2)[:, :, 1]
                tx, th_, ty, tt = (t[:, :] for t in newton)
                dve.tensor_scalar(tx, var, 1e-5, None, ALU.add).then_inc(s_ln, 1)
                rsqrt_steps(dve, s_ln, 33, tx, th_, ty, tt)
                for t in range(16):
                    if t == 0:
                        dve.wait_ge(s_ln, 33 + RSQRT_STEPS)
                    dve.tensor_scalar(X[t], X[t], mv[:, 2 * t:2 * t + 1], ty[:, t:t + 1],
                                      ALU.subtract, ALU.mult).then_inc(s_ln, 1)
                for q in range(8):
                    if q % 2:
                        dve.wait_ge(s_xt, q + 1)
                        dve.tensor_copy(xnT[:, q // 4, (q % 4) * 512:(q % 4 + 1) * 512], banks[q][:, :]).then_inc(s_xte, 1)
                dve.wait_ge(s_z, 1)
                dve.tensor_copy(zs, banks[0][:, :]).then_inc(s_zc, 1)
                dve.wait_ge(s_zc, 1)
                dve.tensor_scalar(na, zs, -1.0, None, ALU.mult).then_inc(s_zc, 1)
                dve.wait_ge(s_zc, 2)
                dve.tensor_tensor(na, na, zs, ALU.min).then_inc(s_abs, 1)
                dve.wait_ge(s_log, 1)
                dve.scalar_tensor_tensor(spl, zs, 0.0, ez, ALU.min, ALU.subtract).then_inc(s_zc, 1)
                dve.wait_ge(s_zc, 3)
                sv = spl.rearrange("p (b c o) -> p b c o", b=NB, c=NC)
                for b in range(NB):
                    for dst, o, f in ((gl, 0, 1.0 / 16.0), (lb, 16, 1.0)):
                        dve.tensor_scalar(dst[:, b * 64:(b + 1) * 64].rearrange("p (g c h) -> p g c h", g=NG, c=NC),
                                          sv[:, b, :, o:o + 16].rearrange("p c (g h) -> p g c h", g=NG),
                                          f, None, ALU.mult).then_inc(s_g, 1)
                dve.wait_ge(s_eg, 2)
                dve.wait_ge(s_g, 8)
                dve.tensor_copy(Gs, banks[1][:, 0:256]).then_inc(s_g, 1)
                dve.tensor_tensor(Hs, lb, banks[1][:, 0:256], ALU.subtract).then_inc(s_g, 1)
                dve.wait_ge(s_g, 10)
                dve.tensor_tensor(Ws, Hs, banks[1][:, 256:512], ALU.add).then_inc(s_w, 1)
                dve.wait_ge(s_bg, 32)
                dve.tensor_scalar(wv[:, :], wv[:, :], 0.5, None, ALU.mult).then_inc(s_w, 1)
                dve.wait_ge(s_rt, 1)
                rp = [rowp[:, :, a, :] for a in range(3)]
                rf = rowf.rearrange("p (q t) -> p q t", q=4)
                rr = rest.rearrange("p (q t) -> p q t", q=4)
                dve.tensor_copy(rp[0], banks[2][:, :].rearrange("p (q t) -> p q t", q=4)).then_inc(s_split, 1)
                dve.wait_ge(s_split, 1)
                dve.tensor_tensor(rf, banks[2][:, :].rearrange("p (q t) -> p q t", q=4), rp[0], ALU.subtract).then_inc(s_split, 1)
                dve.wait_ge(s_split, 2)
                dve.tensor_copy(rp[1], rf).then_inc(s_split, 1)
                dve.wait_ge(s_split, 3)
                dve.tensor_tensor(rr, rf, rp[1], ALU.subtract).then_inc(s_split, 1)
                dve.wait_ge(s_split, 4)
                dve.tensor_copy(rp[2], rr).then_inc(s_split, 1)

            @block.scalar
            def _(act):
                for q in range(0, 8, 2):
                    act.wait_ge(s_xt, q + 1)
                    act.copy(xnT[:, q // 4, (q % 4) * 512:(q % 4 + 1) * 512], banks[q][:, :]).then_inc(s_xte, 1)
                act.wait_ge(s_abs, 1)
                act.activation(ez, na, ACT.Exp).then_inc(s_exp, 1)
                act.wait_ge(s_exp, 1)
                act.activation(ez, ez, ACT.Ln, bias=1.0).then_inc(s_log, 1)
                act.wait_ge(s_cum, 1)
                act.activation(eG[:, :], banks[1][:, 0:256], ACT.Exp).then_inc(s_eg, 1)
                act.activation(eGC[:, :], banks[1][:, 256:512], ACT.Exp).then_inc(s_eg, 1)
                act.wait_ge(s_w, 1)
                act.activation(wK[:, :], Ws, ACT.Exp).then_inc(s_eg, 1)
                act.wait_ge(s_eg, 1)
                act.mul(eG[:, :], eG[:, :], -1.0).then_inc(s_eg, 1)

            @block.tensor
            def _(pe):
                pe.wait_ge(s_c, 32)
                for q in range(8):
                    kk, tq = q // 4, q % 4
                    pe.wait_ge(s_ln, 33 + RSQRT_STEPS + 4 * tq + 4)
                    for j in range(4):
                        mm = pe.transpose(banks[q][:, j * P:(j + 1) * P], X[4 * tq + j][:, kk * P:(kk + 1) * P], ident)
                    mm.then_inc(s_xt, 1)
                pe.wait_ge(s_bg, 32)
                pe.wait_ge(s_xte, 8)
                for t in range(16):
                    for kk in range(KD):
                        mm = pe.matmul(banks[0][:, 32 * t:32 * t + 32], xnT[:, kk, t * P:(t + 1) * P], bgs[:, kk, :],
                                       start=(kk == 0), stop=(kk == KD - 1))
                mm.then_inc(s_z, 1)
                pe.wait_ge(s_g, 8)
                pe.matmul(banks[1][:, 0:256], c0[:, C_TRI - C_ALL:C_TRI - C_ALL + P], gl, start=True, stop=True)
                pe.matmul(banks[1][:, 256:512], cs[:, C_ONES:C_ONES + P], gl, start=True, stop=True).then_inc(s_cum, 1)
                pe.wait_ge(s_g, 10)
                for q, src in enumerate((Gs, Gs, Hs, Hs)):
                    mm = pe.transpose(banks[2][:, q * P:(q + 1) * P], src[:, (q % 2) * P:(q % 2 + 1) * P], ident)
                mm.then_inc(s_rt, 1)

        C = {name: Count(sem(name), per) for name, per in dict(
            proj=NT, raw=6, conv=18, th=6 + HG, silu=6, sq=5, stat=1, sqp=4, nk=1, kn_=1, ks_=3, nq=1,
            tkp=1, kn=1, tvp=1, vn=1, grp=1, gh=1, gtp=1, gr=1, ep=4, e=4, bp=4, qkp=4, pt=4, qrp=3, eq=3, qt=3,
            gate=4, sub=32, x16=4, xm=4, z16=4, t16=4, u32=4, t32=4, x32=4, xe32=4, z32=4, u64=4, x64=4, xe64=4, z64=4, uf=4,
            ks=3, rr=3, y=4, ye=4, o=4, oe=4, su=3, s=3, kh=3, o2=4, sr=4, fx=1, nf=1, clr=3, fs=4, otp=4, ot=4,
            outp=4, acc=4).items()}
        C["outp"].start = C["clr"].start = 1
        for name, per in dict(wkv=1, wq=1, wg=1, cl=1, wol=1, rowl=6, dgw=8, dgr=1, tuw=1, ur=8).items():
            C[name] = Count(sem(name + "_dma"), per, 16)

        def bank(name):
            return banks[RING_AT[name] % BANKS]

        def wait_bank(pe, name, n):
            j, m = RING_AT[name] - BANKS, n
            while True:
                if j < 0:
                    j, m = j + len(RING), m - 1
                    if isinstance(m, int) and m < 0:
                        return
                use = RING[j]
                here = use is not None
                if here and isinstance(m, int):
                    here = 2 <= m < NI + 2 if use[3] else m < NI
                if here:
                    wait(pe, C[use[1]], m - 2 if use[3] else m, use[2])
                    return
                j -= BANKS

        with nc.Block() as block:
            @block.tensor
            def _(pe):
                def project(n, p, t):
                    name = f"P{t}" if t < 6 else f"G{t - 6}"
                    if t in (0, 2, 6):
                        wait(pe, C[{0: "wkv", 2: "wq", 6: "wg"}[t]], n, 1)
                    wait_bank(pe, name, n)
                    for kk in range(KD):
                        mm = pe.matmul(bank(name)[:, :], wt[:, t if t < 6 else t - 4, kk, :], xnT[:, kk, bass.ds((n // NG) * SEQ, SEQ)],
                                       start=(kk == 0), stop=(kk == KD - 1))
                    mm.then_inc(C["proj"].sem, 1)

                def gram(n, p, _):
                    wait(pe, C["silu"], n, 1)
                    wait_bank(pe, "GR0", n)
                    for c in range(NC):
                        kc = KT[p][:, c * P:(c + 1) * P]
                        mm = pe.matmul(bank("GR0")[:, c * P:(c + 1) * P], kc, kc, start=True, stop=True)
                    mm.then_inc(C["grp"].sem, 1)

                def gram_t(n, p, _):
                    wait(pe, C["gh"], n, 1)
                    wait_bank(pe, "GT0", n)
                    for c in range(NC):
                        mm = pe.transpose(bank("GT0")[:, c * P:(c + 1) * P], gsb[:, c * P:(c + 1) * P], ident)
                    mm.then_inc(C["gtp"].sem, 1)

                def rows_of(src, ready, k, name, done):
                    def go(n, p, _):
                        wait(pe, C[ready], n, k)
                        wait_bank(pe, name, n)
                        t = src[p] if isinstance(src, list) else src
                        for c in range(NC):
                            mm = pe.transpose(bank(name)[:, c * P:(c + 1) * P], t[:, c * P:(c + 1) * P], ident)
                        mm.then_inc(C[done].sem, 1)
                    return go

                def stats_k(n, p, _):
                    wait(pe, C["sq"], n, 1)
                    wait_bank(pe, "SK0", n)
                    for c in range(NC):
                        mm = pe.matmul(bank("SK0")[:, c:c + 1], sqr[1][:, c * P:(c + 1) * P], cs[:, C_ONES:C_ONES + 1],
                                       start=True, stop=True)
                    mm.then_inc(C["stat"].sem, 1)

                def stats_q(n, p, c):
                    wait(pe, C["sq"], n, 2 + c)
                    if c == 0:
                        wait_bank(pe, "SQ0", n)
                    for h in range(HG):
                        mm = pe.matmul(bank("SQ0")[:, 4 * c + h:4 * c + h + 1], sqr[c % 2][:, h * P:(h + 1) * P],
                                       cs[:, C_ONES:C_ONES + 1], start=True, stop=True)
                    mm.then_inc(C["sqp"].sem, 1)

                def exponent(n, p, c):
                    wait(pe, C["rowl"], n, 6)
                    wait_bank(pe, f"E{c}", n)
                    b = bank(f"E{c}")
                    pe.matmul(b[:, :], idb[:, :], cau[:, :].unsqueeze(1).to_broadcast([P, HG, P]), start=True, stop=False)
                    pe.matmul(b[:, :], HX[:, c, :], GX[:, c, :], start=False, stop=True).then_inc(C["ep"].sem, 1)

                def row_g(n, p, c):
                    wait_bank(pe, f"QR{c}", n)
                    pe.matmul(bank(f"QR{c}")[:, :], one3[:, :], GX[:, c, :], start=True, stop=True).then_inc(C["qrp"].sem, 1)

                def qk(n, p, c):
                    wait(pe, C["silu"], n, 6)
                    wait_bank(pe, f"QK{c}", n)
                    pe.matmul(bank(f"QK{c}")[:, :], KT[p][:, c * P:(c + 1) * P], QT[p][:, c * SEQ:(c + 1) * SEQ],
                              start=True, stop=True).then_inc(C["qkp"].sem, 1)

                def out_t(n, p, c):
                    wait(pe, C["fs"], n, c + 1)
                    wait_bank(pe, f"OT{c}", n + 2)
                    for h in range(HG):
                        o = c * SEQ + h * P
                        mm = pe.transpose(bank(f"OT{c}")[:, h * P:(h + 1) * P], OB[:, o:o + P], ident)
                    mm.then_inc(C["otp"].sem, 1)

                def out_proj(n, p, c):
                    wait(pe, C["ot"], n, c + 1)
                    wait(pe, C["wol"], n, 1)
                    wait_bank(pe, f"OUT{c}", n + 2)
                    for h in range(HG):
                        mm = pe.matmul(bank(f"OUT{c}")[:, 0:D], OT[c % 2][:, h * P:(h + 1) * P], wot[:, h, :],
                                       start=(h == 0), stop=(h == HG - 1))
                    mm.then_inc(C["outp"].sem, 1)

                def half(t, c, odd, w):
                    a = halves(t, c or 0, odd, w)
                    n = a.shape[1] // HG
                    return [a[:, h * n:(h + 1) * n, :] for h in range(HG)]

                def pair(b, h, o):
                    return b[:, o + 64 * h:o + 64 * h + 64]

                def la(n, p, c):
                    wait(pe, C["t16"], n, c + 1)
                    wait(pe, C["xe64"], n, c)
                    for h in range(HG):
                        mm = pe.matmul(pair(bX, h, 0), heads(BP[p], c)[:, h, :], half(T, c, 0, 16)[h], start=True, stop=True)
                    mm.then_inc(C["x16"].sem, 1)

                def lb_(n, p, c):
                    wait(pe, C["xm"], n, c + 1)
                    wait(pe, C["uf"], n, c)
                    for h in range(HG):
                        mm = pe.matmul(pair(bZ, h, 0), heads(Xf)[:, h, :], half(U[p], c, 1, 16)[h], start=True, stop=True)
                    mm.then_inc(C["z16"].sem, 1)

                def lc(n, p, c):
                    wait(pe, C["t32"], n, c + 1)
                    for h in range(HG):
                        mm = pe.matmul(pair(bX, h, 0), heads(BP[p], c)[:, h, :], half(T, c, 0, 32)[h], start=True, stop=True)
                    mm.then_inc(C["x32"].sem, 1)

                def ld(n, p, c):
                    wait(pe, C["xe32"], n, c + 1)
                    for h in range(HG):
                        mm = pe.matmul(pair(bZ, h, 0), heads(X32)[:, h, :], half(U[p], c, 1, 32)[h], start=True, stop=True)
                    mm.then_inc(C["z32"].sem, 1)

                def le(n, p, c):
                    wait(pe, C["u64"], n, c + 1)
                    for h in range(HG):
                        mm = pe.matmul(bX[64:128, 64 * h:64 * h + 64], heads(BP[p], c)[:, h, 64:128], heads(T, c)[:, h, 0:64],
                                       start=True, stop=True)
                    mm.then_inc(C["x64"].sem, 1)

                def lf(n, p, c):
                    wait(pe, C["xe64"], n, c + 1)
                    for h in range(HG):
                        mm = pe.matmul(bZ[0:64, 64 * h:64 * h + 64], X64[:, 64 * h:64 * h + 64], heads(U[p], c)[:, h, 64:128],
                                       start=True, stop=True)
                    mm.then_inc(C["z64"].sem, 1)

                def ra(n, p, c):
                    wait(pe, C["s"], n, c)
                    wait(pe, C["oe"], n, c)
                    pe.matmul(bO[:, :], KT[p][:, c * P:(c + 1) * P], S[:, :], start=True, stop=True).then_inc(C["ks"].sem, 1)

                def rb(n, p, c):
                    if c:
                        wait(pe, C["rr"], n, c)
                    else:
                        wait(pe, C["vn"], n, 1)
                    wait(pe, C["uf"], n, c + 1)
                    wait(pe, C["ye"], n, c)
                    for h in range(HG):
                        rhs = RY[:, h * P:(h + 1) * P] if c else Vn[p][:, 0:P]
                        mm = pe.matmul(bY[:, h * P:(h + 1) * P], heads(U[p], c)[:, h, :], rhs, start=True, stop=True)
                    mm.then_inc(C["y"].sem, 1)

                def rc(n, p, c):
                    wait(pe, C["ye"], n, c + 1)
                    wait(pe, C["pt"], n, c + 1)
                    if c:
                        wait(pe, C["qt"], n, c)
                    else:
                        wait(pe, C["oe"], n, 0)
                    for h in range(HG):
                        if c:
                            pe.matmul(bO[:, h * P:(h + 1) * P], heads(QT[p], c)[:, h, :], S[:, h * P:(h + 1) * P],
                                      start=True, stop=False)
                        mm = pe.matmul(bO[:, h * P:(h + 1) * P], heads(PT[p], c)[:, h, :], RY[:, h * P:(h + 1) * P],
                                       start=(c == 0), stop=True)
                    mm.then_inc(C["o"].sem, 1)

                def rd(n, p, c):
                    wait(pe, C["kh"], n, c + 1)
                    wait(pe, C["ye"], n, c + 1)
                    if c == 0:
                        wait(pe, C["s"], n, 0)
                    for h in range(HG):
                        mm = pe.matmul(bS[:, h * P:(h + 1) * P], Kh[c % 2][:, h * P:(h + 1) * P], RY[:, h * P:(h + 1) * P],
                                       start=True, stop=True)
                    mm.then_inc(C["su"].sem, 1)

                pe.sem_inc(C["outp"].sem, 1)
                bodies(pe, "pe", dict(
                    P=project, G=lambda n, p, t: project(n, p, t + 6), GR=gram, GT=gram_t,
                    TK=rows_of(KT, "silu", 1, "TK0", "tkp"), TV=rows_of(VT, "silu", 2, "TV0", "tvp"),
                    SK=stats_k, SQ=stats_q, E=exponent, QR=row_g, QK=qk, OT=out_t, OUT=out_proj,
                    La=la, Lb=lb_, Lc=lc, Ld=ld, Le=le, Lf=lf, Ra=ra, Rb=rb, Rc=rc, Rd=rd))

            @block.scalar
            def _(act):
                def conv_start(n, p, t):
                    if t == 0:
                        wait(act, C["cl"], n, 1)
                    wait(act, C["proj"], n, t + 1)
                    wait(act, C["silu"], n, t - 1)
                    act.copy(xr[t % 2][:, :], bank(f"P{t}")[:, :])
                    act.activation(cacc[t % 2][:, :], bank(f"P{t}")[:, :], ACT.Identity,
                                   scale=cwt[:, t, 3:4]).then_inc(C["raw"].sem, 1)

                def silu_tanh(n, p, t):
                    wait(act, C["conv"], n, 3 * t + 3)
                    wait(act, C["silu"], n, t - 1)
                    if t < 2:
                        wait(act, C["gate"], n - 1, HG)
                    act.activation(th[t % 2][:, :], cacc[t % 2][:, :], ACT.Tanh, scale=0.5).then_inc(C["th"].sem, 1)

                def gate_tanh(n, p, h):
                    wait(act, C["proj"], n, 7 + h)
                    if h < 2:
                        wait(act, C["silu"], n, 6)
                    else:
                        wait(act, C["gate"], n, h - 1)
                    act.activation(th[h % 2][:, :], bank(f"G{h}")[:, :], ACT.Tanh, scale=0.5).then_inc(C["th"].sem, 1)

                def gram_scaled(n, p, _):
                    wait(act, C["kn_"], n, 1)
                    wait(act, C["grp"], n, 1)
                    wait(act, C["tvp"], n, 1)
                    for c in range(NC):
                        last = act.activation(gsb[:, c * P:(c + 1) * P], bank("GR0")[:, c * P:(c + 1) * P], ACT.Identity,
                                              scale=rk[p][:, c:c + 1])
                    last.then_inc(C["gh"].sem, 1)

                def k_rows(n, p, _):
                    wait(act, C["tkp"], n, 1)
                    wait(act, C["kh"], n - 2, 3)
                    act.copy(Kn[p][:, :], bank("TK0")[:, :]).then_inc(C["kn"].sem, 1)

                def v_rows(n, p, _):
                    wait(act, C["tvp"], n, 1)
                    wait(act, C["rr"], n - 2, 3)
                    act.mul(Vn[p][:, :], bank("TV0")[:, :], 0.5).then_inc(C["vn"].sem, 1)

                def decay(n, p, c):
                    wait(act, C["ep"], n, c + 1)
                    wait(act, C["o"], n - 2, c + 1)
                    act.activation(PT[p][:, c * SEQ:(c + 1) * SEQ], bank(f"E{c}")[:, :], ACT.Exp).then_inc(C["e"].sem, 1)

                def row_decay(n, p, c):
                    wait(act, C["qrp"], n, c)
                    wait(act, C["bp"], n, 4)
                    wait(act, C["qt"], n, c - 1)
                    act.activation(gr[:, :], bank(f"QR{c}")[:, :], ACT.Exp).then_inc(C["eq"].sem, 1)

                def lc(n, p, c):
                    wait(act, C["x32"], n, c + 1)
                    act.mul(halves(X32, 0, 0, 32), bX[:, 0:256].rearrange("p (g u) -> p g u", u=32), -1.0).then_inc(C["xe32"].sem, 1)

                def le(n, p, c):
                    wait(act, C["x64"], n, c + 1)
                    act.mul(X64[64:128, :], bX[64:128, 0:256], -1.0).then_inc(C["xe64"].sem, 1)

                def lf(n, p, c):
                    wait(act, C["z64"], n, c + 1)
                    act.copy(heads(U[p], c)[0:64, :, 64:128],
                             bZ[0:64, 0:256].rearrange("p (h u) -> p h u", h=HG)).then_inc(C["uf"].sem, 1)

                def rb(n, p, c):
                    wait(act, C["y"], n, c + 1)
                    wait(act, C["o"], n, c)
                    act.copy(RY[:, :], bY[:, :]).then_inc(C["ye"].sem, 1)

                def rc(n, p, c):
                    wait(act, C["o"], n, c + 1)
                    wait(act, C["otp"], n - 1, c + 1)
                    act.copy(OB[:, c * SEQ:(c + 1) * SEQ], bO[:, :]).then_inc(C["oe"].sem, 1)

                def square_k(n, p, _):
                    wait(act, C["silu"], n, 1)
                    wait(act, C["sqp"], n - 1, 4)
                    act.activation(sqr[1][:, :], KT[p][:, :], ACT.Square).then_inc(C["sq"].sem, 1)

                def square_q(n, p, c):
                    wait(act, C["silu"], n, 6)
                    if c < 2:
                        wait(act, C["stat"], n, 1)
                    else:
                        wait(act, C["sqp"], n, c - 1)
                    act.activation(sqr[c % 2][:, :], QT[p][:, c * SEQ:(c + 1) * SEQ], ACT.Square).then_inc(C["sq"].sem, 1)

                def square_o(n, p, c):
                    wait(act, C["oe"], n, c + 1)
                    wait(act, C["sr"], n, c)
                    act.activation(o2[:, :], OB[:, c * SEQ:(c + 1) * SEQ], ACT.Square).then_inc(C["o2"].sem, 1)

                def scale_out(n, p, c):
                    wait(act, C["nf"], n, 1)
                    for h in range(HG):
                        o = OB[:, c * SEQ + h * P:c * SEQ + (h + 1) * P]
                        last = act.activation(o, o, ACT.Identity, scale=fo[:, 4 * c + h:4 * c + h + 1])
                    last.then_inc(C["fs"].sem, 1)

                bodies(act, "act", dict(
                    P=conv_start, H=silu_tanh, G=gate_tanh, GS=gram_scaled, TK=k_rows, TV=v_rows, E=decay,
                    SK=square_k, SQ=square_q, QR=row_decay, Lc=lc, Le=le, Lf=lf, Rb=rb, Rc=rc, Ro=square_o, FS=scale_out))

            @block.vector
            def _(dve):
                def tap(d):
                    def conv(n, p, t):
                        if d == 1:
                            wait(dve, C["raw"], n, t + 1)
                        else:
                            wait(dve, C["conv"], n, 3 * t + d - 1)
                        a, b = cacc[t % 2], xr[t % 2]
                        dve.scalar_tensor_tensor(a[:, d:SEQ], b[:, 0:SEQ - d], cwt[:, t, 3 - d:4 - d], a[:, d:SEQ],
                                                 ALU.mult, ALU.add).then_inc(C["conv"].sem, 1)
                    return conv

                def silu(n, p, t):
                    wait(dve, C["th"], n, t + 1)
                    if t == 0:
                        wait(dve, C["ks"], n - 2, 3)
                        dst = KT[p][:, :]
                    elif t == 1:
                        wait(dve, C["gtp"], n - 1, 1)
                        dst = VT[:, :]
                    else:
                        wait(dve, C["o"], n - 2, 4)
                        dst = QT[p][:, :].rearrange("p (c h t) -> p c h t", c=NC, h=HG)[:, :, t - 2, :]
                    a, b = th[t % 2][:, :], cacc[t % 2][:, :]
                    if t >= 2:
                        a, b = (v.rearrange("p (c t) -> p c t", c=NC) for v in (a, b))
                    dve.scalar_tensor_tensor(dst, a, 1.0, b, ALU.add, ALU.mult).then_inc(C["silu"].sem, 1)

                def gate(n, p, h):
                    wait(dve, C["th"], n, 7 + h)
                    wait(dve, C["ot"], n - 2, 4)
                    dve.scalar_tensor_tensor(SG[p][:, h * SEQ:(h + 1) * SEQ], th[h % 2][:, :], 1.0, bank(f"G{h}")[:, :],
                                             ALU.add, ALU.mult).then_inc(C["gate"].sem, 1)

                def stats_k(n, p, _):
                    wait(dve, C["stat"], n, 1)
                    dve.tensor_scalar(kx[:, :], bank("SK0")[:, 0:NC], 4e-6, None, ALU.add).then_inc(C["nk"].sem, 1)

                def gram_cols(n, p, _):
                    wait(dve, C["gtp"], n, 1)
                    wait(dve, C["kn_"], n, 1)
                    wait(dve, C["qt"], n - 1, 3)
                    for c in range(NC):
                        last = dve.scalar_tensor_tensor(gr[:, c * P:(c + 1) * P], bank("GT0")[:, c * P:(c + 1) * P],
                                                        rk[p][:, c:c + 1], cs[:, C_STR:C_STR + P], ALU.mult, ALU.mult)
                    last.then_inc(C["gr"].sem, 1)

                def stats_q(n, p, _):
                    wait(dve, C["sqp"], n, 4)
                    dve.tensor_scalar(eq2[p][:, :], bank("SQ0")[:, 0:16], OUT_EPS * P, OUT_EPS * P * 4e-6,
                                      ALU.mult, ALU.add).then_inc(C["nq"].sem, 1)

                def weigh(n, p, c):
                    wait(dve, C["qkp"], n, c + 1)
                    wait(dve, C["bp"], n, c + 1)
                    t = PT[p][:, c * SEQ:(c + 1) * SEQ]
                    dve.scalar_tensor_tensor(t, bank(f"QK{c}")[:, :], rk[p][:, c:c + 1], t,
                                             ALU.mult, ALU.mult).then_inc(C["pt"].sem, 1)

                def la(n, p, c):
                    wait(dve, C["x16"], n, c + 1)
                    neg = cs[:, C_NEG:C_NEG + 64].unsqueeze(1).to_broadcast([P, HG, 64])
                    dve.tensor_tensor(halves(Xf, 0, 0, 16).rearrange("p (h m) u -> p h m u", h=HG),
                                      bX[:, 0:256].rearrange("p (h m u) -> p h m u", h=HG, m=4),
                                      neg.rearrange("p h (m u) -> p h m u", m=4), ALU.mult).then_inc(C["xm"].sem, 1)

                def lt(n, p, c):
                    if c == 0:
                        wait(dve, C["ur"], n, 8)
                        wait(dve, C["clr"], n - 2, 3)
                    wait(dve, C["x64"], n - 1, c + 1)
                    dve.transpose(T[:, c * SEQ:(c + 1) * SEQ], U[p][:, c * SEQ:(c + 1) * SEQ]).then_inc(C["t16"].sem, 1)

                def lb_(n, p, c):
                    wait(dve, C["z16"], n, c + 1)
                    dve.tensor_tensor(halves(U[p], c, 1, 16), bZ[:, 0:256].rearrange("p (g u) -> p g u", u=16),
                                      halves(U[p], c, 1, 16), ALU.add).then_inc(C["u32"].sem, 1)
                    wait(dve, C["u32"], n, c + 1)
                    dve.transpose(T[:, c * SEQ:(c + 1) * SEQ], U[p][:, c * SEQ:(c + 1) * SEQ]).then_inc(C["t32"].sem, 1)

                def ld(n, p, c):
                    wait(dve, C["z32"], n, c + 1)
                    u = heads(U[p], c)
                    z = bZ[:, 0:256].rearrange("p (h m u) -> p h m u", h=HG, m=2)
                    dve.tensor_copy(u[0:32, :, 32:64], z[0:32, :, 0, :])
                    dve.transpose(heads(T, c)[32:64, :, 0:32], z[0:32, :, 0, :])
                    dve.tensor_copy(u[64:96, :, 96:128], z[64:96, :, 1, :]).then_inc(C["u64"].sem, 1)

                def ra(n, p, c):
                    wait(dve, C["ks"], n, c)
                    wait(dve, C["o"], n, c)
                    wait(dve, C["vn"], n, 1)
                    wait(dve, C["ks_"], n, 3)
                    for h in range(HG):
                        j = 4 * c + h
                        last = dve.scalar_tensor_tensor(RY[:, h * P:(h + 1) * P], bO[:, h * P:(h + 1) * P], sR[p][:, j:j + 1],
                                                        Vn[p][:, c * P:(c + 1) * P], ALU.mult, ALU.add)
                    last.then_inc(C["rr"].sem, 1)

                def rd(n, p, c):
                    wait(dve, C["su"], n, c + 1)
                    wait(dve, C["o"], n, c + 1)
                    if c == 0:
                        dve.tensor_copy(S[:, :], bS[:, :]).then_inc(C["s"].sem, 1)
                    else:
                        wait(dve, C["s"], n, c)
                        for h in range(HG):
                            j = 4 * c + h
                            s = S[:, h * P:(h + 1) * P]
                            last = dve.scalar_tensor_tensor(s, s, dec[p][:, j:j + 1], bS[:, h * P:(h + 1) * P],
                                                            ALU.mult, ALU.add)
                        last.then_inc(C["s"].sem, 1)

                def rs(n, p, c):
                    wait(dve, C["o2"], n, c + 1)
                    dve.tensor_reduce(so[p][:, 4 * c:4 * c + 4], heads(o2), AX.X, ALU.add).then_inc(C["sr"].sem, 1)

                def out_factor(n, p, _):
                    wait(dve, C["sr"], n, 4)
                    wait(dve, C["nq"], n, 1)
                    wait(dve, C["nf"], n - 1, 1)
                    dve.scalar_tensor_tensor(fx[:, :], so[p][:, :], 1.0 / P, eq2[p][:, :], ALU.mult, ALU.add).then_inc(C["fx"].sem, 1)

                def clear(n, p, _):
                    wait(dve, C["y"], n, 4)
                    u = U[p][:, :].rearrange("p (u t) -> p u t", t=P)
                    for b in range(3):
                        dve.memset(u[32 * b:32 * b + 32, :, 32 * b + 32:P], 0.0).then_inc(C["clr"].sem, 1)

                def gated(n, p, c):
                    wait(dve, C["otp"], n, c + 1)
                    wait(dve, C["outp"], n, max(c - 1, 0))
                    sg = SG[p][:, :].rearrange("p (h t) -> p h t", h=HG)[:, :, c * P:(c + 1) * P]
                    dve.scalar_tensor_tensor(heads(OT[c % 2]), bank(f"OT{c}")[:, :].rearrange("p (h t) -> p h t", h=HG),
                                             wv[:, 0:1], sg, ALU.mult, ALU.mult).then_inc(C["ot"].sem, 1)

                def add_out(n, p, c):
                    wait(dve, C["outp"], n, c + 1)
                    a = acc[:, bass.ds((n // NG) * (NC * D) + c * D, D)]
                    dve.tensor_tensor(a, bank(f"OUT{c}")[:, 0:D], a, ALU.add).then_inc(C["acc"].sem, 1)

                dve.sem_inc(C["clr"].sem, 1)
                bodies(dve, "dve", dict(
                    Ca=tap(1), Cb=tap(2), Cc=tap(3), H=silu, G=gate, SK=stats_k, GT=gram_cols, SQ=stats_q, QK=weigh,
                    Lt=lt, La=la, Lb=lb_, Ld=ld, Ra=ra, Rd=rd, Rs=rs, FN=out_factor, CL=clear, OT=gated, OUT=add_out))

            @block.gpsimd
            def _(pool):
                def build_b(n, p, c):
                    wait(pool, C["e"], n, c + 1)
                    if c == 0:
                        wait(pool, C["gr"], n, 1)
                    g = gr[:, c * P:(c + 1) * P].unsqueeze(1).to_broadcast([P, HG, P])
                    pool.tensor_tensor(heads(BP[p], c), heads(PT[p], c), g, ALU.mult).then_inc(C["bp"].sem, 1)

                def q_decay(n, p, c):
                    wait(pool, C["eq"], n, c)
                    wait(pool, C["qkp"], n, c + 1)
                    wait(pool, C["sq"], n, c + 2)
                    q = QT[p][:, c * SEQ:(c + 1) * SEQ]
                    pool.tensor_tensor(q, q, gr[:, :], ALU.mult).then_inc(C["qt"].sem, 1)

                def invert_blocks(n, p, j):
                    sub = C["sub"]
                    eye = cs[:, C_EYE:C_EYE + 256].rearrange("p (r t) -> p r t", r=16)
                    if j == 0:
                        pool.tensor_copy(blkU[:, :, :], eye).then_inc(sub.sem, 1)
                        wait(pool, C["dgr"], n, 1)
                        wait(pool, C["tuw"], n - 1, 1)
                    for s in range(15 - 5 * j, 10 - 5 * j, -1):
                        w = 16 - s
                        t = blkt[:, 0:s * w].rearrange("p (r t) -> p r t", r=s)
                        col = blkB[:, 0:s, s:s + 1].to_broadcast([P, s, w])
                        row = blkU[:, s:s + 1, s:16].to_broadcast([P, s, w])
                        wait(pool, sub, n, 1 + 2 * (w - 1))
                        pool.tensor_tensor(t, col, row, ALU.mult).then_inc(sub.sem, 1)
                        wait(pool, sub, n, 2 + 2 * (w - 1))
                        u = blkU[:, 0:s, s:16]
                        pool.tensor_tensor(u, u, t, ALU.subtract).then_inc(sub.sem, 1)
                    if j < 2:
                        return
                    wait(pool, sub, n, 31)
                    for half, mcol in ((0, C_EVEN), (1, C_ODD)):
                        last = pool.tensor_tensor(blkO[:, :, 16 * half:16 * half + 16], blkU[:, :, :],
                                                  cs[:, mcol:mcol + 1].unsqueeze(2).to_broadcast([P, 16, 16]), ALU.mult)
                    last.then_inc(sub.sem, 1)

                def norm_k(n, p, _):
                    wait(pool, C["nk"], n, 1)
                    wait(pool, C["rr"], n - 2, 3)
                    wait(pool, C["s"], n - 2, 3)
                    pool.tensor_tensor(rk[p][:, :], kx[:, :], nhalf[:, 0:NC], ALU.pow).then_inc(C["kn_"].sem, 1)
                    r, g = each(rk[p][:, :], HG), bass.ds(n * 16, 16)

                    def by(t):
                        return t.rearrange("p (c h) -> p c h", c=NC)
                    wait(pool, C["kn_"], n, 1)
                    pool.tensor_tensor(by(wk[p][:, :]), by(wK[:, g]), r, ALU.mult).then_inc(C["ks_"].sem, 1)
                    pool.tensor_tensor(by(sR[p][:, :]), by(eG[:, g]), r, ALU.mult).then_inc(C["ks_"].sem, 1)
                    pool.tensor_copy(dec[p][:, :], eGC[:, g]).then_inc(C["ks_"].sem, 1)

                def norm_o(n, p, _):
                    wait(pool, C["fx"], n, 1)
                    wait(pool, C["fs"], n - 1, 4)
                    pool.tensor_tensor(fo[:, :], fx[:, :], nhalf[:, :], ALU.pow).then_inc(C["nf"].sem, 1)

                def k_scaled(n, p, c):
                    wait(pool, C["ks_"], n, 3)
                    wait(pool, C["kn"], n, 1)
                    wait(pool, C["su"], n, c - 1 if c else 0)
                    k = Kn[p][:, c * P:(c + 1) * P].unsqueeze(1).to_broadcast([P, HG, P])
                    pool.tensor_tensor(heads(Kh[c % 2]), k, each(wk[p][:, 4 * c:4 * c + 4]), ALU.mult).then_inc(C["kh"].sem, 1)

                bodies(pool, "pool", dict(E=build_b, QR=q_decay, IV=invert_blocks, SK=norm_k, FN=norm_o, Rk=k_scaled))

            @block.sync
            def _(sp):
                def weights(n, name, lo, hi):
                    wait(sp, C["proj"], n - 1, 2 if lo == 0 else NT)
                    sp.dma_start(wt[:, lo:hi], wa[bass.ds(n % NG, 1), :, lo:hi].rearrange("a p t k o -> (a p) t k o")
                                 ).then_inc(C[name].sem, 16)

                def gate_weights(n):
                    wait(sp, C["proj"], n, 6)
                    sp.dma_start(wt[:, 2:6], wa[bass.ds(n % NG, 1), :, 6:NT].rearrange("a p t k o -> (a p) t k o")
                                 ).then_inc(C["wg"].sem, 16)

                def taps(n):
                    wait(sp, C["conv"], n - 1, 18)
                    sp.dma_start(cwt[:], cw[bass.ds(n % NG, 1)].rearrange("a p t i -> (a p) t i")).then_inc(C["cl"].sem, 16)

                def row_parts(n):
                    wait(sp, C["ep"], n - 1, 4)
                    wait(sp, C["qrp"], n - 1, 3)
                    i = n % NI
                    for a in range(3):
                        g = rows[bass.ds(i * 16, 16), a, :].rearrange("(o r) t -> o r t", o=1)
                        sp.dma_start(GX[a:a + 1].rearrange("p c (h t) -> p (c h) t", h=HG), g).then_inc(C["rowl"].sem, 16)
                        h = rows[bass.ds(256 + i * 16, 16), a, :].rearrange("(c h) t -> h c t", h=HG)
                        sp.dma_start(HX[3 + 4 * a:7 + 4 * a], h).then_inc(C["rowl"].sem, 16)

                def out_weights(n):
                    wait(sp, C["outp"], n - 1, 4)
                    sp.dma_start(wot[:], wo[bass.ds(n % NG, 1)].rearrange("a p h d -> (a p) h d")).then_inc(C["wol"].sem, 16)

                def blocks_out(n, p):
                    wait(sp, C["bp"], n, 4)
                    for b in range(8):
                        src = BP[p][16 * b:16 * b + 16, :].rearrange("p (u t) -> p u t", t=P)[:, :, 16 * b:16 * b + 16]
                        dst = diag.rearrange("(u b) r t -> b r u t", b=8)[b]
                        sp.dma_start(dst, src).then_inc(C["dgw"].sem, 16)
                    wait(sp, C["dgw"], n, 8)
                    wait(sp, C["sub"], n - 1, 32)
                    sp.dma_start(blkB[:], diag).then_inc(C["dgr"].sem, 16)

                def store_inverses(n):
                    wait(sp, C["sub"], n, 32)
                    wait(sp, C["ur"], n - 1, 8)
                    sp.dma_start(tri_d, blkO[:]).then_inc(C["tuw"].sem, 16)
                    wait(sp, C["tuw"], n, 1)

                def place_inverses(n, p):
                    wait(sp, C["y"], n - 2, 4)
                    wait(sp, C["t32"], n - 2, 4)
                    for b in range(8):
                        lo = 32 * (b // 2)
                        dst = U[p][16 * b:16 * b + 16, :].rearrange("p (u t) -> p u t", t=P)[:, :, lo:lo + 32]
                        src = tri_d.rearrange("(u b) r t -> b r u t", b=8)[b]
                        sp.dma_start(dst, src).then_inc(C["ur"].sem, 16)

                def body(k, p):
                    n, q = k + 1, (p + 1) % 2
                    weights(n + 1, "wkv", 0, 2)
                    blocks_out(n, q)
                    gate_weights(n)
                    taps(n + 1)
                    store_inverses(n)
                    place_inverses(n, q)
                    row_parts(n + 1)
                    weights(n + 1, "wq", 2, 6)

                weights(0, "wkv", 0, 2)
                taps(0)
                row_parts(0)
                weights(0, "wq", 2, 6)
                out_weights(0)
                body(-1, 1)
                body(0, 0)
                with sp.Fori(0, (NI - 2) // 2) as i:
                    body(2 * i + 1, 1)
                    out_weights(2 * i + 1)
                    body(2 * i + 2, 0)
                    out_weights(2 * i + 2)
                out_weights(NI - 1)
                for name, m in (("wkv", 1), ("wq", 1), ("cl", 1), ("rowl", 6)):
                    wait(sp, C[name], NI, m)

        FP = FM * P
        raw = [QT[0][:, 0:KD * F], QT[1][:, 0:KD * F], PT[0][:, 0:5 * D], PT[0][0:FR, 5 * D:6 * D]]
        w12 = [t[:, 0:KD * FP // 2].bitcast(BF16).rearrange("p (k f) -> p k f", k=KD) for t in (PT[1], SG[0])]
        lowt = BP[0][:, 0:KD * F]
        q3 = BP[1][:, 0:6 * D].rearrange("p (m d) -> p m d", m=6)
        parts = [t[:, :].bitcast(BF16).rearrange("p (k t) -> p k t", k=KD) for t in (T, U[0], OB)]
        hid = [QT[m // 3][:, (m % 3) * SEQ:(m % 3 + 1) * SEQ] for m in range(6)]
        xin = [Kn[j][:, 0:D] for j in range(2)]
        fin = [Vn[j][:, 0:D] for j in range(2)]
        tg = [Kh[j][:, 0:D] for j in range(2)]
        ug = [OT[j][:, 0:D] for j in range(2)]
        sums, thr, nthr = newton[0][:, 0:4], newton[1][:, 0:4], newton[2][:, 0:4]
        with nc.Block() as block:
            f_w, f_sum, f_tot, f_q, f_lo = (sem(x) for x in ("ffn_w_loaded", "abs_sums", "abs_totals", "ternary_steps", "split_low"))
            f_up, f_th, f_hid, f_dn, f_tg = (sem(x) for x in ("up_ready", "up_tanh", "hidden_ready", "down_ready", "down_tanh"))
            f_ug, f_xin, f_fin, f_st = (sem(x) for x in ("gated_steps", "x_reloaded", "final_ready", "stored"))

            @block.sync
            def _(sp):
                sp.sem_inc(f_st, 16)
                sp.dma_start(raw[0].rearrange("p (k f) -> p k f", k=KD), w1t.rearrange("(k p) f -> p k f", k=KD)).then_inc(f_w, 16)
                sp.dma_start(raw[1].rearrange("p (k f) -> p k f", k=KD), w2t.rearrange("(k p) f -> p k f", k=KD)).then_inc(f_w, 16)
                sp.dma_start(raw[2].rearrange("p (m d) -> p m d", m=5), w3t[0:5 * P].rearrange("(m p) d -> p m d", m=5)).then_inc(f_w, 16)
                sp.dma_start(raw[3], w3t[5 * P:F]).then_inc(f_w, 16)
                with sp.Fori(0, NB) as b:
                    for c in range(NC):
                        t = b * NC + c
                        sp.wait_ge(f_fin, t + 1 if c == 0 else t)
                        sp.dma_start(xin[c % 2], x[bass.ds(t * P, P), :]).then_inc(f_xin, 16)
                        sp.wait_ge(f_fin, t + 2)
                        sp.dma_start(out[bass.ds(t * P, P), :], fin[c % 2]).then_inc(f_st, 16)
                sp.wait_ge(f_st, 16 * NB * NC + 16)

            @block.vector
            def _(dve):
                for x1 in (f_hid, f_ug, f_fin):
                    dve.sem_inc(x1, 1)
                dve.wait_ge(f_w, 64)
                dve.memset(sums, 0.0).then_inc(f_sum, 1)
                dve.wait_ge(f_sum, 1)
                for j in range(4):
                    r = FR if j == 3 else P
                    dve.tensor_reduce(sums[0:r, j:j + 1], raw[j], AX.X, ALU.add, apply_absolute_value=True).then_inc(f_sum, 1)
                dve.wait_ge(f_tot, 1)
                half_mean = 0.5 / (F * D)
                dve.tensor_scalar(thr[:, 0:3], banks[0][:, 0:3], half_mean, 0.5e-8, ALU.mult, ALU.add).then_inc(f_q, 1)
                dve.tensor_scalar(nthr[:, 0:3], banks[0][:, 0:3], -half_mean, -0.5e-8, ALU.mult, ALU.add).then_inc(f_q, 1)
                dve.wait_ge(f_q, 2)
                for j, (dst, rows_, src) in enumerate((
                        (w12[0][:, :, 0:F], P, raw[0]), (w12[1][:, :, 0:F], P, raw[1]), (q3[:, 0:5], P, raw[2]), (q3[0:FR, 5], FR, raw[3]))):
                    col = min(j, 2)
                    low = lowt[0:rows_, 0:src.shape[1]]
                    if j:
                        dve.wait_ge(f_q, 2 + 2 * j)
                    dve.tensor_scalar(low, src, nthr[0:rows_, col:col + 1], None, ALU.is_lt).then_inc(f_q, 1)
                    dve.wait_ge(f_q, 3 + 2 * j)
                    if j < 2:
                        dst, src, low = (dst, *(v.rearrange("p (k f) -> p k f", k=KD) for v in (src, low)))
                    elif j == 2:
                        src, low = (v.rearrange("p (m d) -> p m d", m=5) for v in (src, low))
                    dve.scalar_tensor_tensor(dst, src, thr[0:rows_, col:col + 1], low, ALU.is_gt, ALU.subtract).then_inc(f_q, 1)

                for z in (w12[0][:, :, F:FP], w12[1][:, :, F:FP], q3[FR:P, 5]):
                    dve.memset(z, 0.0).then_inc(f_q, 1)

                def split(b):
                    at = bass.ds(b * SEQ, SEQ)
                    r = xnT[:, :, at]
                    for j in range(3):
                        if j:
                            dve.wait_ge(f_lo, b * 5 + 2 * j)
                        dve.tensor_copy(parts[j][:, :, at], r).then_inc(f_lo, 1)
                        if j < 2:
                            dve.wait_ge(f_lo, b * 5 + 2 * j + 1)
                            dve.tensor_tensor(r, r, parts[j][:, :, at], ALU.subtract).then_inc(f_lo, 1)

                for b in range(NB):
                    split(b)
                with dve.Fori(0, NB) as b:
                    for m in range(FM):
                        dve.wait_ge(f_th, b * FM + m + 1)
                        dve.wait_ge(f_dn, b * NC + 1)
                        dve.scalar_tensor_tensor(hid[m], th[m % 2][:, :], 1.0, banks[2 + m % 2][:, :],
                                                 ALU.add, ALU.mult).then_inc(f_hid, 1)
                    for c in range(NC):
                        t = b * NC + c
                        dve.wait_ge(f_tg, t + 1)
                        dve.scalar_tensor_tensor(ug[c % 2], tg[c % 2], 1.0, banks[4 + c % 2][:, 0:D], ALU.add, ALU.mult).then_inc(f_ug, 1)
                        dve.wait_ge(f_ug, 2 * t + 2)
                        dve.scalar_tensor_tensor(ug[c % 2], ug[c % 2], 0.25, acc[:, bass.ds(t * D, D)], ALU.mult, ALU.mult).then_inc(f_ug, 1)
                        dve.wait_ge(f_ug, 2 * t + 3)
                        dve.wait_ge(f_xin, 16 * t + 16)
                        dve.wait_ge(f_st, 16 * t + 16 if c == 0 else 16 * t)
                        dve.tensor_tensor(fin[c % 2], ug[c % 2], xin[c % 2], ALU.add).then_inc(f_fin, 1)

            @block.scalar
            def _(act):
                with act.Fori(0, NB) as b:
                    for m in range(FM):
                        act.wait_ge(f_up, b * FM + m + 1)
                        act.wait_ge(f_hid, b * FM + (m or 1))
                        act.activation(th[m % 2][:, :], banks[m % 2][:, :], ACT.Tanh, scale=0.5).then_inc(f_th, 1)
                    for c in range(NC):
                        t = b * NC + c
                        act.wait_ge(f_dn, t + 2)
                        act.wait_ge(f_ug, 2 * t - 1 if c > 0 else 2 * t + 1)
                        act.activation(tg[c % 2], banks[4 + c % 2][:, 0:D], ACT.Tanh, scale=0.25).then_inc(f_tg, 1)

            @block.tensor
            def _(pe):
                pe.sem_inc(f_dn, 1)
                pe.wait_ge(f_sum, 5)
                pe.matmul(banks[0][:, 0:2], cs[:, C_ONES:C_ONES + P], sums[:, 0:2], start=True, stop=True)
                pe.matmul(banks[0][:, 2:3], cs[:, C_ONES:C_ONES + P], sums[:, 2:3], start=True, stop=False)
                pe.matmul(banks[0][:, 2:3], cs[:, C_ONES:C_ONES + P], sums[:, 3:4], start=False, stop=True).then_inc(f_tot, 1)
                pe.wait_ge(f_q, 13)
                pe.wait_ge(f_lo, 5 * NB)
                with pe.Fori(0, NB) as b:
                    at = bass.ds(b * SEQ, SEQ)
                    for m in range(FM):
                        pe.wait_ge(f_hid, b * FM + (m or 1))
                        for w in range(2):
                            o = banks[2 * w + m % 2][:, :]
                            for kk in range(KD):
                                for a in range(3):
                                    mm = pe.matmul(o, w12[w][:, kk, m * P:(m + 1) * P], parts[a][:, kk, at],
                                                   start=(kk == 0 and a == 0), stop=(kk == KD - 1 and a == 2))
                        mm.then_inc(f_up, 1)
                    for c in range(NC):
                        t = b * NC + c
                        if c == 0:
                            pe.wait_ge(f_hid, b * FM + FM + 1)
                            pe.wait_ge(f_ug, 2 * t + 1)
                        else:
                            pe.wait_ge(f_ug, 2 * t - 1)
                        for m in range(FM):
                            mm = pe.matmul(banks[4 + c % 2][:, 0:D], hid[m][:, c * P:(c + 1) * P], q3[:, m, :],
                                           start=(m == 0), stop=(m == FM - 1))
                        mm.then_inc(f_dn, 1)


def constants():
    import numpy as np
    p, t = np.arange(P)[:, None], np.arange(P)[None, :]
    c = np.zeros((P, C_END), np.float32)
    c[:, C_ID:C_ID + P] = p == t
    c[:, C_TRI:C_TRI + P] = p <= t
    c[:, C_STR:C_STR + P] = p < t
    c[:, C_CAU:C_CAU + P] = np.where(p <= t, 0.0, -1e30)
    head = np.arange(HG * P)[None, :] // P
    c[:, C_IND:C_IND + HG * P] = (p >= 3) & (p < 15) & ((p - 3) % HG == head)
    c[:, C_THREE:C_THREE + P] = p < 3
    j = np.arange(64)[None, :]
    c[:, C_NEG:C_NEG + 64] = np.where((p // 32 == j // 16) & (p % 32 >= 16), -1.0, 0.0)
    c[:, C_EVEN] = np.arange(P) % 2 == 0
    c[:, C_ODD] = np.arange(P) % 2 == 1
    c[:, C_ONES:C_ONES + P] = 1.0
    c[:, C_EYE:C_EYE + 256] = np.eye(16, dtype=np.float32).reshape(1, 256)
    return c


def kernel(**inputs):
    import numpy as np
    import concourse.bacc as bacc
    from concourse import mybir as mb
    from concourse.bass_utils import run_bass_kernel_spmd

    a = {k.replace("L0_", ""): np.ascontiguousarray(v) for k, v in inputs.items()}
    qkv = a["attn_qkv_w"].reshape(6 * HG, P, D)
    tap = a["attn_conv_w"].reshape(6 * HG, P, 4)
    gw = a["attn_g_w"].reshape(4 * HG, P, D)
    order = [[16 + g, 20 + g] + [4 * g + h for h in range(HG)] for g in range(NG)]
    tiles = np.stack([np.concatenate([qkv[order[g]], gw[4 * g:4 * g + 4]]) for g in range(NG)])
    arrays = {
        "x": a["attn_hidden_states"].reshape(NI * P, D),
        "wa": tiles.reshape(NG, NT, P, KD, P).transpose(0, 4, 1, 3, 2),
        "cw": np.stack([tap[order[g]] for g in range(NG)]).transpose(0, 2, 1, 3),
        "bgk": np.concatenate([a["attn_gk_w"], a["attn_b_w"]]).reshape(32, KD, P).transpose(2, 1, 0),
        "wo": a["attn_o_w"].reshape(D, NG, HG, P).transpose(1, 3, 2, 0),
        "onw": a["attn_out_norm_w"].reshape(P, 1),
        "w1t": a["ffn_w1"].T, "w2t": a["ffn_w2"].T, "w3t": a["ffn_w3"].T,
        "cst": constants(),
    }
    arrays = {f"in_{k}": np.ascontiguousarray(v) for k, v in arrays.items()}
    nc = bacc.Bacc("TRN2", target_bir_lowering=False, num_devices=1)
    args = {k[3:]: nc.dram_tensor(k, v.shape, mb.dt.from_np(v.dtype), kind="ExternalInput").ap() for k, v in arrays.items()}
    args["rows"] = nc.dram_tensor("rows", (4 * P, 3, P), BF16, kind="Internal").ap()
    args["diag"] = nc.dram_tensor("diag", (P, 16, 16), F32, kind="Internal").ap()
    args["tri_d"] = nc.dram_tensor("tri_d", (P, 16, 32), F32, kind="Internal").ap()
    out = nc.dram_tensor("out", (NI * P, D), F32, kind="ExternalOutput").ap()
    attention_kernel(nc, out=out, **args)
    r = run_bass_kernel_spmd(nc, [arrays], core_ids=[0])
    return r.results[0]["out"].reshape(NB, SEQ, D)
```

```python
from contextlib import ExitStack

import concourse.bass as bass
from concourse import mybir

F32 = mybir.dt.float32
BF16 = mybir.dt.bfloat16
I32 = mybir.dt.int32
ALU = mybir.AluOpType
ACT = mybir.ActivationFunctionType
AX = mybir.AxisListType

P = 128
NB = 4
HG = 4
NC = 4
SEQ = NC * P
NG = 4
NI = NB * NG
D = 256
KD = D // P
F = 704
FM = 6
FR = F - (FM - 1) * P
NT = 2 * HG + 2
RSQRT_SEED = float(0x5F3759DF)
OUT_EPS = 1e-5
NEWTON = 3

C_ID, C_STR, C_ONES, C_EYE, C_NEG, C_EVEN, C_ODD = 0, 128, 256, 384, 640, 704, 705
C_ALL = 706
C_CAU, C_IND, C_THREE, C_TRI = C_ALL, C_ALL + P, C_ALL + P + HG * P, C_ALL + (2 + HG) * P
C_END = C_TRI + P


class Count:

    def __init__(self, sem, per, step=1, start=0):
        self.sem, self.per, self.step, self.start = sem, per, step, start

    def after(self, n, k):
        return (n * self.per + k) * self.step + self.start


def wait(eng, count, n, k):
    v = count.after(n, k)
    if not isinstance(v, int) or v > count.start:
        eng.wait_ge(count.sem, v)


ORDER = dict(
    pe="""
        P0 Ra3 La0 P1 Lb0 Rb3 P2 Lc0 Rc3 Ld0 SK Le0 TV GR Lf0 E0 La1 Rb0 TK Lb1 E1 E2 Rc0 P3 Lc1 GT E3 Rd0
        Ld1 P4 OT0 Le1 P5 La2 Lf1 Ra1 OT1 Lb2 OUT0 OUT1 Rb1 Lc2 OT2 OT3 Rc1 Ld2 Rd1 OUT2 OUT3 G0 Le2 G1 La3
        Lf2 Ra2 SQ0 SQ1 Lb3 Rb2 SQ2 SQ3 QR1 Lc3 QK0 QK1 Ld3 QK2 Rc2 QK3 QR2 G2 Le3 QR3 Rd2 G3 Lf3""".split(),
    act="""
        P0 P1 Rb3 H0 Lc0 H1 SK Rc3 P2 Ro3 Le0 TV Lf0 E0 GS Rb0 TK E1 E2 H2 P3 Lc1 FS0 FS1 E3 P4 Le1 Rc0 H3
        Ro0 Lf1 FS2 P5 FS3 Rb1 Lc2 H4 H5 Rc1 Le2 Ro1 SQ0 SQ1 G0 G1 Lf2 SQ2 SQ3 Lc3 Rb2 QR1 Rc2 Ro2 QR2 QR3
        Le3 G2 G3 Lf3""".split(),
    dve="""
        Lt0 Lt1 Ra3 La0 Ca0 Cb0 Cc0 Lb0 Ca1 Cb1 Cc1 H0 H1 Ld0 Lt2 Lt3 SK Ca2 Cb2 Cc2 La1 Rs3 FN Lb1 GT Rd0
        Ld1 H2 Ca3 Cb3 Cc3 OT0 La2 H3 OT1 Ra1 Rs0 Lb2 OUT0 OUT1 Ca4 OT2 Cb4 Cc4 OT3 Ca5 Cb5 Cc5 Ld2 H4 OUT2
        Rd1 H5 Rs1 OUT3 La3 G0 Ra2 Lb3 G1 SQ3 CL QK0 QK1 Ld3 QK2 QK3 Rd2 Rs2 G2 G3""".split(),
    pool="""
        SK Rk0 Rk1 FN E0 E1 E2 E3 Rk2 IV0 IV1 IV2 QR1 QR2 QR3""".split())
BACK = ("FN", "CL", "FS", "OT", "OUT")

FREED = {"P": ("raw", 6), "SK0": ("nk", 1), "GR0": ("gh", 1), "TV0": ("vn", 1), "TK0": ("kn", 1), "GT0": ("gr", 1),
         "E": ("e", 4), "OT": ("ot", 4), "OUT": ("acc", 4), "SQ0": ("nq", 1), "QK": ("pt", 4), "QR": ("eq", 3),
         "G": ("gate", 4)}
BANKS = 3


def parts_of(stage):
    name = stage.rstrip("0123456789")
    j = int(stage[len(name):] or 0)
    if name[0] in "LR":
        return name, j, -1 if name[0] == "R" and j == NC - 1 else 0
    return name, j, -1 if name in BACK else 1


def ring():
    uses = []
    for stage in ORDER["pe"]:
        name, j, shift = parts_of(stage)
        if name in FREED:
            uses.append((stage, FREED[name][0], j if name == "QR" else j + 1, shift < 0))
        elif f"{name}{j}" in FREED:
            uses.append((f"{name}{j}", FREED[f"{name}{j}"][0], 1, False))
    return uses + [None] * (-len(uses) % BANKS)


RING = ring()
RING_AT = {u[0]: j for j, u in enumerate(RING) if u}
assert not any(u[3] for u in RING[-BANKS:] if u)


def bodies(eng, name_, stages, before={}, after={}, last={}):
    def body(k, parity):
        for stage in ORDER[name_]:
            name, j, shift = parts_of(stage)
            n = k + shift
            if isinstance(n, int) and n == 0 and shift == 1 and stage in before:
                before[stage]()
            if isinstance(n, int) and n == NI - 1 and shift == -1 and stage in last:
                last[stage]()
            if not (isinstance(n, int) and not 0 <= n < NI):
                stages[name](n, (parity + shift) % 2, j)
            elif n == NI and stage in after:
                after[stage]()

    body(-1, 1)
    body(0, 0)
    with eng.Fori(0, (NI - 2) // 2) as i:
        body(2 * i + 1, 1)
        body(2 * i + 2, 0)
    body(NI - 1, 1)
    body(NI, 0)


RSQRT_STEPS = 3 + 3 * NEWTON


def rsqrt_steps(dve, sem, done, x, h, y, t):
    dve.wait_ge(sem, done)
    dve.tensor_scalar(h, x, -0.5, None, ALU.mult).then_inc(sem, 1)
    dve.tensor_scalar(y.bitcast(I32), x.bitcast(I32), 1, None, ALU.arith_shift_right).then_inc(sem, 1)
    dve.wait_ge(sem, done + 2)
    dve.tensor_scalar(y.bitcast(I32), y.bitcast(I32), -1.0, RSQRT_SEED, ALU.mult, ALU.add).then_inc(sem, 1)
    for i in range(NEWTON):
        dve.wait_ge(sem, done + 3 + 3 * i)
        dve.tensor_tensor(t, y, y, ALU.mult).then_inc(sem, 1)
        dve.wait_ge(sem, done + 4 + 3 * i)
        dve.tensor_tensor(t, t, h, ALU.mult).then_inc(sem, 1)
        dve.wait_ge(sem, done + 5 + 3 * i)
        dve.scalar_tensor_tensor(y, t, 1.5, y, ALU.add, ALU.mult).then_inc(sem, 1)


def attention_kernel(nc, x, wa, cw, bgk, wo, onw, w1t, w2t, w3t, cst, rows, diag, tri_d, out):
    ctx = ExitStack()
    with ctx:
        def sb(name, shape, dt=F32):
            return ctx.enter_context(nc.sbuf_tensor(name, shape, dt))

        def two(name, cols, dt=F32):
            return [sb(f"{name}{j}", [P, cols], dt) for j in range(2)]

        xnT = sb("xnT", [P, KD, NB * SEQ])
        acc = sb("acc", [P, NB * NC * D])
        cs = sb("cs", [P, C_ALL])
        cau = sb("cau", [P, P], BF16)
        idb = sb("idb", [P, P], BF16)
        one3 = sb("one3", [P, P], BF16)
        HX = sb("HX", [P, NC, P], BF16)
        GX = sb("GX", [P, NC, HG * P], BF16)
        eG, eGC, wK = sb("eG", [P, NI * 16]), sb("eGC", [P, NI * 16]), sb("wK", [P, NI * 16])
        wv = sb("wv", [P, 1])
        KT, Kn, Vn = two("KT", SEQ), two("Kn", SEQ), two("Vn", SEQ)
        QT, SG, BP, PT = two("QT", 4 * SEQ), two("SG", 4 * SEQ), two("BP", 4 * SEQ), two("PT", 4 * SEQ)
        rk, eq2, so = two("rk", NC), two("eq2", 16), two("so", 16)
        wk, sR, dec = two("wk", 16), two("sR", 16), two("dec", 16)
        T, U = sb("T", [P, 4 * SEQ]), two("U", 4 * SEQ)
        OB = sb("OB", [P, 4 * SEQ])
        wt = sb("wt", [P, 6, KD, P])
        wot = sb("wot", [P, HG, D])
        cwt = sb("cwt", [P, 6, 4])
        taps4 = sb("taps4", [P, 4 * SEQ])
        xr, cacc = ([taps4[:, (2 * a + j) * SEQ:(2 * a + j + 1) * SEQ] for j in range(2)] for a in range(2))
        th = two("th", SEQ)
        sqr = two("sqr", SEQ)
        VT = sb("VT", [P, SEQ])
        gr = sb("gr", [P, SEQ])
        Xf, X32, X64 = sb("Xf", [P, SEQ]), sb("X32", [P, SEQ]), sb("X64", [P, HG * 64])
        RY = sb("RY", [P, SEQ])
        S, o2 = sb("S", [P, SEQ]), sb("o2", [P, SEQ])
        Kh, OT = two("Kh", SEQ), two("OT", SEQ)
        blkB, blkU, blkt = sb("blkB", [P, 16, 16]), sb("blkU", [P, 16, 16]), sb("blkt", [P, 64])
        blkO = sb("blkO", [P, 16, 32])
        newton = [sqr[0][:, 16 * j:16 * j + 16] for j in range(4)]
        kx, fx, fo = sb("kx", [P, NC]), sb("fx", [P, 16]), sb("fo", [P, 16])
        nhalf = sb("nhalf", [P, 16])

        banks = [ctx.enter_context(nc.psum_tensor(f"bank{j}", [P, 512], F32)) for j in range(8)]
        bX, bZ, bO, bY, bS = banks[3:8]

        def sem(name):
            return ctx.enter_context(nc.semaphore(name))

        def heads(t, c=None):
            a = t[:, :] if c is None else t[:, c * SEQ:(c + 1) * SEQ]
            return a.rearrange("p (h t) -> p h t", h=HG)

        def halves(t, c, odd, w):
            a = t[:, c * SEQ:(c + 1) * SEQ] if not isinstance(t, bass.AP) else t
            return a.rearrange("p (g a u) -> p g a u", a=2, u=w)[:, :, odd, :]

        def each(v, n=P):
            return v.unsqueeze(2).to_broadcast([P, v.shape[1], n])

        ident = cs[:, C_ID:C_ID + P]

        X = [QT[t // 8][:, (t % 8) * D:(t % 8 + 1) * D] for t in range(16)]
        bst, mv = SG[0][:, 0:96], SG[0][:, 128:160]
        zs, na, ez, spl = SG[0][:, 256:768], SG[0][:, 768:1280], SG[0][:, 1280:1792], SG[1][:, 0:512]
        gl, ln_beta, Gs, Hs, Ws = (SG[1][:, 512 + 256 * j:768 + 256 * j] for j in range(5))
        rowf = BP[0][:, 0:512]
        rest = BP[0][:, 512:1024]
        rowp = BP[1][:, 0:768].bitcast(BF16).rearrange("p (q a t) -> p q a t", q=4, a=3)
        c0 = PT[0][:, 0:C_END - C_ALL]
        bgs = BP[1][:, 1024:1088].rearrange("p (k o) -> p k o", k=KD)
        with nc.Block() as block:
            s_x, s_c, s_bg, s_rows = [sem(f"x_loaded{j}") for j in range(4)], sem("constants_loaded"), sem("bgk_loaded"), sem("rows_stored")
            s_init, s_ln, s_xt, s_xte = sem("constants_cast"), sem("layernorm_steps"), sem("x_transposed"), sem("xT_copied")
            s_z, s_zc, s_abs, s_exp, s_log = sem("z_ready"), sem("z_steps"), sem("abs_ready"), sem("exp_ready"), sem("log_ready")
            s_cum, s_g, s_w, s_rt, s_split = sem("cumsum_ready"), sem("G_steps"), sem("weights_ready"), sem("rows_transposed"), sem("split_steps")
            s_eg = sem("decays_ready")

            @block.sync
            def _(sp):
                xv = x.rearrange("(n t p) d -> n p t d", p=P, n=4)
                for j in range(4):
                    half = QT[j // 2][:, (j % 2) * 4 * D:(j % 2 + 1) * 4 * D]
                    sp.dma_start(half.rearrange("p (t d) -> p t d", d=D), xv[j]).then_inc(s_x[j], 16)
                sp.dma_start(cs[:, :], cst[:, 0:C_ALL]).then_inc(s_c, 16)
                sp.dma_start(c0, cst[:, C_ALL:C_END]).then_inc(s_c, 16)
                sp.dma_start(bgs, bgk).then_inc(s_bg, 16)
                sp.dma_start(wv[:, :], onw).then_inc(s_bg, 16)
                sp.wait_ge(s_bg, 32)

            @block.gpsimd
            def _(pool):
                for t in (Xf, X32, X64, HX, GX):
                    pool.memset(t[:], 0.0).then_inc(s_init, 1)
                pool.memset(acc[:, :], 0.0).then_inc(s_init, 1)
                for t in U:
                    pool.memset(t[:, :], 0.0).then_inc(s_init, 1)
                pool.memset(nhalf[:, :], -0.5).then_inc(s_init, 1)
                pool.wait_ge(s_c, 32)
                pool.wait_ge(s_init, 9)
                for c in range(NC):
                    pool.tensor_copy(GX[:, c, :], c0[:, C_IND - C_ALL:C_IND - C_ALL + 512]).then_inc(s_init, 1)
                    pool.tensor_copy(HX[:, c, :], c0[:, C_THREE - C_ALL:C_THREE - C_ALL + P]).then_inc(s_init, 1)
                pool.tensor_copy(cau[:, :], c0[:, C_CAU - C_ALL:C_CAU - C_ALL + P]).then_inc(s_init, 1)
                pool.tensor_copy(one3[:, :], c0[:, C_THREE - C_ALL:C_THREE - C_ALL + P]).then_inc(s_init, 1)
                pool.tensor_copy(idb[:, :], ident).then_inc(s_init, 1)

            @block.vector
            def _(dve):
                for t in range(16):
                    if t % 4 == 0:
                        dve.wait_ge(s_x[t // 4], 16)
                    dve.bn_stats(bst[:, 6 * t:6 * t + 6], X[t]).then_inc(s_ln, 1)
                for t in range(16):
                    dve.wait_ge(s_ln, t + 1)
                    dve.bn_aggr(mv[:, 2 * t:2 * t + 2], bst[:, 6 * t:6 * t + 6]).then_inc(s_ln, 1)
                dve.wait_ge(s_ln, 32)
                var = mv.rearrange("p (t a) -> p t a", a=2)[:, :, 1]
                tx, th_, ty, tt = (t[:, :] for t in newton)
                dve.tensor_scalar(tx, var, 1e-5, None, ALU.add).then_inc(s_ln, 1)
                rsqrt_steps(dve, s_ln, 33, tx, th_, ty, tt)
                for t in range(16):
                    if t == 0:
                        dve.wait_ge(s_ln, 33 + RSQRT_STEPS)
                    dve.tensor_scalar(X[t], X[t], mv[:, 2 * t:2 * t + 1], ty[:, t:t + 1],
                                      ALU.subtract, ALU.mult).then_inc(s_ln, 1)
                for q in range(8):
                    if q % 2:
                        dve.wait_ge(s_xt, q + 1)
                        dve.tensor_copy(xnT[:, q // 4, (q % 4) * 512:(q % 4 + 1) * 512], banks[q][:, :]).then_inc(s_xte, 1)

            @block.scalar
            def _(act):
                for q in range(0, 8, 2):
                    act.wait_ge(s_xt, q + 1)
                    act.copy(xnT[:, q // 4, (q % 4) * 512:(q % 4 + 1) * 512], banks[q][:, :]).then_inc(s_xte, 1)

            @block.tensor
            def _(pe):
                pe.wait_ge(s_c, 32)
                for q in range(8):
                    kk, tq = q // 4, q % 4
                    pe.wait_ge(s_ln, 33 + RSQRT_STEPS + 4 * tq + 4)
                    for j in range(4):
                        mm = pe.transpose(banks[q][:, j * P:(j + 1) * P], X[4 * tq + j][:, kk * P:(kk + 1) * P], ident)
                    mm.then_inc(s_xt, 1)

        FP = FM * P
        raw = [U[0][:, 0:KD * F], wt[:].rearrange("p t k o -> p (t k o)")[:, 0:KD * F]]
        w3 = [t[:, j * D:(j + 1) * D] for t in (KT[0], Kn[0], Vn[0]) for j in range(2)]
        w12 = [SG[0][:, j * KD * FP // 2:(j + 1) * KD * FP // 2].bitcast(BF16).rearrange("p (k f) -> p k f", k=KD) for j in range(2)]
        parts = [t[:, :].bitcast(BF16).rearrange("p (k t) -> p k t", k=KD) for t in (QT[0], BP[0], PT[0])]
        sums, thr, nthr = sqr[0][:, 0:6], sqr[0][:, 16:19], sqr[0][:, 32:35]
        hid = [t[:, j * SEQ:(j + 1) * SEQ] for t in (QT[1], PT[1]) for j in range(3)]
        f_w, f_sum, f_q, f_lo = (sem(x) for x in ("ffn_w_loaded", "abs_sums", "ternary_steps", "split_low"))
        f_up, f_th, f_hid, f_dn = (sem(x) for x in ("up_ready", "up_tanh", "hidden_ready", "down_ready"))

        def up(pe, b, m):
            if m == 0:
                pe.wait_ge(f_lo, 10 * b + 10)
            pe.wait_ge(f_hid, b * FM + (m or 1))
            for w in range(2):
                for kk in range(KD):
                    for a in range(3):
                        mm = pe.matmul(banks[3 + 3 * w + m % 2][:, :], w12[w][:, kk, m * P:(m + 1) * P],
                                       parts[a][:, kk, bass.ds(b * SEQ, SEQ)],
                                       start=(kk == 0 and a == 0), stop=(kk == KD - 1 and a == 2))
            mm.then_inc(f_up, 1)

        def up_tanh(act, b, m):
            act.wait_ge(f_up, b * FM + m + 1)
            act.wait_ge(f_hid, b * FM + (m or 1))
            act.activation(th[m % 2][:, :], banks[3 + m % 2][:, :], ACT.Tanh, scale=0.5).then_inc(f_th, 1)

        def hidden(dve, b, m):
            dve.wait_ge(f_th, b * FM + m + 1)
            dve.wait_ge(f_dn, b * NC + 1)
            dve.scalar_tensor_tensor(hid[m], th[m % 2][:, :], 1.0, banks[6 + m % 2][:, :],
                                     ALU.add, ALU.mult).then_inc(f_hid, 1)

        C = {name: Count(sem(name), per) for name, per in dict(
            proj=NT, raw=6, conv=18, th=6 + HG, silu=6, sq=5, stat=1, sqp=4, nk=1, kn_=1, ks_=3, nq=1,
            tkp=1, kn=1, tvp=1, vn=1, grp=1, gh=1, gtp=1, gr=1, ep=4, e=4, bp=4, qkp=4, pt=4, qrp=3, eq=3, qt=3,
            gate=4, sub=32, x16=4, xm=4, z16=4, t16=4, u32=4, t32=4, x32=4, xe32=4, z32=4, u64=4, x64=4, xe64=4, z64=4, uf=4,
            ks=3, rr=3, y=4, ye=4, o=4, oe=4, su=3, s=3, kh=3, o2=4, sr=4, fx=1, nf=1, clr=3, fs=4, otp=4, ot=4,
            outp=4, acc=4).items()}
        for name in ("outp", "clr", "nf", "fs"):
            C[name].start = 1
        for name, per in dict(wkv=1, wq=1, wg=1, cl=1, wol=1, rowl=6, dgw=8, dgr=1, tuw=1, ur=8).items():
            C[name] = Count(sem(name + "_dma"), per, 16)

        def bank(name):
            return banks[RING_AT[name] % BANKS]

        def wait_bank(pe, name, n):
            j, m = RING_AT[name] - BANKS, n
            while True:
                if j < 0:
                    j, m = j + len(RING), m - 1
                    if isinstance(m, int) and m < 0:
                        return
                use = RING[j]
                here = use is not None
                if here and isinstance(m, int):
                    here = 2 <= m < NI + 2 if use[3] else m < NI
                if here:
                    wait(pe, C[use[1]], m - 2 if use[3] else m, use[2])
                    return
                j -= BANKS

        def split(pool, q):
            b, kk = q // KD, q % KD

            def go():
                if q == 0:
                    wait(pool, C["o"], NI - 2, 4)
                    wait(pool, C["proj"], NI - 1, NT)
                r = xnT[:, kk, b * SEQ:(b + 1) * SEQ]
                for j in range(3):
                    part = parts[j][:, kk, b * SEQ:(b + 1) * SEQ]
                    if j:
                        pool.wait_ge(f_lo, 5 * q + 2 * j)
                    pool.tensor_copy(part, r).then_inc(f_lo, 1)
                    if j < 2:
                        pool.wait_ge(f_lo, 5 * q + 2 * j + 1)
                        pool.tensor_tensor(r, r, part, ALU.subtract).then_inc(f_lo, 1)
            return go

        with nc.Block() as block:
            @block.tensor
            def _(pe):
                def project(n, p, t):
                    name = f"P{t}" if t < 6 else f"G{t - 6}"
                    if t in (0, 2, 6):
                        wait(pe, C[{0: "wkv", 2: "wq", 6: "wg"}[t]], n, 1)
                    wait_bank(pe, name, n)
                    for kk in range(KD):
                        mm = pe.matmul(bank(name)[:, :], wt[:, t if t < 6 else t - 4, kk, :], xnT[:, kk, bass.ds((n // NG) * SEQ, SEQ)],
                                       start=(kk == 0), stop=(kk == KD - 1))
                    mm.then_inc(C["proj"].sem, 1)

                def gram(n, p, _):
                    wait(pe, C["silu"], n, 1)
                    wait_bank(pe, "GR0", n)
                    for c in range(NC):
                        kc = KT[p][:, c * P:(c + 1) * P]
                        mm = pe.matmul(bank("GR0")[:, c * P:(c + 1) * P], kc, kc, start=True, stop=True)
                    mm.then_inc(C["grp"].sem, 1)

                def gram_t(n, p, _):
                    wait(pe, C["gh"], n, 1)
                    wait_bank(pe, "GT0", n)
                    for c in range(NC):
                        mm = pe.transpose(bank("GT0")[:, c * P:(c + 1) * P], VT[:, c * P:(c + 1) * P], ident)
                    mm.then_inc(C["gtp"].sem, 1)

                def rows_of(src, ready, k, name, done):
                    def go(n, p, _):
                        wait(pe, C[ready], n, k)
                        wait_bank(pe, name, n)
                        t = src[p] if isinstance(src, list) else src
                        for c in range(NC):
                            mm = pe.transpose(bank(name)[:, c * P:(c + 1) * P], t[:, c * P:(c + 1) * P], ident)
                        mm.then_inc(C[done].sem, 1)
                    return go

                def stats_k(n, p, _):
                    wait(pe, C["sq"], n, 1)
                    wait_bank(pe, "SK0", n)
                    for c in range(NC):
                        mm = pe.matmul(bank("SK0")[:, c:c + 1], sqr[1][:, c * P:(c + 1) * P], cs[:, C_ONES:C_ONES + 1],
                                       start=True, stop=True)
                    mm.then_inc(C["stat"].sem, 1)

                def stats_q(n, p, c):
                    wait(pe, C["sq"], n, 2 + c)
                    if c == 0:
                        wait_bank(pe, "SQ0", n)
                    for h in range(HG):
                        mm = pe.matmul(bank("SQ0")[:, 4 * c + h:4 * c + h + 1], sqr[c % 2][:, h * P:(h + 1) * P],
                                       cs[:, C_ONES:C_ONES + 1], start=True, stop=True)
                    mm.then_inc(C["sqp"].sem, 1)

                def exponent(n, p, c):
                    wait(pe, C["rowl"], n, 6)
                    wait_bank(pe, f"E{c}", n)
                    b = bank(f"E{c}")
                    pe.matmul(b[:, :], idb[:, :], cau[:, :].unsqueeze(1).to_broadcast([P, HG, P]), start=True, stop=False)
                    pe.matmul(b[:, :], HX[:, c, :], GX[:, c, :], start=False, stop=True).then_inc(C["ep"].sem, 1)

                def row_g(n, p, c):
                    wait_bank(pe, f"QR{c}", n)
                    pe.matmul(bank(f"QR{c}")[:, :], one3[:, :], GX[:, c, :], start=True, stop=True).then_inc(C["qrp"].sem, 1)

                def qk(n, p, c):
                    wait(pe, C["silu"], n, 6)
                    wait_bank(pe, f"QK{c}", n)
                    pe.matmul(bank(f"QK{c}")[:, :], KT[p][:, c * P:(c + 1) * P], QT[p][:, c * SEQ:(c + 1) * SEQ],
                              start=True, stop=True).then_inc(C["qkp"].sem, 1)

                def out_t(n, p, c):
                    wait(pe, C["fs"], n, c + 1)
                    wait_bank(pe, f"OT{c}", n + 2)
                    for h in range(HG):
                        o = c * SEQ + h * P
                        mm = pe.transpose(bank(f"OT{c}")[:, h * P:(h + 1) * P], OB[:, o:o + P], ident)
                    mm.then_inc(C["otp"].sem, 1)

                def out_proj(n, p, c):
                    wait(pe, C["ot"], n, c + 1)
                    wait(pe, C["wol"], n, 1)
                    wait_bank(pe, f"OUT{c}", n + 2)
                    for h in range(HG):
                        mm = pe.matmul(bank(f"OUT{c}")[:, 0:D], OT[c % 2][:, h * P:(h + 1) * P], wot[:, h, :],
                                       start=(h == 0), stop=(h == HG - 1))
                    mm.then_inc(C["outp"].sem, 1)

                def half(t, c, odd, w):
                    a = halves(t, c or 0, odd, w)
                    n = a.shape[1] // HG
                    return [a[:, h * n:(h + 1) * n, :] for h in range(HG)]

                def pair(b, h):
                    return b[:, 64 * h:64 * h + 64]

                def la(n, p, c):
                    wait(pe, C["t16"], n, c + 1)
                    wait(pe, C["xe64"], n, c)
                    for h in range(HG):
                        mm = pe.matmul(pair(bX, h), heads(BP[p], c)[:, h, :], half(T, c, 0, 16)[h], start=True, stop=True)
                    mm.then_inc(C["x16"].sem, 1)

                def lb(n, p, c):
                    wait(pe, C["xm"], n, c + 1)
                    wait(pe, C["uf"], n, c)
                    if isinstance(n, int) and n == NI - 1 and c == NC - 1:
                        pe.wait_ge(f_sum, 7)
                        ones = cs[:, C_ONES:C_ONES + P]
                        pe.matmul(bZ[:, 256:258], ones, sums[:, 0:2], start=True, stop=True)
                        for j in range(2, 6):
                            pe.matmul(bZ[:, 258:259], ones, sums[:, j:j + 1], start=(j == 2), stop=(j == 5))
                    for h in range(HG):
                        mm = pe.matmul(pair(bZ, h), heads(Xf)[:, h, :], half(U[p], c, 1, 16)[h], start=True, stop=True)
                    mm.then_inc(C["z16"].sem, 1)

                def lc(n, p, c):
                    wait(pe, C["t32"], n, c + 1)
                    for h in range(HG):
                        mm = pe.matmul(pair(bX, h), heads(BP[p], c)[:, h, :], half(T, c, 0, 32)[h], start=True, stop=True)
                    mm.then_inc(C["x32"].sem, 1)

                def ld(n, p, c):
                    wait(pe, C["xe32"], n, c + 1)
                    for h in range(HG):
                        mm = pe.matmul(pair(bZ, h), heads(X32)[:, h, :], half(U[p], c, 1, 32)[h], start=True, stop=True)
                    mm.then_inc(C["z32"].sem, 1)

                def le(n, p, c):
                    wait(pe, C["u64"], n, c + 1)
                    for h in range(HG):
                        mm = pe.matmul(bX[64:128, 64 * h:64 * h + 64], heads(BP[p], c)[:, h, 64:128], heads(T, c)[:, h, 0:64],
                                       start=True, stop=True)
                    mm.then_inc(C["x64"].sem, 1)

                def lf(n, p, c):
                    wait(pe, C["xe64"], n, c + 1)
                    for h in range(HG):
                        mm = pe.matmul(bZ[0:64, 64 * h:64 * h + 64], X64[:, 64 * h:64 * h + 64], heads(U[p], c)[:, h, 64:128],
                                       start=True, stop=True)
                    mm.then_inc(C["z64"].sem, 1)

                def ra(n, p, c):
                    wait(pe, C["s"], n, c)
                    wait(pe, C["oe"], n, c)
                    pe.matmul(bO[:, :], KT[p][:, c * P:(c + 1) * P], S[:, :], start=True, stop=True).then_inc(C["ks"].sem, 1)

                def rb(n, p, c):
                    if c:
                        wait(pe, C["rr"], n, c)
                    else:
                        wait(pe, C["vn"], n, 1)
                    wait(pe, C["uf"], n, c + 1)
                    wait(pe, C["ye"], n, c)
                    for h in range(HG):
                        rhs = RY[:, h * P:(h + 1) * P] if c else Vn[p][:, 0:P]
                        mm = pe.matmul(bY[:, h * P:(h + 1) * P], heads(U[p], c)[:, h, :], rhs, start=True, stop=True)
                    mm.then_inc(C["y"].sem, 1)

                def rc(n, p, c):
                    wait(pe, C["ye"], n, c + 1)
                    wait(pe, C["pt"], n, c + 1)
                    if c:
                        wait(pe, C["qt"], n, c)
                    else:
                        wait(pe, C["oe"], n, 0)
                    for h in range(HG):
                        if c:
                            pe.matmul(bO[:, h * P:(h + 1) * P], heads(QT[p], c)[:, h, :], S[:, h * P:(h + 1) * P],
                                      start=True, stop=False)
                        mm = pe.matmul(bO[:, h * P:(h + 1) * P], heads(PT[p], c)[:, h, :], RY[:, h * P:(h + 1) * P],
                                       start=(c == 0), stop=True)
                    mm.then_inc(C["o"].sem, 1)

                def rd(n, p, c):
                    wait(pe, C["kh"], n, c + 1)
                    wait(pe, C["ye"], n, c + 1)
                    if c == 0:
                        wait(pe, C["s"], n, 0)
                    for h in range(HG):
                        mm = pe.matmul(bS[:, h * P:(h + 1) * P], Kh[c % 2][:, h * P:(h + 1) * P], RY[:, h * P:(h + 1) * P],
                                       start=True, stop=True)
                    mm.then_inc(C["su"].sem, 1)

                def scalars():
                    for t in range(16):
                        for kk in range(KD):
                            mm = pe.matmul(bX[:, 32 * t:32 * t + 32], xnT[:, kk, t * P:(t + 1) * P], bgs[:, kk, :],
                                           start=(kk == 0), stop=(kk == KD - 1))
                    mm.then_inc(s_z, 1)

                def cumsums():
                    pe.wait_ge(s_g, 8)
                    pe.matmul(bZ[:, 0:256], c0[:, C_TRI - C_ALL:C_TRI - C_ALL + P], gl, start=True, stop=True)
                    pe.matmul(bZ[:, 256:512], cs[:, C_ONES:C_ONES + P], gl, start=True, stop=True).then_inc(s_cum, 1)

                def transpose_rows():
                    pe.wait_ge(s_g, 10)
                    for q, src in enumerate((Gs, Gs, Hs, Hs)):
                        mm = pe.transpose(bO[:, q * P:(q + 1) * P], src[:, (q % 2) * P:(q % 2 + 1) * P], ident)
                    mm.then_inc(s_rt, 1)

                def first_ups(*ms):
                    if ms[0] == 0:
                        pe.wait_ge(f_q, 6)
                    for m in ms:
                        up(pe, 0, m)

                pe.sem_inc(C["outp"].sem, 1)
                pe.sem_inc(f_dn, 1)
                bodies(pe, "pe", dict(
                    P=project, G=lambda n, p, t: project(n, p, t + 6), GR=gram, GT=gram_t,
                    TK=rows_of(KT, "silu", 1, "TK0", "tkp"), TV=rows_of(VT, "silu", 2, "TV0", "tvp"),
                    SK=stats_k, SQ=stats_q, E=exponent, QR=row_g, QK=qk, OT=out_t, OUT=out_proj,
                    La=la, Lb=lb, Lc=lc, Ld=ld, Le=le, Lf=lf, Ra=ra, Rb=rb, Rc=rc, Rd=rd),
                    before=dict(P0=scalars, P2=cumsums, SK=transpose_rows),
                    last=dict(OT0=lambda: first_ups(0, 1, 2), OT1=lambda: first_ups(3), OUT0=lambda: first_ups(4),
                              OUT1=lambda: first_ups(5)))

            @block.scalar
            def _(act):
                def conv_start(n, p, t):
                    if t == 0:
                        wait(act, C["cl"], n, 1)
                    wait(act, C["proj"], n, t + 1)
                    wait(act, C["silu"], n, t - 1)
                    act.copy(xr[t % 2][:, :], bank(f"P{t}")[:, :])
                    act.activation(cacc[t % 2][:, :], bank(f"P{t}")[:, :], ACT.Identity,
                                   scale=cwt[:, t, 3:4]).then_inc(C["raw"].sem, 1)

                def silu_tanh(n, p, t):
                    wait(act, C["conv"], n, 3 * t + 3)
                    wait(act, C["silu"], n, t - 1)
                    if t < 2:
                        wait(act, C["gate"], n - 1, HG)
                    act.activation(th[t % 2][:, :], cacc[t % 2][:, :], ACT.Tanh, scale=0.5).then_inc(C["th"].sem, 1)

                def gate_tanh(n, p, h):
                    wait(act, C["proj"], n, 7 + h)
                    if h < 2:
                        wait(act, C["silu"], n, 6)
                    else:
                        wait(act, C["gate"], n, h - 1)
                    act.activation(th[h % 2][:, :], bank(f"G{h}")[:, :], ACT.Tanh, scale=0.5).then_inc(C["th"].sem, 1)

                def gram_scaled(n, p, _):
                    wait(act, C["kn_"], n, 1)
                    wait(act, C["grp"], n, 1)
                    wait(act, C["tvp"], n, 1)
                    for c in range(NC):
                        last = act.activation(VT[:, c * P:(c + 1) * P], bank("GR0")[:, c * P:(c + 1) * P], ACT.Identity,
                                              scale=rk[p][:, c:c + 1])
                    last.then_inc(C["gh"].sem, 1)

                def k_rows(n, p, _):
                    wait(act, C["tkp"], n, 1)
                    wait(act, C["kh"], n - 2, 3)
                    act.copy(Kn[p][:, :], bank("TK0")[:, :]).then_inc(C["kn"].sem, 1)

                def v_rows(n, p, _):
                    wait(act, C["tvp"], n, 1)
                    wait(act, C["rr"], n - 2, 3)
                    act.mul(Vn[p][:, :], bank("TV0")[:, :], 0.5).then_inc(C["vn"].sem, 1)

                def decay(n, p, c):
                    wait(act, C["ep"], n, c + 1)
                    wait(act, C["o"], n - 2, c + 1)
                    act.activation(PT[p][:, c * SEQ:(c + 1) * SEQ], bank(f"E{c}")[:, :], ACT.Exp).then_inc(C["e"].sem, 1)

                def row_decay(n, p, c):
                    wait(act, C["qrp"], n, c)
                    wait(act, C["bp"], n, 4)
                    wait(act, C["qt"], n, c - 1)
                    act.activation(gr[:, :], bank(f"QR{c}")[:, :], ACT.Exp).then_inc(C["eq"].sem, 1)

                def lc(n, p, c):
                    wait(act, C["x32"], n, c + 1)
                    act.mul(halves(X32, 0, 0, 32), bX[:, 0:256].rearrange("p (g u) -> p g u", u=32), -1.0).then_inc(C["xe32"].sem, 1)

                def le(n, p, c):
                    wait(act, C["x64"], n, c + 1)
                    act.mul(X64[64:128, :], bX[64:128, 0:256], -1.0).then_inc(C["xe64"].sem, 1)

                def lf(n, p, c):
                    wait(act, C["z64"], n, c + 1)
                    act.copy(heads(U[p], c)[0:64, :, 64:128],
                             bZ[0:64, 0:256].rearrange("p (h u) -> p h u", h=HG)).then_inc(C["uf"].sem, 1)

                def rb(n, p, c):
                    wait(act, C["y"], n, c + 1)
                    wait(act, C["o"], n, c)
                    act.copy(RY[:, :], bY[:, :]).then_inc(C["ye"].sem, 1)

                def rc(n, p, c):
                    wait(act, C["o"], n, c + 1)
                    wait(act, C["outp" if c == NC - 1 else "otp"], n - 1, c + 1)
                    act.copy(OB[:, c * SEQ:(c + 1) * SEQ], bO[:, :]).then_inc(C["oe"].sem, 1)

                def square_k(n, p, _):
                    wait(act, C["silu"], n, 1)
                    wait(act, C["sqp"], n - 1, 4)
                    act.activation(sqr[1][:, :], KT[p][:, :], ACT.Square).then_inc(C["sq"].sem, 1)

                def square_q(n, p, c):
                    wait(act, C["silu"], n, 6)
                    if c < 2:
                        wait(act, C["stat"], n, 1)
                    else:
                        wait(act, C["sqp"], n, c - 1)
                    act.activation(sqr[c % 2][:, :], QT[p][:, c * SEQ:(c + 1) * SEQ], ACT.Square).then_inc(C["sq"].sem, 1)

                def square_o(n, p, c):
                    wait(act, C["oe"], n, c + 1)
                    wait(act, C["sr"], n, c)
                    act.activation(o2[:, :], OB[:, c * SEQ:(c + 1) * SEQ], ACT.Square).then_inc(C["o2"].sem, 1)

                def scale_out(n, p, c):
                    wait(act, C["nf"], n, 1)
                    for h in range(HG):
                        o = OB[:, c * SEQ + h * P:c * SEQ + (h + 1) * P]
                        last = act.activation(o, o, ACT.Identity, scale=fo[:, 4 * c + h:4 * c + h + 1])
                    last.then_inc(C["fs"].sem, 1)

                def softplus():
                    act.wait_ge(s_abs, 1)
                    act.activation(ez, na, ACT.Exp).then_inc(s_exp, 1)
                    act.wait_ge(s_exp, 1)
                    act.activation(ez, ez, ACT.Ln, bias=1.0).then_inc(s_log, 1)

                def decays():
                    act.wait_ge(s_cum, 1)
                    act.activation(eG[:, :], bZ[:, 0:256], ACT.Exp).then_inc(s_eg, 1)
                    act.activation(eGC[:, :], bZ[:, 256:512], ACT.Exp).then_inc(s_eg, 1)
                    act.wait_ge(s_w, 1)
                    act.activation(wK[:, :], Ws, ACT.Exp).then_inc(s_eg, 1)
                    act.wait_ge(s_eg, 1)
                    act.mul(eG[:, :], eG[:, :], -1.0).then_inc(s_eg, 1)

                def first_tanhs(*ms):
                    if ms[0] == 0:
                        wait(act, C["gate"], NI - 1, HG)
                    for m in ms:
                        up_tanh(act, 0, m)

                act.sem_inc(C["fs"].sem, 1)
                bodies(act, "act", dict(
                    P=conv_start, H=silu_tanh, G=gate_tanh, GS=gram_scaled, TK=k_rows, TV=v_rows, E=decay,
                    SK=square_k, SQ=square_q, QR=row_decay, Lc=lc, Le=le, Lf=lf, Rb=rb, Rc=rc, Ro=square_o, FS=scale_out),
                       before=dict(P0=softplus, H0=decays),
                       last=dict(FS0=lambda: first_tanhs(0, 1), FS2=lambda: first_tanhs(2), FS3=lambda: first_tanhs(3)))
                first_tanhs(4, 5)

            @block.vector
            def _(dve):
                def tap(d):
                    def conv(n, p, t):
                        if d == 1:
                            wait(dve, C["raw"], n, t + 1)
                        else:
                            wait(dve, C["conv"], n, 3 * t + d - 1)
                        a, b = cacc[t % 2], xr[t % 2]
                        dve.scalar_tensor_tensor(a[:, d:SEQ], b[:, 0:SEQ - d], cwt[:, t, 3 - d:4 - d], a[:, d:SEQ],
                                                 ALU.mult, ALU.add).then_inc(C["conv"].sem, 1)
                    return conv

                def silu(n, p, t):
                    wait(dve, C["th"], n, t + 1)
                    if t == 0:
                        wait(dve, C["ks"], n - 2, 3)
                        dst = KT[p][:, :]
                    elif t == 1:
                        wait(dve, C["gtp"], n - 1, 1)
                        dst = VT[:, :]
                    else:
                        wait(dve, C["o"], n - 2, 4)
                        dst = QT[p][:, :].rearrange("p (c h t) -> p c h t", c=NC, h=HG)[:, :, t - 2, :]
                    a, b = th[t % 2][:, :], cacc[t % 2][:, :]
                    if t >= 2:
                        a, b = (v.rearrange("p (c t) -> p c t", c=NC) for v in (a, b))
                    dve.scalar_tensor_tensor(dst, a, 1.0, b, ALU.add, ALU.mult).then_inc(C["silu"].sem, 1)

                def gate(n, p, h):
                    wait(dve, C["th"], n, 7 + h)
                    wait(dve, C["ot"], n - 2, 4)
                    dve.scalar_tensor_tensor(SG[p][:, h * SEQ:(h + 1) * SEQ], th[h % 2][:, :], 1.0, bank(f"G{h}")[:, :],
                                             ALU.add, ALU.mult).then_inc(C["gate"].sem, 1)

                def stats_k(n, p, _):
                    wait(dve, C["stat"], n, 1)
                    dve.tensor_scalar(kx[:, :], bank("SK0")[:, 0:NC], 4e-6, None, ALU.add).then_inc(C["nk"].sem, 1)

                def gram_cols(n, p, _):
                    wait(dve, C["gtp"], n, 1)
                    wait(dve, C["kn_"], n, 1)
                    wait(dve, C["qt"], n - 1, 3)
                    for c in range(NC):
                        last = dve.scalar_tensor_tensor(gr[:, c * P:(c + 1) * P], bank("GT0")[:, c * P:(c + 1) * P],
                                                        rk[p][:, c:c + 1], cs[:, C_STR:C_STR + P], ALU.mult, ALU.mult)
                    last.then_inc(C["gr"].sem, 1)

                def stats_q(n, p, _):
                    wait(dve, C["sqp"], n, 4)
                    dve.tensor_scalar(eq2[p][:, :], bank("SQ0")[:, 0:16], OUT_EPS * P, OUT_EPS * P * 4e-6,
                                      ALU.mult, ALU.add).then_inc(C["nq"].sem, 1)

                def weigh(n, p, c):
                    wait(dve, C["qkp"], n, c + 1)
                    wait(dve, C["bp"], n, c + 1)
                    t = PT[p][:, c * SEQ:(c + 1) * SEQ]
                    dve.scalar_tensor_tensor(t, bank(f"QK{c}")[:, :], rk[p][:, c:c + 1], t,
                                             ALU.mult, ALU.mult).then_inc(C["pt"].sem, 1)

                def la(n, p, c):
                    wait(dve, C["x16"], n, c + 1)
                    neg = cs[:, C_NEG:C_NEG + 64].unsqueeze(1).to_broadcast([P, HG, 64])
                    dve.tensor_tensor(halves(Xf, 0, 0, 16).rearrange("p (h m) u -> p h m u", h=HG),
                                      bX[:, 0:256].rearrange("p (h m u) -> p h m u", h=HG, m=4),
                                      neg.rearrange("p h (m u) -> p h m u", m=4), ALU.mult).then_inc(C["xm"].sem, 1)

                def lt(n, p, c):
                    if c == 0:
                        wait(dve, C["ur"], n, 8)
                        wait(dve, C["clr"], n - 2, 3)
                    wait(dve, C["x64"], n - 1, c + 1)
                    dve.transpose(T[:, c * SEQ:(c + 1) * SEQ], U[p][:, c * SEQ:(c + 1) * SEQ]).then_inc(C["t16"].sem, 1)

                def lb(n, p, c):
                    wait(dve, C["z16"], n, c + 1)
                    if isinstance(n, int) and n == NI - 1 and c == NC - 1:
                        dve.tensor_scalar(thr, bZ[:, 256:259], 0.5 / (F * D), 0.5e-8, ALU.mult, ALU.add).then_inc(f_q, 1)
                        dve.tensor_scalar(nthr, bZ[:, 256:259], -0.5 / (F * D), -0.5e-8, ALU.mult, ALU.add).then_inc(f_q, 1)
                    dve.tensor_tensor(halves(U[p], c, 1, 16), bZ[:, 0:256].rearrange("p (g u) -> p g u", u=16),
                                      halves(U[p], c, 1, 16), ALU.add).then_inc(C["u32"].sem, 1)
                    wait(dve, C["u32"], n, c + 1)
                    dve.transpose(T[:, c * SEQ:(c + 1) * SEQ], U[p][:, c * SEQ:(c + 1) * SEQ]).then_inc(C["t32"].sem, 1)

                def ld(n, p, c):
                    wait(dve, C["z32"], n, c + 1)
                    u = heads(U[p], c)
                    z = bZ[:, 0:256].rearrange("p (h m u) -> p h m u", h=HG, m=2)
                    dve.tensor_copy(u[0:32, :, 32:64], z[0:32, :, 0, :])
                    dve.transpose(heads(T, c)[32:64, :, 0:32], z[0:32, :, 0, :])
                    dve.tensor_copy(u[64:96, :, 96:128], z[64:96, :, 1, :]).then_inc(C["u64"].sem, 1)

                def ra(n, p, c):
                    wait(dve, C["ks"], n, c)
                    wait(dve, C["o"], n, c)
                    wait(dve, C["vn"], n, 1)
                    wait(dve, C["ks_"], n, 3)
                    for h in range(HG):
                        j = 4 * c + h
                        last = dve.scalar_tensor_tensor(RY[:, h * P:(h + 1) * P], bO[:, h * P:(h + 1) * P], sR[p][:, j:j + 1],
                                                        Vn[p][:, c * P:(c + 1) * P], ALU.mult, ALU.add)
                    last.then_inc(C["rr"].sem, 1)
                    if isinstance(n, int) and n == NI - 1 and c == NC - 1:
                        ternary(1)()

                def rd(n, p, c):
                    wait(dve, C["su"], n, c + 1)
                    wait(dve, C["o"], n, c + 1)
                    if c == 0:
                        dve.tensor_copy(S[:, :], bS[:, :]).then_inc(C["s"].sem, 1)
                    else:
                        wait(dve, C["s"], n, c)
                        for h in range(HG):
                            j = 4 * c + h
                            s = S[:, h * P:(h + 1) * P]
                            last = dve.scalar_tensor_tensor(s, s, dec[p][:, j:j + 1], bS[:, h * P:(h + 1) * P],
                                                            ALU.mult, ALU.add)
                        last.then_inc(C["s"].sem, 1)

                def rs(n, p, c):
                    wait(dve, C["o2"], n, c + 1)
                    dve.tensor_reduce(so[p][:, 4 * c:4 * c + 4], heads(o2), AX.X, ALU.add).then_inc(C["sr"].sem, 1)

                def out_factor(n, p, _):
                    wait(dve, C["sr"], n, 4)
                    wait(dve, C["nq"], n, 1)
                    wait(dve, C["nf"], n - 1, 1)
                    dve.scalar_tensor_tensor(fx[:, :], so[p][:, :], 1.0 / P, eq2[p][:, :], ALU.mult, ALU.add).then_inc(C["fx"].sem, 1)

                def clear(n, p, _):
                    if isinstance(n, int) and n >= NI - 2:
                        return
                    wait(dve, C["y"], n, 4)
                    u = U[p][:, :].rearrange("p (u t) -> p u t", t=P)
                    for b in range(3):
                        dve.memset(u[32 * b:32 * b + 32, :, 32 * b + 32:P], 0.0).then_inc(C["clr"].sem, 1)

                def gated(n, p, c):
                    wait(dve, C["otp"], n, c + 1)
                    wait(dve, C["outp"], n, max(c - 1, 0))
                    sg = SG[p][:, :].rearrange("p (h t) -> p h t", h=HG)[:, :, c * P:(c + 1) * P]
                    dve.scalar_tensor_tensor(heads(OT[c % 2]), bank(f"OT{c}")[:, :].rearrange("p (h t) -> p h t", h=HG),
                                             wv[:, 0:1], sg, ALU.mult, ALU.mult).then_inc(C["ot"].sem, 1)

                def add_out(n, p, c):
                    wait(dve, C["outp"], n, c + 1)
                    a = acc[:, bass.ds((n // NG) * (NC * D) + c * D, D)]
                    dve.tensor_tensor(a, bank(f"OUT{c}")[:, 0:D], a, ALU.add).then_inc(C["acc"].sem, 1)

                def log_sigmoids():
                    dve.wait_ge(s_z, 1)
                    dve.tensor_copy(zs, bX[:, :]).then_inc(s_zc, 1)
                    dve.wait_ge(s_zc, 1)
                    dve.tensor_scalar(na, zs, -1.0, None, ALU.mult).then_inc(s_zc, 1)
                    dve.wait_ge(s_zc, 2)
                    dve.tensor_tensor(na, na, zs, ALU.min).then_inc(s_abs, 1)
                    dve.wait_ge(s_log, 1)
                    dve.scalar_tensor_tensor(spl, zs, 0.0, ez, ALU.min, ALU.subtract).then_inc(s_zc, 1)
                    dve.wait_ge(s_zc, 3)
                    sv = spl.rearrange("p (b c o) -> p b c o", b=NB, c=NC)
                    for b in range(NB):
                        for dst, o, f in ((gl, 0, 1.0 / 16.0), (ln_beta, 16, 1.0)):
                            dve.tensor_scalar(dst[:, b * 64:(b + 1) * 64].rearrange("p (g c h) -> p g c h", g=NG, c=NC),
                                              sv[:, b, :, o:o + 16].rearrange("p c (g h) -> p g c h", g=NG),
                                              f, None, ALU.mult).then_inc(s_g, 1)

                def decays():
                    dve.wait_ge(s_eg, 2)
                    dve.wait_ge(s_g, 8)
                    dve.tensor_copy(Gs, bZ[:, 0:256]).then_inc(s_g, 1)
                    dve.tensor_tensor(Hs, ln_beta, bZ[:, 0:256], ALU.subtract).then_inc(s_g, 1)
                    dve.wait_ge(s_g, 10)
                    dve.tensor_tensor(Ws, Hs, bZ[:, 256:512], ALU.add).then_inc(s_w, 1)
                    dve.wait_ge(s_bg, 32)
                    dve.tensor_scalar(wv[:, :], wv[:, :], 0.5, None, ALU.mult).then_inc(s_w, 1)

                def row_splits():
                    dve.wait_ge(s_rt, 1)
                    rp = [rowp[:, :, a, :] for a in range(3)]
                    rf = rowf.rearrange("p (q t) -> p q t", q=4)
                    rr = rest.rearrange("p (q t) -> p q t", q=4)
                    dve.tensor_copy(rp[0], bO[:, :].rearrange("p (q t) -> p q t", q=4)).then_inc(s_split, 1)
                    dve.wait_ge(s_split, 1)
                    dve.tensor_tensor(rf, bO[:, :].rearrange("p (q t) -> p q t", q=4), rp[0], ALU.subtract).then_inc(s_split, 1)
                    dve.wait_ge(s_split, 2)
                    dve.tensor_copy(rp[1], rf).then_inc(s_split, 1)
                    dve.wait_ge(s_split, 3)
                    dve.tensor_tensor(rr, rf, rp[1], ALU.subtract).then_inc(s_split, 1)
                    dve.wait_ge(s_split, 4)
                    dve.tensor_copy(rp[2], rr).then_inc(s_split, 1)

                def abs_sums(*js):
                    def go():
                        if js[0] == 0:
                            dve.memset(sums, 0.0).then_inc(f_sum, 1)
                            dve.wait_ge(f_w, 16 * (2 + FM))
                            dve.wait_ge(f_sum, 1)
                        for j in js:
                            src = raw[j] if j < 2 else (KT[0], Kn[0])[j - 2][:, :] if j < 4 else w3[4]
                            dve.tensor_reduce(sums[:, j:j + 1], src, AX.X, ALU.add, apply_absolute_value=True).then_inc(f_sum, 1)
                        if js[-1] == 4:
                            dve.tensor_reduce(sums[0:FR, 5:6], w3[5][0:FR], AX.X, ALU.add, apply_absolute_value=True).then_inc(f_sum, 1)
                    return go

                def ternary(j):
                    def go():
                        if j < 2:
                            todo = [(w12[j][:, :, 0:F], raw[j].rearrange("p (k f) -> p k f", k=KD),
                                     taps4[:, 0:KD * F].rearrange("p (k f) -> p k f", k=KD), P)]
                        else:
                            todo = [(t[0:r, 0:w], t[0:r, 0:w], taps4[0:r, i * SEQ:i * SEQ + w], r) for i, (t, r, w) in enumerate(
                                ((KT[0], P, SEQ), (Kn[0], P, SEQ), (Vn[0], P, D)))]
                            todo.append((w3[5][0:FR], w3[5][0:FR], taps4[0:FR, 3 * SEQ:3 * SEQ + D], FR))
                            dve.memset(w3[5][FR:P], 0.0).then_inc(f_q, 1)
                        done = 2 + 2 * j + (j == 2)
                        dve.wait_ge(f_q, done)
                        for i, (dst, src, low, r) in enumerate(todo):
                            dve.tensor_scalar(low, src, nthr[0:r, j:j + 1], None, ALU.is_lt).then_inc(f_q, 1)
                            dve.wait_ge(f_q, done + 1 + 2 * i)
                            dve.scalar_tensor_tensor(dst, src, thr[0:r, j:j + 1], low, ALU.is_gt, ALU.subtract).then_inc(f_q, 1)
                    return go

                def pads():
                    for w in w12:
                        dve.memset(w[:, :, F:FP], 0.0)

                ffn = dict(H2=abs_sums(0), H3=abs_sums(1), H4=abs_sums(2, 3), H5=abs_sums(4), QK2=pads, QK3=ternary(0))
                def first_hiddens(*ms):
                    if ms[0] == 0:
                        ternary(2)()
                    for m in ms:
                        hidden(dve, 0, m)

                dve.sem_inc(f_hid, 1)
                dve.sem_inc(C["clr"].sem, 1)
                bodies(dve, "dve", dict(
                    Ca=tap(1), Cb=tap(2), Cc=tap(3), H=silu, G=gate, SK=stats_k, GT=gram_cols, SQ=stats_q, QK=weigh,
                    Lt=lt, La=la, Lb=lb, Ld=ld, Ra=ra, Rd=rd, Rs=rs, FN=out_factor, CL=clear, OT=gated, OUT=add_out),
                       before=dict(Ca0=log_sigmoids, Cc0=decays, Ca1=row_splits), after=ffn,
                       last=dict(OT0=lambda: first_hiddens(0, 1), OT1=lambda: first_hiddens(2), OUT0=lambda: first_hiddens(3)))
                first_hiddens(4, 5)

            @block.gpsimd
            def _(pool):
                def build_b(n, p, c):
                    wait(pool, C["e"], n, c + 1)
                    if c == 0:
                        wait(pool, C["gr"], n, 1)
                    g = gr[:, c * P:(c + 1) * P].unsqueeze(1).to_broadcast([P, HG, P])
                    pool.tensor_tensor(heads(BP[p], c), heads(PT[p], c), g, ALU.mult).then_inc(C["bp"].sem, 1)

                def q_decay(n, p, c):
                    wait(pool, C["eq"], n, c)
                    wait(pool, C["qkp"], n, c + 1)
                    wait(pool, C["sq"], n, c + 2)
                    q = QT[p][:, c * SEQ:(c + 1) * SEQ]
                    pool.tensor_tensor(q, q, gr[:, :], ALU.mult).then_inc(C["qt"].sem, 1)

                def invert_blocks(n, p, j):
                    sub = C["sub"]
                    eye = cs[:, C_EYE:C_EYE + 256].rearrange("p (r t) -> p r t", r=16)
                    if j == 0:
                        pool.tensor_copy(blkU[:, :, :], eye).then_inc(sub.sem, 1)
                        wait(pool, C["dgr"], n, 1)
                        wait(pool, C["tuw"], n - 1, 1)
                    for s in range(15 - 5 * j, 10 - 5 * j, -1):
                        w = 16 - s
                        t = blkt[:, 0:s * w].rearrange("p (r t) -> p r t", r=s)
                        col = blkB[:, 0:s, s:s + 1].to_broadcast([P, s, w])
                        row = blkU[:, s:s + 1, s:16].to_broadcast([P, s, w])
                        wait(pool, sub, n, 1 + 2 * (w - 1))
                        pool.tensor_tensor(t, col, row, ALU.mult).then_inc(sub.sem, 1)
                        wait(pool, sub, n, 2 + 2 * (w - 1))
                        u = blkU[:, 0:s, s:16]
                        pool.tensor_tensor(u, u, t, ALU.subtract).then_inc(sub.sem, 1)
                    if j < 2:
                        return
                    wait(pool, sub, n, 31)
                    for half, mcol in ((0, C_EVEN), (1, C_ODD)):
                        last = pool.tensor_tensor(blkO[:, :, 16 * half:16 * half + 16], blkU[:, :, :],
                                                  cs[:, mcol:mcol + 1].unsqueeze(2).to_broadcast([P, 16, 16]), ALU.mult)
                    last.then_inc(sub.sem, 1)

                def norm_k(n, p, _):
                    wait(pool, C["nk"], n, 1)
                    wait(pool, C["rr"], n - 2, 3)
                    wait(pool, C["s"], n - 2, 3)
                    pool.tensor_tensor(rk[p][:, :], kx[:, :], nhalf[:, 0:NC], ALU.pow).then_inc(C["kn_"].sem, 1)
                    r, g = each(rk[p][:, :], HG), bass.ds(n * 16, 16)

                    def by(t):
                        return t.rearrange("p (c h) -> p c h", c=NC)
                    wait(pool, C["kn_"], n, 1)
                    pool.tensor_tensor(by(wk[p][:, :]), by(wK[:, g]), r, ALU.mult).then_inc(C["ks_"].sem, 1)
                    pool.tensor_tensor(by(sR[p][:, :]), by(eG[:, g]), r, ALU.mult).then_inc(C["ks_"].sem, 1)
                    pool.tensor_copy(dec[p][:, :], eGC[:, g]).then_inc(C["ks_"].sem, 1)

                def norm_o(n, p, _):
                    wait(pool, C["fx"], n, 1)
                    wait(pool, C["fs"], n - 1, 4)
                    pool.tensor_tensor(fo[:, :], fx[:, :], nhalf[:, :], ALU.pow).then_inc(C["nf"].sem, 1)

                def k_scaled(n, p, c):
                    wait(pool, C["ks_"], n, 3)
                    wait(pool, C["kn"], n, 1)
                    wait(pool, C["su"], n, c - 1 if c else 0)
                    k = Kn[p][:, c * P:(c + 1) * P].unsqueeze(1).to_broadcast([P, HG, P])
                    pool.tensor_tensor(heads(Kh[c % 2]), k, each(wk[p][:, 4 * c:4 * c + 4]), ALU.mult).then_inc(C["kh"].sem, 1)

                split_at = ("E0", "E1", "E2", "E3")
                pool.sem_inc(C["nf"].sem, 1)
                bodies(pool, "pool", dict(E=build_b, QR=q_decay, IV=invert_blocks, SK=norm_k, FN=norm_o, Rk=k_scaled),
                       after={stage: split(pool, q) for q, stage in enumerate(split_at)})

            @block.sync
            def _(sp):
                def weights(n, name, lo, hi):
                    wait(sp, C["proj"], n - 1, 2 if lo == 0 else NT)
                    sp.dma_start(wt[:, lo:hi], wa[bass.ds(n % NG, 1), :, lo:hi].rearrange("a p t k o -> (a p) t k o")
                                 ).then_inc(C[name].sem, 16)

                def gate_weights(n):
                    wait(sp, C["proj"], n, 6)
                    sp.dma_start(wt[:, 2:6], wa[bass.ds(n % NG, 1), :, 6:NT].rearrange("a p t k o -> (a p) t k o")
                                 ).then_inc(C["wg"].sem, 16)

                def taps(n):
                    wait(sp, C["conv"], n - 1, 18)
                    sp.dma_start(cwt[:], cw[bass.ds(n % NG, 1)].rearrange("a p t i -> (a p) t i")).then_inc(C["cl"].sem, 16)

                def row_parts(n):
                    wait(sp, C["ep"], n - 1, 4)
                    wait(sp, C["qrp"], n - 1, 3)
                    i = n % NI
                    for a in range(3):
                        g = rows[bass.ds(i * 16, 16), a, :].rearrange("(o r) t -> o r t", o=1)
                        sp.dma_start(GX[a:a + 1].rearrange("p c (h t) -> p (c h) t", h=HG), g).then_inc(C["rowl"].sem, 16)
                        h = rows[bass.ds(256 + i * 16, 16), a, :].rearrange("(c h) t -> h c t", h=HG)
                        sp.dma_start(HX[3 + 4 * a:7 + 4 * a], h).then_inc(C["rowl"].sem, 16)

                def out_weights(n):
                    wait(sp, C["outp"], n - 1, 4)
                    sp.dma_start(wot[:], wo[bass.ds(n % NG, 1)].rearrange("a p h d -> (a p) h d")).then_inc(C["wol"].sem, 16)

                def blocks_out(n, p):
                    wait(sp, C["bp"], n, 4)
                    for b in range(8):
                        src = BP[p][16 * b:16 * b + 16, :].rearrange("p (u t) -> p u t", t=P)[:, :, 16 * b:16 * b + 16]
                        dst = diag.rearrange("(u b) r t -> b r u t", b=8)[b]
                        sp.dma_start(dst, src).then_inc(C["dgw"].sem, 16)
                    wait(sp, C["dgw"], n, 8)
                    wait(sp, C["sub"], n - 1, 32)
                    sp.dma_start(blkB[:], diag).then_inc(C["dgr"].sem, 16)

                def store_inverses(n):
                    wait(sp, C["sub"], n, 32)
                    wait(sp, C["ur"], n - 1, 8)
                    sp.dma_start(tri_d, blkO[:]).then_inc(C["tuw"].sem, 16)
                    wait(sp, C["tuw"], n, 1)

                def place_inverses(n, p):
                    wait(sp, C["y"], n - 2, 4)
                    wait(sp, C["t32"], n - 2, 4)
                    for b in range(8):
                        lo = 32 * (b // 2)
                        dst = U[p][16 * b:16 * b + 16, :].rearrange("p (u t) -> p u t", t=P)[:, :, lo:lo + 32]
                        src = tri_d.rearrange("(u b) r t -> b r u t", b=8)[b]
                        sp.dma_start(dst, src).then_inc(C["ur"].sem, 16)

                def body(k, p):
                    n, q = k + 1, (p + 1) % 2
                    weights(n + 1, "wkv", 0, 2)
                    first = isinstance(k, int) and k == -1
                    if first:
                        gate_weights(n)
                    blocks_out(n, q)
                    if not first:
                        gate_weights(n)
                    taps(n + 1)
                    store_inverses(n)
                    place_inverses(n, q)
                    row_parts(n + 1)
                    weights(n + 1, "wq", 2, 6)

                weights(0, "wkv", 0, 2)
                taps(0)
                weights(0, "wq", 2, 6)
                out_weights(0)
                for q in range(4):
                    sp.wait_ge(s_split, 5)
                    sp.dma_start(rows[q * P:(q + 1) * P], rowp[:, q]).then_inc(s_rows, 16)
                sp.wait_ge(s_rows, 64)
                row_parts(0)
                body(-1, 1)
                body(0, 0)
                with sp.Fori(0, (NI - 2) // 2) as i:
                    body(2 * i + 1, 1)
                    out_weights(2 * i + 1)
                    body(2 * i + 2, 0)
                    out_weights(2 * i + 2)
                for name, m in (("wkv", 1), ("wq", 1), ("cl", 1), ("rowl", 6)):
                    wait(sp, C[name], NI, m)
                wait(sp, C["o"], NI - 2, 4)
                wait(sp, C["y"], NI - 2, 4)
                wait(sp, C["t32"], NI - 2, 4)
                wait(sp, C["kh"], NI - 2, 3)
                wait(sp, C["proj"], NI - 1, NT)
                sp.dma_start(raw[0].rearrange("p (k f) -> p k f", k=KD), w1t.rearrange("(k p) f -> p k f", k=KD)).then_inc(f_w, 16)
                sp.dma_start(raw[1].rearrange("p (k f) -> p k f", k=KD), w2t.rearrange("(k p) f -> p k f", k=KD)).then_inc(f_w, 16)
                for m in range(FM):
                    r = FR if m == FM - 1 else P
                    sp.dma_start(w3[m][0:r], w3t[m * P:m * P + r]).then_inc(f_w, 16)
                out_weights(NI - 1)

        xin, fin = (VT[:, 0:D], VT[:, D:2 * D]), (gr[:, 0:D], gr[:, D:2 * D])
        tg = [Kh[j][:, 0:D] for j in range(2)]
        ug = [OT[j][:, 0:D] for j in range(2)]
        with nc.Block() as block:
            f_tg, f_ug, f_xin, f_fin, f_st = (sem(x) for x in ("down_tanh", "gated_steps", "x_reloaded", "final_ready", "stored"))

            @block.sync
            def _(sp):
                sp.sem_inc(f_st, 16)
                with sp.Fori(0, NB) as b:
                    for c in range(NC):
                        t = b * NC + c
                        sp.wait_ge(f_fin, t + 1 if c == 0 else t)
                        sp.dma_start(xin[c % 2], x[bass.ds(t * P, P), :]).then_inc(f_xin, 16)
                        sp.wait_ge(f_fin, t + 2)
                        sp.dma_start(out[bass.ds(t * P, P), :], fin[c % 2]).then_inc(f_st, 16)
                sp.wait_ge(f_st, 16 * NB * NC + 16)

            @block.gpsimd
            def _(pool):
                for q in range(4, KD * NB):
                    split(pool, q)()

            @block.vector
            def _(dve):
                for x1 in (f_ug, f_fin):
                    dve.sem_inc(x1, 1)

                def gated(b):
                    for c in range(NC):
                        t = b * NC + c
                        dve.wait_ge(f_tg, t + 1)
                        dve.scalar_tensor_tensor(ug[c % 2], tg[c % 2], 1.0, banks[c % 2][:, 0:D], ALU.add, ALU.mult).then_inc(f_ug, 1)
                        dve.wait_ge(f_ug, 2 * t + 2)
                        dve.scalar_tensor_tensor(ug[c % 2], ug[c % 2], 0.25, acc[:, bass.ds(t * D, D)], ALU.mult, ALU.mult).then_inc(f_ug, 1)
                        dve.wait_ge(f_ug, 2 * t + 3)
                        dve.wait_ge(f_xin, 16 * t + 16)
                        dve.wait_ge(f_st, 16 * t + 16 if c == 0 else 16 * t)
                        dve.tensor_tensor(fin[c % 2], ug[c % 2], xin[c % 2], ALU.add).then_inc(f_fin, 1)

                with dve.Fori(0, NB - 1) as b:
                    gated(b)
                    for m in range(FM):
                        hidden(dve, b + 1, m)
                gated(NB - 1)

            @block.scalar
            def _(act):
                def down_tanh(b):
                    for c in range(NC):
                        t = b * NC + c
                        act.wait_ge(f_dn, t + 2)
                        act.wait_ge(f_ug, 2 * t - 1 if c > 0 else 2 * t + 1)
                        act.activation(tg[c % 2], banks[c % 2][:, 0:D], ACT.Tanh, scale=0.25).then_inc(f_tg, 1)

                with act.Fori(0, NB - 1) as b:
                    down_tanh(b)
                    for m in range(FM):
                        up_tanh(act, b + 1, m)
                down_tanh(NB - 1)

            @block.tensor
            def _(pe):
                def down(b):
                    for c in range(NC):
                        t = b * NC + c
                        pe.wait_ge(f_ug, 2 * t + 1 if c == 0 else 2 * t - 1)
                        for m in range(FM):
                            if c == 0:
                                pe.wait_ge(f_hid, b * FM + m + 2)
                            mm = pe.matmul(banks[c % 2][:, 0:D], hid[m][:, c * P:(c + 1) * P], w3[m],
                                           start=(m == 0), stop=(m == FM - 1))
                        mm.then_inc(f_dn, 1)

                with pe.Fori(0, NB - 1) as b:
                    down(b)
                    for m in range(FM):
                        up(pe, b + 1, m)
                down(NB - 1)


def constants():
    import numpy as np
    p, t = np.arange(P)[:, None], np.arange(P)[None, :]
    c = np.zeros((P, C_END), np.float32)
    c[:, C_ID:C_ID + P] = p == t
    c[:, C_TRI:C_TRI + P] = p <= t
    c[:, C_STR:C_STR + P] = p < t
    c[:, C_CAU:C_CAU + P] = np.where(p <= t, 0.0, -1e30)
    head = np.arange(HG * P)[None, :] // P
    c[:, C_IND:C_IND + HG * P] = (p >= 3) & (p < 15) & ((p - 3) % HG == head)
    c[:, C_THREE:C_THREE + P] = p < 3
    j = np.arange(64)[None, :]
    c[:, C_NEG:C_NEG + 64] = np.where((p // 32 == j // 16) & (p % 32 >= 16), -1.0, 0.0)
    c[:, C_EVEN] = np.arange(P) % 2 == 0
    c[:, C_ODD] = np.arange(P) % 2 == 1
    c[:, C_ONES:C_ONES + P] = 1.0
    c[:, C_EYE:C_EYE + 256] = np.eye(16, dtype=np.float32).reshape(1, 256)
    return c


def kernel(**inputs):
    import numpy as np
    import concourse.bacc as bacc
    from concourse import mybir as mb
    from concourse.bass_utils import run_bass_kernel_spmd

    a = {k.replace("L0_", ""): np.ascontiguousarray(v) for k, v in inputs.items()}
    qkv = a["attn_qkv_w"].reshape(6 * HG, P, D)
    tap = a["attn_conv_w"].reshape(6 * HG, P, 4)
    gw = a["attn_g_w"].reshape(4 * HG, P, D)
    order = [[16 + g, 20 + g] + [4 * g + h for h in range(HG)] for g in range(NG)]
    tiles = np.stack([np.concatenate([qkv[order[g]], gw[4 * g:4 * g + 4]]) for g in range(NG)])
    arrays = {
        "x": a["attn_hidden_states"].reshape(NI * P, D),
        "wa": tiles.reshape(NG, NT, P, KD, P).transpose(0, 4, 1, 3, 2),
        "cw": np.stack([tap[order[g]] for g in range(NG)]).transpose(0, 2, 1, 3),
        "bgk": np.concatenate([a["attn_gk_w"], a["attn_b_w"]]).reshape(32, KD, P).transpose(2, 1, 0),
        "wo": a["attn_o_w"].reshape(D, NG, HG, P).transpose(1, 3, 2, 0),
        "onw": a["attn_out_norm_w"].reshape(P, 1),
        "w1t": a["ffn_w1"].T, "w2t": a["ffn_w2"].T, "w3t": a["ffn_w3"].T,
        "cst": constants(),
    }
    arrays = {f"in_{k}": np.ascontiguousarray(v) for k, v in arrays.items()}
    nc = bacc.Bacc("TRN2", target_bir_lowering=False, num_devices=1)
    args = {k[3:]: nc.dram_tensor(k, v.shape, mb.dt.from_np(v.dtype), kind="ExternalInput").ap() for k, v in arrays.items()}
    args["rows"] = nc.dram_tensor("rows", (4 * P, 3, P), BF16, kind="Internal").ap()
    args["diag"] = nc.dram_tensor("diag", (P, 16, 16), F32, kind="Internal").ap()
    args["tri_d"] = nc.dram_tensor("tri_d", (P, 16, 32), F32, kind="Internal").ap()
    out = nc.dram_tensor("out", (NI * P, D), F32, kind="ExternalOutput").ap()
    attention_kernel(nc, out=out, **args)
    r = run_bass_kernel_spmd(nc, [arrays], core_ids=[0])
    return r.results[0]["out"].reshape(NB, SEQ, D)
```
